# Optimizing a Trainium2 kernel written in Bass

```python
import numpy as np
import jax
import jax.numpy as jnp

def _softmax(x, axis=-1):
    return jax.nn.softmax(x, axis=axis)

def _gelu(x):
    return jax.nn.gelu(x, approximate=True)

def _silu(x):
    return jax.nn.silu(x)

def _sigmoid(x):
    return jax.nn.sigmoid(x)

def _layernorm(x, axis=-1, eps=1e-05):
    m = jnp.mean(x, axis=axis, keepdims=True)
    v = jnp.var(x, axis=axis, keepdims=True)
    return (x - m) / jnp.sqrt(v + eps)

def _scatter_add(tgt, idx, src, axis=0):
    return tgt.at[idx].add(src)

def _segment_sum(src, seg, n):
    return jax.ops.segment_sum(src, seg, n)
kernel_name = 'mk_gps_d1_gnn_r8_58dd70'

def setup_inputs(seed: int=0):
    np.random.seed(seed)
    _w = jnp.asarray

    def _rec_inputs():
        import jax
        import jax.numpy as jnp
        _gk = jax.random.key(seed)
        x = -0.0003929 + 0.9999 * jax.random.normal(jax.random.fold_in(_gk, 1), (1250, 1024), jnp.float32)
        src = jax.random.randint(jax.random.fold_in(_gk, 2), (40000,), 0, 1250, jnp.int32)
        dst = jax.random.randint(jax.random.fold_in(_gk, 3), (40000,), 0, 1250, jnp.int32)
        _o = jnp.argsort(dst, stable=True)
        src = src[_o]
        dst = dst[_o]
        edge_weight = jax.random.uniform(jax.random.fold_in(_gk, 12), (40000,), jnp.float32, 0.0, 0.999994)
        return (x, src, dst, edge_weight)
    x, src, dst, edge_weight = _rec_inputs()

    def _L0_gnn_setup():
        import jax, jax.numpy as jnp
        import numpy as np
        N_NODES = 2048
        N_EDGES = 16384
        D = 1024
        key = jax.random.key(seed)
        k_x, k_w, k_W, k_s, k_d = jax.random.split(key, 5)
        x = jax.random.normal(k_x, (N_NODES, D), dtype=jnp.float32)
        edge_w = jax.random.uniform(k_w, (N_EDGES,), dtype=jnp.float32)
        W = jax.random.normal(k_W, (D, D), dtype=jnp.float32) * (1.0 / np.sqrt(D))
        b = jnp.zeros((D,), dtype=jnp.float32)
        src = jax.random.randint(k_s, (N_EDGES,), 0, N_NODES)
        dst = jax.random.randint(k_d, (N_EDGES,), 0, N_NODES)
        return {'x': x, 'edge_w': edge_w, 'W': W, 'b': b, 'src': src, 'dst': dst}
    _L0_gnn_all = _L0_gnn_setup()
    _L0_gnn_in = {k: v for k, v in _L0_gnn_all.items() if k in ('W', 'b')}
    del _L0_gnn_all

    def _L0_mix_setup():
        import jax, jax.numpy as jnp
        import numpy as np
        B, S, E, H = (4, 512, 1024, 16)
        D = E // H

        def _phi(x):
            return jax.nn.elu(x) + 1.0
        key = jax.random.key(seed)
        k1, k2, k3 = jax.random.split(key, 3)
        x = jax.random.normal(k1, (B, S, E), dtype=jnp.float32)
        W_qkv = jax.random.normal(k2, (E, 3 * E), dtype=jnp.float32) * E ** (-0.5)
        b_qkv = jnp.zeros((3 * E,), dtype=jnp.float32)
        W_proj = jax.random.normal(k3, (E, E), dtype=jnp.float32) * E ** (-0.5)
        b_proj = jnp.zeros((E,), dtype=jnp.float32)
        return {'x': x, 'W_qkv': W_qkv, 'b_qkv': b_qkv, 'W_proj': W_proj, 'b_proj': b_proj}
    _L0_mix_all = _L0_mix_setup()
    _L0_mix_in = {k: v for k, v in _L0_mix_all.items() if k in ('W_qkv', 'b_qkv', 'W_proj', 'b_proj')}
    del _L0_mix_all

    def _L0_ffn_setup():
        import jax, jax.numpy as jnp
        import numpy as np
        import math
        DMODEL = 1024
        DFF = 512
        NUM_EXPERTS = 8
        TOPK = 2
        CAP_FACTOR = 1.25
        EPS = 1.1920929e-07

        def _trunc_normal(key, shape, fan_in, scale=1.0):
            std = scale * (1.0 / fan_in) ** 0.5
            return jax.random.truncated_normal(key, -2.0, 2.0, shape, jnp.float32) * std
        key = jax.random.key(seed)
        ks = jax.random.split(key, 5)
        return {'x': jax.random.normal(ks[0], (2, 256, DMODEL), jnp.float32), 'router_weight': _trunc_normal(ks[1], (NUM_EXPERTS, DMODEL), DMODEL), 'ff_pre_act_weight': _trunc_normal(ks[2], (NUM_EXPERTS, DFF, DMODEL), DMODEL), 'gate_weight': _trunc_normal(ks[3], (NUM_EXPERTS, DFF, DMODEL), DMODEL), 'ff_post_act_weight': _trunc_normal(ks[4], (NUM_EXPERTS, DMODEL, DFF), DFF)}
    _L0_ffn_all = _L0_ffn_setup()
    _L0_ffn_in = {k: v for k, v in _L0_ffn_all.items() if k in ('router_weight', 'ff_pre_act_weight', 'gate_weight', 'ff_post_act_weight')}
    del _L0_ffn_all
    return {'x': x, 'src': src, 'dst': dst, 'edge_weight': edge_weight, 'L0_gnn_W': _L0_gnn_in['W'], 'L0_gnn_b': _L0_gnn_in['b'], 'L0_mix_W_qkv': _L0_mix_in['W_qkv'], 'L0_mix_b_qkv': _L0_mix_in['b_qkv'], 'L0_mix_W_proj': _L0_mix_in['W_proj'], 'L0_mix_b_proj': _L0_mix_in['b_proj'], 'L0_ffn_router_weight': _L0_ffn_in['router_weight'], 'L0_ffn_ff_pre_act_weight': _L0_ffn_in['ff_pre_act_weight'], 'L0_ffn_gate_weight': _L0_ffn_in['gate_weight'], 'L0_ffn_ff_post_act_weight': _L0_ffn_in['ff_post_act_weight']}

def reference(x, src, dst, edge_weight, L0_gnn_W, L0_gnn_b, L0_mix_W_qkv, L0_mix_b_qkv, L0_mix_W_proj, L0_mix_b_proj, L0_ffn_router_weight, L0_ffn_ff_pre_act_weight, L0_ffn_gate_weight, L0_ffn_ff_post_act_weight):
    import jax
    import jax.numpy as jnp

    def _L0_gnn_ref(x, edge_w, W, b, src, dst):
        import jax, jax.numpy as jnp
        import numpy as np
        N_NODES = 2048
        N_EDGES = 16384
        D = 1024
        "EdgeWeightNorm(norm='both') -> GraphConv(norm='both', weight, bias) -> ReLU.\n\n            Matches DGL semantics:\n              c_ij   = w_ij / sqrt(sum_out_w[src] * sum_in_w[dst])   (EdgeWeightNorm 'both')\n              h_j    = relu( D_in[j]^-1/2 * sum_i c_ij * D_out[i]^-1/2 * x_i  @ W + b )\n            where D_out/D_in are structural degrees clamped to >= 1.\n            "
        n = x.shape[0]
        ones = jnp.ones_like(edge_w)
        w_out = jax.ops.segment_sum(edge_w, src, num_segments=n)
        w_in = jax.ops.segment_sum(edge_w, dst, num_segments=n)
        c = edge_w * jax.lax.rsqrt(w_out[src] * w_in[dst])
        deg_out = jnp.clip(jax.ops.segment_sum(ones, src, num_segments=n), 1.0)
        deg_in = jnp.clip(jax.ops.segment_sum(ones, dst, num_segments=n), 1.0)
        xs = x * jax.lax.rsqrt(deg_out)[:, None]
        msg = xs[src] * c[:, None]
        agg = jax.ops.segment_sum(msg, dst, num_segments=n)
        agg = agg * jax.lax.rsqrt(deg_in)[:, None]
        return jax.nn.relu(agg @ W + b)

    def _L0_mix_ref(x, W_qkv, b_qkv, W_proj, b_proj):
        import jax, jax.numpy as jnp
        import numpy as np
        B, S, E, H = (4, 512, 1024, 16)
        D = E // H

        def _phi(x):
            return jax.nn.elu(x) + 1.0
        b, s, _ = x.shape
        qkv = (x @ W_qkv + b_qkv).reshape(b, s, 3, H, D)
        q, k, v = (qkv[:, :, 0], qkv[:, :, 1], qkv[:, :, 2])
        pq, pk = (_phi(q), _phi(k))
        kv = jnp.einsum('bshd,bshm->bhmd', pk, v)
        z = 1.0 / (jnp.einsum('bshd,bhd->bsh', pq, pk.sum(axis=1)) + 1e-06)
        attn = jnp.einsum('bshd,bhmd,bsh->bshm', pq, kv, z)
        attn = attn.reshape(b, s, H * D)
        _proj = attn @ W_proj + b_proj
        return attn

    def _L0_ffn_ref(x, router_weight, ff_pre_act_weight, gate_weight, ff_post_act_weight):
        import jax, jax.numpy as jnp
        import numpy as np
        import math
        DMODEL = 1024
        DFF = 512
        NUM_EXPERTS = 8
        TOPK = 2
        CAP_FACTOR = 1.25
        EPS = 1.1920929e-07

        def _trunc_normal(key, shape, fan_in, scale=1.0):
            std = scale * (1.0 / fan_in) ** 0.5
            return jax.random.truncated_normal(key, -2.0, 2.0, shape, jnp.float32) * std
        orig_shape = x.shape
        h = x.reshape(-1, DMODEL)
        T = h.shape[0]
        logits = jnp.einsum('th,eh->te', h, router_weight)
        probs = jax.nn.softmax(logits.astype(jnp.float32), axis=-1)
        topk_probs, selected = jax.lax.top_k(probs, TOPK)
        topk_probs = topk_probs / jnp.maximum(topk_probs.sum(-1, keepdims=True), EPS)
        flat_tokens = jnp.repeat(jnp.arange(T), TOPK)
        flat_experts = selected.reshape(-1)
        flat_weights = topk_probs.reshape(-1)
        A = T * TOPK
        capacity = max(1, math.ceil(CAP_FACTOR * A / NUM_EXPERTS))
        weight_order = jnp.argsort(-flat_weights, stable=True)
        grouped_order = jnp.argsort(flat_experts[weight_order], stable=True)
        sort_order = weight_order[grouped_order]
        se = flat_experts[sort_order]
        st = flat_tokens[sort_order]
        sw = flat_weights[sort_order]
        counts = jnp.bincount(se, length=NUM_EXPERTS)
        offsets = jnp.cumsum(counts) - counts
        slot = jnp.arange(A) - offsets[se]
        keep = slot < capacity
        sw = jnp.where(keep, sw, 0.0)
        token_wsum = jnp.zeros(T, jnp.float32).at[st].add(sw)
        kept_w = sw / jnp.maximum(token_wsum[st], EPS)
        FC = NUM_EXPERTS * capacity
        dispatch = jnp.where(keep, se * capacity + slot, FC)
        expert_inputs = jnp.zeros((FC + 1, DMODEL), x.dtype).at[dispatch].set(h[st])
        expert_inputs = expert_inputs[:FC].reshape(NUM_EXPERTS, capacity, DMODEL)
        pre = jnp.einsum('ech,edh->ecd', expert_inputs, ff_pre_act_weight)
        gate = jnp.einsum('ech,edh->ecd', expert_inputs, gate_weight)
        expert_out = jnp.einsum('ecd,ehd->ech', pre * jax.nn.silu(gate), ff_post_act_weight)
        eo_flat = jnp.concatenate([expert_out.reshape(FC, DMODEL), jnp.zeros((1, DMODEL), x.dtype)], axis=0)
        updates = eo_flat[dispatch] * kept_w.astype(x.dtype)[:, None]
        out = jnp.zeros((T, DMODEL), x.dtype).at[st].add(updates)
        return out.reshape(orig_shape)
    xn = _layernorm(x, axis=-1)
    x = x + _L0_gnn_ref(xn, edge_weight, L0_gnn_W, L0_gnn_b, src, dst) + _L0_mix_ref(xn[None], L0_mix_W_qkv, L0_mix_b_qkv, L0_mix_W_proj, L0_mix_b_proj)[0]
    x = x + _L0_ffn_ref(_layernorm(x, axis=-1)[None], L0_ffn_router_weight, L0_ffn_ff_pre_act_weight, L0_ffn_gate_weight, L0_ffn_ff_post_act_weight)[0]
    return x

_drawn_inputs = setup_inputs


def setup_inputs(seed=0):
    import zlib

    import numpy as np

    out = dict(_drawn_inputs(seed))
    spreads = {'L0_gnn_b': (0.0, 0.1), 'L0_mix_b_qkv': (0.0, 0.1), 'L0_mix_b_proj': (0.0, 0.1)}
    factors = {'edge_weight': 3.758, 'L0_gnn_W': 4.104}
    for name, (base, spread) in spreads.items():
        noise = np.random.default_rng([zlib.crc32(name.encode()), seed]).standard_normal(out[name].shape)
        drawn = base * np.exp(spread * noise) if base else spread * noise
        out[name] = jnp.asarray(drawn.astype(out[name].dtype))
    for name, factor in factors.items():
        out[name] = (out[name] * factor).astype(out[name].dtype)
    return out
```

```python
from contextlib import ExitStack, contextmanager

import concourse.bass as bass
from concourse import mybir

F32 = mybir.dt.float32
FR = mybir.dt.float32r
BF16 = mybir.dt.bfloat16
I32 = mybir.dt.int32
ALU = mybir.AluOpType
ACT = mybir.ActivationFunctionType
X = mybir.AxisListType.X

T = 1250
TT = 125
NT = T // TT
D = 1024
HC = D // 128
SC = 512
NG = 8
HG = 2
PAIRS = 4
KVW = 129
AW = 130
QCUT = [0, 418, 834, 1250]
UNITS = 2 * NT + 3 * PAIRS

NE = 40000
EC = NE // TT
BC = 8
EB = BC * TT
NBLK = EC // BC
BPG = NBLK // HG
NB = NT * NT
CHUNK = 128
NCH = -(-((NE + NB * (CHUNK - 1)) // CHUNK) // 4) * 4
BW = 129
MAGIC = 1.5 * 2.0**23

NX = 8
DFF = 512
FC = DFF // 128
CAP = 391
CAPR = CAP + 1
CA = CAPR // 4
EPS = 1.1920929e-07
LNEPS = 1e-05


class Count:

    def __init__(self, engine, sem):
        self.engine, self.sem, self.n = engine, sem, 0

    def then(self, instruction):
        instruction.then_inc(self.sem, 1)
        self.n = self.n + 1
        self.engine.wait_ge(self.sem, self.n)

    @contextmanager
    def loop(self, it, times, per):
        start = self.n
        self.n = start + it * per
        self.used = 0
        before = self.n
        inner = Body(self, before, per)
        yield inner
        assert inner.k == per, f"the body raises its semaphore {inner.k} times"
        self.n = start + times * per


class Body:
    def __init__(self, count, base, per):
        self.count, self.base, self.k = count, base, 0

    def then(self, instruction):
        instruction.then_inc(self.count.sem, 1)
        self.k += 1
        self.count.engine.wait_ge(self.count.sem, self.base + self.k)


def build(nc, x, edges_n, edges_c, w_c, wmain, bqkv, bg, wr_t, wpre, wgate, wpost, out, debug=None):
    with ExitStack() as ctx:
        names = [0]

        def at(off, shape, dt, name):
            t = nc.alloc_sbuf_tensor_at(name, shape, dt, offset=BASE + off)
            size = 4 if dt != BF16 else 2
            for n in shape[1:]:
                size *= n
            assert BASE + off + size <= nc.sbuf_usable_end, (name, BASE + off + size - nc.sbuf_usable_end)
            return t

        def sem(name):
            return ctx.enter_context(nc.semaphore(name))

        def dram(name, shape, dt=F32):
            return nc.dram_tensor(name, shape, dt).ap()

        BASE = -(-nc.sbuf_base // 32) * 32
        A = 0
        SL = A + 81920
        RAW = SL + 32768
        WR = RAW + 16384
        RR = WR + NB * BW * 4 + 16
        RR = -(-RR // 32) * 32
        xt_hi = at(A, [128, HC, T], FR, "xt_hi")
        xt_lo = at(A + 40000, [128, HC, T], FR, "xt_lo")
        s0_hi = at(SL, [128, 8, SC], FR, "s0_hi")
        s0_lo = at(SL + 16384, [128, 8, SC], FR, "s0_lo")
        raw = at(RAW, [128, 8, SC], F32, "raw")

        xin = at(WR, [TT, 2, D], F32, "xin")
        en = at(WR + 8192, [TT, 2, EC], I32, "en")
        ec = at(WR + 10752, [TT, 2, EC], I32, "ec")
        wc = at(WR + 13312, [TT, EC], F32, "wc")
        tn = at(WR + 14592, [TT, 3, EC], F32, "tn")
        tc = at(WR + 18432, [TT, 3, EC], F32, "tc")
        bkt = at(WR + 22272, [TT, EC], BF16, "bkt")
        oh_d = at(WR + 22912, [TT, EC, NT], BF16, "oh_d")
        oh_s = at(WR + 29312, [TT, EC, NT], BF16, "oh_s")
        hq = at(WR + 35712, [80, 8, NT], F32, "hq")
        mask80 = at(WR + 36032, [80, 8, NT], F32, "mask80")
        hs = at(WR + 36352, [80, NT], F32, "hs")
        sel80 = at(WR + 36416, [80, NT], F32, "sel80")
        hist10 = at(WR + 36480, [NT, NT], F32, "hist10")
        upper = at(WR + 36544, [NB, NB], F32, "upper")
        iotak = at(WR + 36960, [NB, NCH], F32, "iotak")
        ge = at(WR + 38624, [NB, NCH], F32, "ge")
        phik = at(WR, [TT, NT, SC], F32, "phik")
        vt = at(WR + 20480, [TT, 2, PAIRS, KVW], F32, "vt")
        phiq = at(WR + 24640, [128, 2, T], F32, "phiq")
        sa = at(WR + 34656, [TT, 2, NT, 128], F32, "sa")
        kvblk = at(WR + 44896, [128, PAIRS, AW], F32, "kvblk")
        bkv = at(WR + 46976, [TT, 2, SC], F32, "bkv")
        bq = at(WR + 51072, [128, PAIRS], F32, "bq")
        adj = at(WR, [TT, NB * BW], F32, "adj")
        h2a = at(WR, [TT, NT, D], F32, "h2a")
        s1_hi = at(WR, [128, 8, SC], FR, "s1_hi")
        s1_lo = at(WR + 16384, [128, 8, SC], FR, "s1_lo")
        g_hi = at(WR + 32768, [128, FC, CAPR], FR, "g_hi")
        g_lo = at(WR + 39040, [128, FC, CAPR], FR, "g_lo")

        o = RR
        def take(nbytes):
            nonlocal o
            r = o
            o += -(-nbytes // 32) * 32
            return r
        ident = at(take(512), [128, 128], F32, "ident")
        ones = at(take(512), [128, 128], F32, "ones")
        onesb = at(take(4), [128, 2], BF16, "onesb")
        iota = at(take(500), [128, TT], F32, "iota")
        iotap = at(take(4), [128, 1], F32, "iotap")
        lower = at(take(500), [TT, TT], F32, "lower")
        zero = at(take(2048), [128, SC], F32, "zero")
        offs = at(take(NCH * 4), [1, NCH], I32, "offs")
        stats = at(take(48), [TT, 2, 6], F32, "stats")
        mv = at(take(8), [TT, 2], F32, "mv")
        rstd = at(take(8), [TT, 2], F32, "rstd")
        nrm = at(take(160), [TT, 4, NT], F32, "nrm")
        nsc = at(take(80), [TT, 2, NT], F32, "nsc")
        hist = at(take(4), [NB, 1], F32, "hist")
        nch = at(take(8), [NB, 2], F32, "nch")
        incl = at(take(4), [NB, 1], F32, "incl")
        base1 = at(take(4), [NB, 1], F32, "base1")
        carry = at(take(4), [NB, 1], F32, "carry")
        zt = at(take(32), [TT, 2, 2, 2], F32, "zt")
        pw = at(take(4), [1, 1], F32, "pw")
        CST = o
        br = at(take(4000), [NB, 2, EB], BF16, "br")
        oht = at(take(2000), [NB, EB], BF16, "oht")
        sm = at(take(4000), [NB, EB], F32, "sm")
        RECO = o
        rec = at(take(EC * 16), [TT, EC, 4], F32, "rec")
        pk = at(take(64), [TT, 2, BC], F32, "pk")
        idx = at(take(64), [TT, 2, BC], I32, "idx")
        rs = at(take(256), [TT, 2, BC, 4], F32, "rs")
        t_b = at(take(4096), [128, 2, SC], F32, "t_b")
        e_b = at(take(4096), [128, 2, SC], F32, "e_b")
        rl = at(CST, [128, NCH, 4], F32, "rl")
        ohs = at(RECO, [128, 2, 128], F32, "ohs")
        ohd = at(RECO + 1024, [128, 2, 128], F32, "ohd")
        mvt = at(RECO + 2048, [128, 2, 128], F32, "mvt")
        y_hi = at(A, [TT, NT, D], FR, "y_hi")
        y_lo = at(A + 40960, [TT, NT, D], FR, "y_lo")
        yraw = at(RAW, [TT, 4, D], F32, "yraw")
        w_hi = at(CST, [TT, NT, TT], FR, "w_hi")
        w_lo = at(CST + 5024, [TT, NT, TT], FR, "w_lo")
        bgb = at(SL, [TT, D], F32, "bgb")
        xt2 = at(SL + 4096, [TT, 2, D], F32, "xt2")
        at2 = at(SL + 12288, [TT, 2, D], F32, "at2")
        gt2 = at(SL + 20480, [TT, 2, D], F32, "gt2")
        wrt = at(SL, [128, HC, NX], F32, "wrt")
        h2t = at(SL + 256, [128, 2, HC, TT], F32, "h2t")
        diag = at(SL + 8320, [TT, 2, NX, TT], F32, "diag")
        vb = at(A, [TT, NX, T], F32, "vb")
        MW = TT * NT * (NT + 1) // 2
        cmpm = at(A + 40000, [TT, 2, MW], BF16, "cmpm")
        o = CST + 10080
        small = {}
        for name in ("lg", "pr", "ohe1", "ohe2", "cand", "v", "r1", "r2", "rank", "keep"):
            small[name] = at(take(320), [TT, NT, NX], F32, name)
        for name in ("m1", "m2", "den", "wk1", "wk2", "sl1", "sl2", "kp1", "kp2", "cm", "left"):
            small[name] = at(take(40), [TT, NT], F32, name)
        io8 = at(take(32), [TT, NX], F32, "io8")
        io392 = at(take(32), [TT, NX], F32, "io392")
        sidx = at(take(80), [TT, 2, NT], I32, "sidx")
        gidx = at(take(80), [TT, 2, NT], I32, "gidx")
        ex_hi = at(A, [128, HC, CAPR], FR, "ex_hi")
        ex_lo = at(A + 12544, [128, HC, CAPR], FR, "ex_lo")
        s2_hi = at(A + 25088, [128, 8, SC], FR, "s2_hi")
        s2_lo = at(A + 41472, [128, 8, SC], FR, "s2_lo")
        rows = at(A + 57856, [CA, 4, D], F32, "rows")
        sg = at(CST, [128, 2, CAPR], F32, "sg")
        gf = at(CST + 3136, [128, 2, CAPR], F32, "gf")
        eo = at(o, [CA, 4, SC], F32, "eo")
        r1t = at(A, [TT, 2, D], F32, "r1t")
        r2t = at(A + 8192, [TT, 2, D], F32, "r2t")
        x2t = at(A + 16384, [TT, 2, D], F32, "x2t")

        P = ctx.enter_context(nc.psum_tensor("P", [128, 8, 512], F32))

        bkt_d = dram("bkt_d", [NE], BF16)
        hist_d = dram("hist_d", [NB])
        rec_d = dram("rec_d", [128 * NCH, 4])
        attn_d = dram("attn_d", [T, D])
        y_d = dram("y_d", [T, D])
        x2_d = dram("x2_d", [T, D])
        h2_d = dram("h2_d", [T, D])
        ein_d = dram("ein_d", [NX * CAPR, D])
        eo_d = dram("eo_d", [NX * CAPR, D])

        x_in = [sem(f"x_in{i}") for i in range(2)]
        edges_in = sem("edges_in")
        const_ok = sem("const_ok")
        dve_step = sem("dve_step")
        act_step = sem("act_step")
        pool_step = sem("pool_step")
        var_ok = sem("var_ok")
        std_ok = sem("std_ok")
        xn_ok = sem("xn_ok")
        tr_done = sem("tr_done")
        hi_x = sem("hi_x")
        lo_x = sem("lo_x")
        bkt_ok = sem("bkt_ok")
        bkt_st = sem("bkt_st")
        ohb_ok = sem("ohb_ok")
        graph_mm = sem("graph_mm")
        gstep = sem("gstep")
        hist_st = sem("hist_st")
        hist_in = sem("hist_in")
        raw_in = [sem(f"raw_in{i}") for i in range(4)]
        hi_ok = sem("hi_ok")
        lo_ok = sem("lo_ok")
        w_used = sem("w_used")
        bias_in = sem("bias_in")
        bias_free = sem("bias_free")
        proj = sem("proj")
        kv_evac = sem("kv_evac")
        er = sem("er")
        phik_ok = sem("phik_ok")
        kv_mm = sem("kv_mm")
        kvblk_ok = sem("kvblk_ok")
        q_evac = sem("q_evac")
        phiq_ok = sem("phiq_ok")
        at_mm = sem("at_mm")
        at_evac = sem("at_evac")
        sa_st = [sem(f"sa_st{i}") for i in range(2)]
        br_in = [sem(f"br_in{i}") for i in range(2)]
        br_free = sem("br_free")
        sm_ok = sem("sm_ok")
        rs_ok = sem("rs_ok")
        scat = [sem(f"scat{i}") for i in range(2)]
        ein_zero = sem("ein_zero")
        g_evac = sem("g_evac")
        y_st = [sem(f"y_st{i}") for i in range(2)]
        rl_in = sem("rl_in")
        oh_ok = sem("oh_ok")
        mv_ok = sem("mv_ok")
        oh_free = sem("oh_free")
        acc_free = sem("acc_free")
        ch_mm = sem("ch_mm")
        nrm_ok = sem("nrm_ok")
        nrm_sq = sem("nrm_sq")
        nsc_ok = sem("nsc_ok")
        y_in = [sem(f"y_in{i}") for i in range(4)]
        yh_ok = sem("yh_ok")
        yl_ok = sem("yl_ok")
        wh_ok = sem("wh_ok")
        wl_ok = sem("wl_ok")
        wh_free = sem("wh_free")
        agg_mm = sem("agg_mm")
        agg_evac = sem("agg_evac")
        bg_in = sem("bg_in")
        res_in = [sem(f"res_in{i}") for i in range(2)]
        res_ok = sem("res_ok")
        var2 = sem("var2")
        std2 = sem("std2")
        x2_ok = sem("x2_ok")
        h2_ok = sem("h2_ok")
        x2_st = [sem(f"x2_st{i}") for i in range(2)]
        h2_in = sem("h2_in")
        wr_in = sem("wr_in")
        tr2 = sem("tr2")
        h2t_ok = sem("h2t_ok")
        lg_mm = sem("lg_mm")
        lg_evac = sem("lg_evac")
        dmax_ok = sem("dmax_ok")
        exp_ok = sem("exp_ok")
        diag_ok = sem("diag_ok")
        vb_mm = sem("vb_mm")
        vb_ok = sem("vb_ok")
        cmp_ok = sem("cmp_ok")
        cs_mm = sem("cs_mm")
        sidx_ok = sem("sidx_ok")
        kw_ok = sem("kw_ok")
        ein_st = sem("ein_st")
        rows_in = sem("rows_in")
        rows_free = sem("rows_free")
        etr = sem("etr")
        exh = sem("exh")
        exl = sem("exl")
        pg_mm = sem("pg_mm")
        sg_ok = sem("sg_ok")
        gf_ok = sem("gf_ok")
        gh_ok = sem("gh_ok")
        gl_ok = sem("gl_ok")
        dn_mm = sem("dn_mm")
        eo_ok = sem("eo_ok")
        eo_st = [sem(f"eo_st{i}") for i in range(4)]
        g1_in = [sem(f"g1_in{i}") for i in range(2)]
        x2_in = [sem(f"x2_in{i}") for i in range(2)]
        o_ok = sem("o_ok")
        o_st = [sem(f"o_st{i}") for i in range(2)]

        MOE = 8 * NG
        GM0 = 4

        x_v = x.rearrange("(i p) d -> p i d", p=TT)
        attn_v = attn_d.rearrange("(i p) (g c) -> p i g c", p=TT, c=128)
        y_v = y_d.rearrange("(i p) (g c) -> p i g c", p=TT, c=SC)
        yt_v = y_d.rearrange("(i p) d -> p i d", p=TT)
        att_v = attn_d.rearrange("(i p) d -> p i d", p=TT)
        x2_v = x2_d.rearrange("(i p) d -> p i d", p=TT)
        h2_v = h2_d.rearrange("(i p) d -> p i d", p=TT)
        out_v = out.rearrange("(i p) d -> p i d", p=TT)
        wm_v = wmain.rearrange("g (s p) n -> p g s n", p=128)
        ein_v = ein_d.rearrange("(e a p) d -> p e a d", a=4, p=CA)
        eo_v = eo_d.rearrange("(e a p) (h n) -> p e a h n", a=4, p=CA, h=2)

        block = ctx.enter_context(nc.Block())

        @block.sync
        def _(sp):
            def load_group(g, first=False):
                for p in range(4):
                    if not first:
                        sp.wait_ge(lo_ok, g * 8 + 2 * p - 6)
                    sp.dma_start(raw[:, 2 * p:2 * p + 2, :], wm_v[:, g, 2 * p:2 * p + 2, :]).then_inc(raw_in[p], 16)

            for c in range(2):
                sp.dma_start(xin[:, c, :], x_v[:, c, :]).then_inc(x_in[c], 16)
            load_group(0, first=True)
            with sp.Fori(1, NT // 2) as it:
                for c in range(2):
                    sp.wait_ge(tr_done, it * 2 + c - 1)
                    sp.dma_start(xin[:, c, :], x_v[:, it * 2 + c, :]).then_inc(x_in[c], 16)
            with sp.Fori(0, HG) as cg:
                for k in range(1, 4):
                    load_group(cg * 3 + k)
                for j in range(PAIRS):
                    sp.wait_ge(at_evac, cg * 20 + 5 * j + 6)
                    sp.dma_start(attn_v[:, :, cg * PAIRS + j, :], sa[:, j % 2, :, :]).then_inc(sa_st[j % 2], 16)
            load_group(7)
            for g in range(2):
                with sp.Fori(0, NT // 2) as it:
                    for c in range(2):
                        sp.wait_ge(g_evac, it * 2 + (g * NT + c + 1))
                        sp.dma_start(y_v[:, it * 2 + c, g, :], t_b[0:TT, c, :]).then_inc(y_st[c], 16)
            for c in range(2):
                sp.wait_ge(scat[c], 16 + 16 * BC * NBLK // 2)
            sp.wait_ge(rs_ok, NBLK)
            sp.dma_start(rl[:, :, :], rec_d.rearrange("(p k) f -> p k f", p=128)).then_inc(rl_in, 16)
            sp.wait_ge(g_evac, 2 * NT)
            sp.dma_start(bgb[:, :], bg.partition_broadcast(TT)).then_inc(bg_in, 16)
            for c in range(2):
                sp.wait_ge(y_st[c], 16 * NT)
                sp.wait_ge(sa_st[c], 64)
            for j in range(NT):
                if j >= 4:
                    sp.wait_ge(yl_ok, j - 3)
                sp.dma_start(yraw[:, j % 4, :], yt_v[:, j, :]).then_inc(y_in[j % 4], 16)
            for c in range(2):
                sp.dma_start(xt2[:, c, :], x_v[:, c, :]).then_inc(res_in[c], 16)
                sp.dma_start(at2[:, c, :], att_v[:, c, :]).then_inc(res_in[c], 16)
            with sp.Fori(0, NT // 2 - 1) as it:
                for c in range(2):
                    sp.wait_ge(x2_ok, it * 2 + c + 1)
                    sp.dma_start(x2_v[:, it * 2 + c, :], xt2[:, c, :]).then_inc(x2_st[c], 16)
                    sp.wait_ge(h2_ok, it * 2 + c + 1)
                    sp.dma_start(h2_v[:, it * 2 + c, :], at2[:, c, :]).then_inc(x2_st[c], 16)
                    sp.wait_ge(x2_st[c], it * 32 + 32)
                    sp.dma_start(xt2[:, c, :], x_v[:, it * 2 + (c + 2), :]).then_inc(res_in[c], 16)
                    sp.dma_start(at2[:, c, :], att_v[:, it * 2 + (c + 2), :]).then_inc(res_in[c], 16)
            for c in range(2):
                sp.wait_ge(x2_ok, NT - 1 + c)
                sp.dma_start(x2_v[:, NT - 2 + c, :], xt2[:, c, :]).then_inc(x2_st[c], 16)
                sp.wait_ge(h2_ok, NT - 1 + c)
                sp.dma_start(h2_v[:, NT - 2 + c, :], at2[:, c, :]).then_inc(x2_st[c], 16)
            for c in range(2):
                sp.wait_ge(x2_st[c], 16 * NT)
            sp.wait_ge(wl_ok, 2 * NT)
            sp.dma_start(h2a[:, :, :], h2_v).then_inc(h2_in, 16)
            sp.dma_start(wrt[:, :, :], wr_t.rearrange("p (h e) -> p h e", e=NX)).then_inc(wr_in, 16)

            def load_moe(e, k, src):
                for p in range(4):
                    sp.wait_ge(lo_ok, e * 24 + (MOE + 8 * k + 2 * p - 6))
                    sp.dma_start(raw[:, 2 * p:2 * p + 2, :], src[:, 2 * p:2 * p + 2, :]).then_inc(raw_in[p], 16)

            load_moe(0, 0, wpre[:, 0, :, :])
            load_moe(0, 1, wgate[:, 0, :, :])
            sp.wait_ge(ein_st, 16 * 2 * NT)
            sp.wait_ge(cs_mm, NX)
            sp.dma_start(rows[:, :, :], ein_v[:, 0, :, :]).then_inc(rows_in, 16)
            load_moe(0, 2, wpost[:, 0, :, :])
            with sp.Fori(0, NX - 1) as e:
                load_moe(e + 1, 0, wpre[:, e + 1, :, :])
                sp.wait_ge(etr, e * 8 + 8)
                sp.dma_start(rows[:, :, :], ein_v[:, e + 1, :, :]).then_inc(rows_in, 16)
                load_moe(e + 1, 1, wgate[:, e + 1, :, :])
                load_moe(e + 1, 2, wpost[:, e + 1, :, :])
                for u in range(8):
                    sp.wait_ge(eo_ok, e * 8 + (u + 1))
                    sp.dma_start(eo_v[:, e, u // 2, u % 2, :], eo[:, u % 4, :]).then_inc(eo_st[u % 4], 16)
            for u in range(8):
                sp.wait_ge(eo_ok, (NX - 1) * 8 + u + 1)
                sp.dma_start(eo_v[:, NX - 1, u // 2, u % 2, :], eo[:, u % 4, :]).then_inc(eo_st[u % 4], 16)
            sp.wait_ge(dn_mm, NX * 8)
            for i in range(NT):
                if i >= 2:
                    sp.wait_ge(o_ok, i - 1)
                    sp.dma_start(out_v[:, i - 2, :], x2t[:, i % 2, :]).then_inc(o_st[i % 2], 16)
                    sp.wait_ge(o_st[i % 2], 16 * (i // 2))
                sp.dma_start(x2t[:, i % 2, :], x2_v[:, i, :]).then_inc(x2_in[i % 2], 16)
            for i in range(NT - 2, NT):
                sp.wait_ge(o_ok, i + 1)
                sp.dma_start(out_v[:, i, :], x2t[:, i % 2, :]).then_inc(o_st[i % 2], 16)
            for c in range(2):
                sp.wait_ge(o_st[c], 16 * NT // 2)

        @block.scalar
        def _(act):
            act.dma_start(en[:, :, :], edges_n.rearrange("a p c -> p a c")).then_inc(edges_in, 16)
            act.dma_start(ec[:, :, :], edges_c.rearrange("a p c -> p a c")).then_inc(edges_in, 16)
            act.dma_start(wc[:, :], w_c).then_inc(edges_in, 16)
            act.wait_ge(bkt_ok, 1)
            act.dma_start(bkt_d.rearrange("(p c) -> p c", p=TT), bkt[:, :]).then_inc(bkt_st, 16)

            def split_hi(g, dst, first=False, src=None):
                for s in range(8):
                    act.wait_ge(raw_in[s // 2], g * 16 + 16)
                    if not first:
                        act.wait_ge(w_used, g * 8 + (s - 7))
                    act.copy(dst[:, s, :], raw[:, s, :]).then_inc(hi_ok, 1)

            split_hi(0, s0_hi, first=True)
            with act.Fori(0, NT // 2) as it:
                for c in range(2):
                    act.wait_ge(var_ok, it * 2 + (c + 1))
                    act.activation(rstd[:, 0:1], rstd[:, 1:2], ACT.Sqrt).then_inc(std_ok, 1)
                    act.wait_ge(tr_done, it * 2 + (c + 1))
                    act.copy(xt_hi[:, :, bass.ds(it * 250 + c * TT, TT)].rearrange("p (b h) t -> p b h t", b=2),
                             P[:, 2 * c:2 * c + 2, 0:500].rearrange("p b (h t) -> p b h t", h=4)).then_inc(hi_x, 1)
            act.wait_ge(gstep, 2)
            act.dma_start(hist_d.rearrange("(a b) -> a b", a=NT), hist10[:, :]).then_inc(hist_st, 16)
            act.wait_ge(hist_st, 16)
            act.dma_start(hist[:, :], hist_d.rearrange("(p o) -> p o", o=1)).then_inc(hist_in, 16)
            act.wait_ge(bkt_st, 16)
            act.wait_ge(gstep, 6)

            def load_rows(cg, b):
                act.wait_ge(br_free, cg * BPG + (b + 1))
                act.dma_start(br[:, b % 2, :],
                              bkt_d[bass.ds(cg * (BPG * EB) + b * EB, EB)].partition_broadcast(NB)).then_inc(br_in[b % 2], 16)

            with act.Fori(0, HG) as cg:
                act.wait_ge(bias_free, cg + 1)
                for k in range(2):
                    act.dma_start(bkv[:, k, :], bqkv[bass.ds(cg * SC + (k + 1) * D, SC)].partition_broadcast(TT)).then_inc(bias_in, 16)
                act.dma_start(bq[:, :], bqkv[bass.ds(cg * SC, SC)].rearrange("(j p) -> p j", p=128),
                              allow_slow_non_contiguous=True).then_inc(bias_in, 16)
                for i in range(NT):
                    act.wait_ge(kv_evac, cg * 20 + (i + 1))
                    if i >= 2:
                        act.wait_ge(phik_ok, cg * NT + (i - 1))
                    act.activation(e_b[0:TT, i % 2, :], t_b[0:TT, i % 2, :], ACT.Exp).then_inc(act_step, 1)
                    act.activation(t_b[0:TT, i % 2, :], t_b[0:TT, i % 2, :], ACT.Relu).then_inc(er, 1)
                    if i == NT - 2:
                        split_hi(cg * 3 + 1, s0_hi)
                load_rows(cg, 0)
                for i in range(NT):
                    if i >= 2:
                        load_rows(cg, i - 1)
                    if i == NT - 2:
                        split_hi(cg * 3 + 2, s0_hi)
                act.wait_ge(phik_ok, cg * NT + NT)
                act.wait_ge(bias_in, cg * 48 + 48)
                for q in range(3 * PAIRS):
                    j, n = q // 3, QCUT[q % 3 + 1] - QCUT[q % 3]
                    if q == 3 * PAIRS - 1:
                        split_hi(cg * 3 + 3, s0_hi)
                    act.wait_ge(proj, cg * UNITS + (2 * NT + q + 1))
                    if q >= 2:
                        act.wait_ge(phiq_ok, cg * 12 + (q - 1))
                    act.activation(e_b[:, q % 2, 0:n], P[:, q % 4, 0:n], ACT.Exp, bias=bq[:, j:j + 1]).then_inc(act_step, 1)
                    act.activation(t_b[:, q % 2, 0:n], P[:, q % 4, 0:n], ACT.Relu, bias=bq[:, j:j + 1]).then_inc(q_evac, 1)
                    if q + 9 < BPG:
                        load_rows(cg, q + 9)
            act.wait_ge(phiq_ok, 24)
            for g in range(2):
                for i in range(NT):
                    n = g * NT + i
                    act.wait_ge(proj, HG * UNITS + n + 1)
                    if n >= 2:
                        act.wait_ge(y_st[i % 2], 16 * (n // 2))
                    act.copy(t_b[0:TT, i % 2, :], P[0:TT, n % 4, :]).then_inc(g_evac, 1)
                    if g == 0 and i == NT - 2:
                        split_hi(7, s0_hi)
            zv = ein_d.rearrange("(p r) (h n) -> p (r h) n", p=128 - 16, h=2)
            act.dma_start(zv, zero[0:112, None, :].broadcast_to([112, NX * CAPR // 112 * 2, SC])).then_inc(ein_zero, 16)
            act.wait_ge(rl_in, 16)
            with act.Fori(0, NCH // 2) as it:
                for c in range(2):
                    act.wait_ge(oh_ok, it * 2 + (c + 1))
                    act.activation(mvt[:, c, 0:TT], ohd[:, c, 0:TT], ACT.Copy, scale=rl[:, bass.ds(it * 2 + c, 1), 2]).then_inc(act_step, 1)
                    act.copy(mvt[:, c, TT:TT + 2], rl[:, bass.ds(it * 2 + c, 1), 2:4].rearrange("p a b -> p (a b)")).then_inc(mv_ok, 1)
            act.wait_ge(nrm_ok, 1)
            act.activation(nrm[:, :, :], nrm[:, :, :], ACT.Sqrt).then_inc(nrm_sq, 1)
            act.wait_ge(nsc_ok, 1)
            act.wait_ge(w_used, 8 * NG)
            for j in range(NT):
                act.wait_ge(y_in[j % 4], 16 * (j // 4 + 1))
                act.activation(y_hi[:, j, :], yraw[:, j % 4, :], ACT.Copy, scale=nsc[:, 0, j:j + 1]).then_inc(yh_ok, 1)

            def adj_hi(i, h):
                act.copy(w_hi[:, 5 * h:5 * h + 5, :],
                         adj[:, bass.ds(i * (NT * BW) + h * (5 * BW), 5 * BW)].rearrange("p (j c) -> p j c", c=BW)[:, :, 0:TT]).then_inc(wh_ok, 1)

            for h in range(2):
                adj_hi(0, h)
            with act.Fori(0, NT) as i:
                act.wait_ge(var2, i + 1)
                act.activation(rstd[:, 0:1], rstd[:, 1:2], ACT.Sqrt).then_inc(std2, 1)
            with act.Fori(0, NT // 2) as it:
                for c in range(2):
                    act.wait_ge(tr2, it * 2 + (c + 1))
                    act.copy(h2t[:, c, :, :].rearrange("p (b h) t -> p b (h t)", b=2), P[:, 2 * c:2 * c + 2, 0:500]).then_inc(h2t_ok, 1)
            act.wait_ge(dmax_ok, 1)
            act.activation(small["pr"][:, :, :], small["pr"][:, :, :], ACT.Exp).then_inc(exp_ok, 1)
            with act.Fori(0, NT // 2) as it:
                for c in range(2):
                    act.wait_ge(vb_mm, it * 2 + (c + 1))
                    act.copy(vb[:, :, bass.ds(it * 250 + c * TT, TT)].rearrange("p (b e) t -> p b e t", b=2),
                             P[0:TT, 2 * c:2 * c + 2, 0:500].rearrange("p b (e t) -> p b e t", e=4)).then_inc(vb_ok, 1)

            def split_moe(e, k, dst):
                for s in range(8):
                    act.wait_ge(raw_in[s // 2], e * 48 + 16 * (NG + k + 1))
                    if k == 0:
                        act.wait_ge(w_used, e * 24 + (MOE - 24 + s + 1 + 0))
                    else:
                        act.wait_ge(w_used, e * 24 + (MOE - 24 + 8 * k + s + 1))
                    act.copy(dst[:, s, :], raw[:, s, :]).then_inc(hi_ok, 1)

            def ex_split_hi(e1):
                for h in range(HC):
                    act.wait_ge(etr, e1 * 8 + (h + 1))
                    act.copy(ex_hi[:, h, :], P[:, h % 2, 0:CAPR]).then_inc(exh, 1)

            act.wait_ge(lg_evac, NT)
            act.wait_ge(vb_mm, NT)
            split_moe(0, 0, s0_hi)
            act.wait_ge(ein_st, 16 * 2 * NT)
            act.wait_ge(cs_mm, NX)
            split_moe(0, 1, s1_hi)
            split_moe(0, 2, s2_hi)
            ex_split_hi(0)

            def swiglu(e):
                for m in range(FC):
                    act.wait_ge(pg_mm, e * FC + (m + 1))
                    if m >= 2:
                        act.wait_ge(gf_ok, e * FC + (m - 1))
                    act.activation(sg[:, m % 2, :], P[:, 4 + m % 2, 0:CAPR], ACT.Silu).then_inc(sg_ok, 1)
                    act.wait_ge(gf_ok, e * FC + (m + 1))
                    act.copy(g_hi[:, m, :], gf[:, m % 2, :]).then_inc(gh_ok, 1)

            def results(e):
                for u in range(0, 8, 2):
                    act.wait_ge(dn_mm, e * 8 + (u + 1))
                    act.wait_ge(eo_st[u % 4], e * 32 + 16 * (u // 4))
                    act.copy(eo[:, u % 4, :], P[0:CA, 6 + u % 2, :]).then_inc(eo_ok, 1)

            with act.Fori(0, NX - 1) as e:
                swiglu(e)
                split_moe(e + 1, 0, s0_hi)
                split_moe(e + 1, 1, s1_hi)
                ex_split_hi(e + 1)
                act.wait_ge(sg_ok, e * FC + FC)
                split_moe(e + 1, 2, s2_hi)
            swiglu(NX - 1)

        @block.gpsimd
        def _(pool):
            steps = Count(pool, pool_step)
            nc.gpsimd.memset(zero[:, :], 0.0).then_inc(const_ok, 1)
            steps.then(nc.gpsimd.memset(ident[:, :], 0.0))
            steps.then(nc.gpsimd.memset(ones[:, :], 1.0))
            nc.gpsimd.memset(onesb[:, :], 1.0).then_inc(const_ok, 1)
            nc.gpsimd.affine_select(out=ident[:, :], in_=ident[:, :], compare_op=ALU.not_equal, fill=1.0, base=0,
                                    pattern=[[-1, 128]], channel_multiplier=1).then_inc(const_ok, 1)
            nc.gpsimd.iota(iota[:, :], [[1, TT]], base=0, channel_multiplier=0,
                           allow_small_or_imprecise_dtypes=True).then_inc(const_ok, 1)
            nc.gpsimd.iota(iotap[:, :], [[1, 1]], base=0, channel_multiplier=1,
                           allow_small_or_imprecise_dtypes=True).then_inc(const_ok, 1)
            nc.gpsimd.iota(iotak[:, :], [[1, NCH]], base=0, channel_multiplier=0,
                           allow_small_or_imprecise_dtypes=True).then_inc(const_ok, 1)
            nc.gpsimd.affine_select(out=upper[:, :], in_=ones[0:NB, 0:NB], compare_op=ALU.is_ge, fill=0.0, base=0,
                                    pattern=[[1, NB]], channel_multiplier=-1).then_inc(const_ok, 1)
            nc.gpsimd.affine_select(out=lower[:, :], in_=ones[0:TT, 0:TT], compare_op=ALU.is_ge, fill=0.0, base=-1,
                                    pattern=[[-1, TT]], channel_multiplier=1).then_inc(const_ok, 1)
            o80 = ones[0:80, 0:80].rearrange("p (a b) -> p a b", a=8)
            steps.then(nc.gpsimd.affine_select(out=mask80[:, :, :], in_=o80, compare_op=ALU.is_ge, fill=0.0, base=0,
                                               pattern=[[-10, 8], [0, 10]], channel_multiplier=1))
            nc.gpsimd.affine_select(out=mask80[:, :, :], in_=mask80[:, :, :], compare_op=ALU.is_ge, fill=0.0, base=9,
                                    pattern=[[10, 8], [0, 10]], channel_multiplier=-1).then_inc(const_ok, 1)
            pool.wait_ge(const_ok, 1)
            rz = rec_d.rearrange("(p k) f -> p (k f)", p=128).rearrange("p (r n) -> p r n", r=4)
            for c in range(2):
                pool.dma_start(rz[:, 2 * c:2 * c + 2, :],
                               zero[:, None, 0:NCH].broadcast_to([128, 2, NCH])).then_inc(scat[c], 16)
            for c in range(2):
                pool.wait_ge(scat[c], 16)
            with pool.Fori(0, NBLK // 2) as it:
                for c in range(2):
                    pool.wait_ge(rs_ok, it * 2 + (c + 1))
                    pool.wait_ge(pool_step, it * 2 + (steps.n + c))
                    nc.gpsimd.tensor_tensor(pw[:, :], ones[0:1, 0:1], ones[0:1, 0:1], ALU.add).then_inc(pool_step, 1)
                    for k in range(BC):
                        pool.indirect_dma_start(out=rec_d, out_offset=bass.IndirectOffsetOnAxis(ap=idx[:, c, k:k + 1], axis=0),
                                                in_=rs[:, c, k, :], in_offset=None, bounds_check=128 * NCH - 1,
                                                oob_is_err=True).then_inc(scat[c], 16)
            with pool.Fori(0, NT // 2) as it:
                for c in range(2):
                    pool.wait_ge(res_in[c], it * 32 + 32)
                    nc.gpsimd.tensor_tensor(xt2[:, c, :], xt2[:, c, :], at2[:, c, :], ALU.add).then_inc(res_ok, 1)
            pool.wait_ge(x2_ok, NT)
            nc.gpsimd.iota(io8[:, :], [[1, NX]], base=-NX, channel_multiplier=0,
                           allow_small_or_imprecise_dtypes=True).then_inc(const_ok, 1)
            nc.gpsimd.iota(io392[:, :], [[CAPR, NX]], base=0, channel_multiplier=0,
                           allow_small_or_imprecise_dtypes=True).then_inc(const_ok, 1)
            nc.gpsimd.iota(small["left"][:, :], [[-TT, NT]], base=T - 1, channel_multiplier=-1,
                           allow_small_or_imprecise_dtypes=True).then_inc(const_ok, 1)
            pool.wait_ge(ein_zero, 16)
            pool.wait_ge(sidx_ok, 1)
            pool.wait_ge(h2_in, 16)
            for i in range(NT):
                for k in range(2):
                    pool.indirect_dma_start(out=ein_d, out_offset=bass.IndirectOffsetOnAxis(ap=sidx[:, k, i:i + 1], axis=0),
                                            in_=h2a[:, i, :], in_offset=None, bounds_check=NX * CAPR - 1,
                                            oob_is_err=False).then_inc(ein_st, 16)
            pool.wait_ge(dn_mm, NX * 8)
            for c in range(4):
                pool.wait_ge(eo_st[c], 16 * 2 * NX)
            for i in range(NT):
                if i >= 2:
                    pool.wait_ge(o_ok, i - 1)
                for k, dst in ((0, r1t), (1, r2t)):
                    pool.indirect_dma_start(out=dst[:, i % 2, :], out_offset=None, in_=eo_d,
                                            in_offset=bass.IndirectOffsetOnAxis(ap=gidx[:, k, i:i + 1], axis=0),
                                            bounds_check=NX * CAPR - 1, oob_is_err=True).then_inc(g1_in[i % 2], 16)

        @block.vector
        def _(dve):
            v = nc.vector
            steps = Count(dve, dve_step)

            def floor_div(dst, src, by, add=0.0):
                steps.then(v.tensor_scalar(dst, src, 1.0 / by, add / by - 0.498, ALU.mult, ALU.add))
                steps.then(v.tensor_scalar(dst, dst, MAGIC, MAGIC, ALU.add, ALU.subtract))

            dve.wait_ge(edges_in, 48)
            for a in range(2):
                floor_div(tn[:, a, :], en[:, a, :], TT)
            v.scalar_tensor_tensor(out=bkt[:, :], in0=tn[:, 1, :], scalar=float(NT), in1=tn[:, 0, :],
                                   op0=ALU.mult, op1=ALU.add).then_inc(bkt_ok, 1)
            for a in range(2):
                floor_div(tc[:, a, :], ec[:, a, :], TT)
                v.scalar_tensor_tensor(out=rec[:, :, a], in0=tc[:, a, :], scalar=-float(TT), in1=ec[:, a, :],
                                       op0=ALU.mult, op1=ALU.add)
            v.tensor_copy(rec[:, :, 2], wc[:, :])
            v.memset(rec[:, :, 3:4], 1.0)
            dve.wait_ge(const_ok, 9)
            for a, oh in ((0, oh_s), (1, oh_d)):
                v.tensor_tensor(oh[:, :, :], iota[0:TT, None, 0:NT].broadcast_to([TT, EC, NT]),
                                tc[:, a, :, None].broadcast_to([TT, EC, NT]), ALU.is_equal).then_inc(ohb_ok, 1)

            def split_lo(g, hi, lo):
                for s in range(8):
                    dve.wait_ge(hi_ok, g * 8 + (s + 1))
                    v.tensor_tensor(lo[:, s, :], raw[:, s, :], hi[:, s, :].bitcast(F32), ALU.subtract).then_inc(lo_ok, 1)

            def normalize(st, src, dst, var, std, n):
                for h in range(2):
                    ins = v.bn_stats(stats[:, h, :], src[:, h * SC:(h + 1) * SC])
                st.then(ins)
                v.memset(rstd[:, 0:1], 0.0)
                st.then(v.bn_aggr(mv[:, :], stats[:, :, :]))
                v.tensor_scalar(rstd[:, 1:2], mv[:, 1:2], LNEPS, None, ALU.add).then_inc(var, 1)
                dve.wait_ge(std, n)
                st.then(v.reciprocal(rstd[:, 0:1], rstd[:, 0:1]))
                return v.tensor_scalar(dst, src, mv[:, 0:1], rstd[:, 0:1], ALU.subtract, ALU.mult)

            with dve.Fori(0, NT // 2) as it, steps.loop(it, NT // 2, 6) as st:
                for c in range(2):
                    dve.wait_ge(x_in[c], it * 16 + 16)
                    normalize(st, xin[:, c, :], xin[:, c, :], var_ok, std_ok, it * 2 + (c + 1)).then_inc(xn_ok, 1)
                    dve.wait_ge(hi_x, it * 2 + (c + 1))
                    sl = bass.ds(it * 250 + c * TT, TT)
                    v.tensor_tensor(xt_lo[:, :, sl].rearrange("p (b h) t -> p b h t", b=2),
                                    P[:, 2 * c:2 * c + 2, 0:500].rearrange("p b (h t) -> p b h t", h=4),
                                    xt_hi[:, :, sl].bitcast(F32).rearrange("p (b h) t -> p b h t", b=2),
                                    ALU.subtract).then_inc(lo_x, 1)
            split_lo(0, s0_hi, s0_lo)

            dve.wait_ge(graph_mm, 1)
            steps.then(v.tensor_tensor(hq[:, :, :], P[0:80, 7, 0:80].rearrange("p (a b) -> p a b", a=8), mask80[:, :, :], ALU.mult))
            v.tensor_reduce(sel80[:, :], ident[0:80, 0:80].rearrange("p (a b) -> p b a", a=8), X, ALU.add)
            v.tensor_reduce(hs[:, :], hq[:, :, :].rearrange("p a b -> p b a"), X, ALU.add).then_inc(gstep, 1)
            dve.wait_ge(graph_mm, 2)
            v.tensor_copy(hist10[:, :], P[0:NT, 7, 128:128 + NT]).then_inc(gstep, 1)
            dve.wait_ge(hist_in, 16)
            floor_div(nch[:, 0:1], hist[:, :], CHUNK, CHUNK - 1.0)
            v.tensor_copy(nch[:, 1:2], nch[:, 0:1]).then_inc(gstep, 1)
            dve.wait_ge(graph_mm, 3)
            steps.then(v.tensor_copy(incl[:, :], P[0:NB, 7, 160:161]))
            v.tensor_scalar(ge[:, :], iotak[:, :], incl[:, 0:1], None, ALU.is_ge).then_inc(gstep, 1)
            steps.then(v.tensor_tensor(base1[:, :], incl[:, :], nch[:, 0:1], ALU.subtract))
            steps.then(v.tensor_scalar(base1[:, :], base1[:, :], float(CHUNK), -1.0, ALU.mult, ALU.add))
            dve.wait_ge(graph_mm, 4)
            v.tensor_scalar(offs[:, :], P[0:1, 6, 0:NCH], float(NB - 1), float(BW), ALU.min, ALU.mult).then_inc(gstep, 1)
            v.memset(carry[:, :], 0.0).then_inc(br_free, 2)
            dve.wait_ge(bkt_st, 16)
            v.memset(vt[:, :, :, 128:129], 1.0).then_inc(at_evac, 1)
            v.memset(kvblk[:, :, :], 0.0).then_inc(bias_free, 1)
            v.memset(zt[:, :, :, :], 0.0).then_inc(gstep, 1)

            def places(cg, b, st):
                dve.wait_ge(br_in[b % 2], cg * (8 * BPG) + 16 * (b // 2 + 1))
                v.tensor_scalar(oht[:, :], br[:, b % 2, :], iotap[0:NB, 0:1], None, ALU.is_equal).then_inc(br_free, 1)
                dve.wait_ge(br_free, cg * BPG + (b + 3))
                dve.wait_ge(graph_mm, cg * BPG + (GM0 + b))
                st.then(v.tensor_tensor_scan(sm[:, :], oht[:, :], oht[:, :], carry[:, 0:1], ALU.add, ALU.max))
                st.then(v.tensor_copy(carry[:, :], sm[:, EB - 1:EB]))
                v.scalar_tensor_tensor(out=sm[:, :], in0=sm[:, :], scalar=base1[:, 0:1], in1=oht[:, :],
                                       op0=ALU.add, op1=ALU.mult).then_inc(sm_ok, 1)

            def records(cg, b, st):
                c = b % 2
                dve.wait_ge(graph_mm, cg * BPG + (GM0 + b + 1))
                pos = P[0:TT, 7, 256:256 + BC]
                st.then(v.tensor_scalar(pk[:, 0, :], pos, 1.0 / CHUNK, -0.498, ALU.mult, ALU.add))
                st.then(v.tensor_scalar(pk[:, 0, :], pk[:, 0, :], MAGIC, MAGIC, ALU.add, ALU.subtract))
                st.then(v.scalar_tensor_tensor(out=pk[:, 1, :], in0=pk[:, 0, :], scalar=-float(CHUNK), in1=pos,
                                               op0=ALU.mult, op1=ALU.add))
                dve.wait_ge(scat[c], cg * (8 * BPG * BC) + (16 + 16 * BC * (b // 2)))
                st.then(v.scalar_tensor_tensor(out=idx[:, c, :], in0=pk[:, 1, :], scalar=float(NCH), in1=pk[:, 0, :],
                                               op0=ALU.mult, op1=ALU.add))
                v.tensor_copy(rs[:, c, :, :], rec[:, bass.ds(cg * (BPG * BC) + b * BC, BC), :]).then_inc(rs_ok, 1)

            def attention(cg, j, st):
                for gg in range(5):
                    u = 5 * j + gg
                    dve.wait_ge(at_mm, cg * 20 + (u + 1))
                    pv = P[0:TT, 4 + u % 2, 0:2 * AW].rearrange("p (t c) -> p t c", t=2)
                    z = zt[:, u % 2, :, :]
                    st.then(v.tensor_scalar(z, pv[:, :, 128:130], 1e-6, None, ALU.add))
                    st.then(v.reciprocal(z, z))
                    if gg == 0 and j >= 2:
                        dve.wait_ge(sa_st[j % 2], cg * 32 + 16)
                    for t in range(2):
                        ins = v.tensor_tensor(sa[:, j % 2, 2 * gg + t, :].rearrange("p (h m) -> p h m", h=2),
                                              pv[:, t, 0:128].rearrange("p (h m) -> p h m", h=2),
                                              z[:, t, :, None].broadcast_to([TT, 2, 64]), ALU.mult)
                    ins.then_inc(at_evac, 1)

            with dve.Fori(0, HG) as cg, steps.loop(cg, HG, 2 * BPG + 4 * BPG + 2 * 20) as st:
                dve.wait_ge(bias_in, cg * 48 + 48)
                for i in range(NT):
                    dve.wait_ge(proj, cg * UNITS + (i + 1))
                    if i >= 2:
                        dve.wait_ge(phik_ok, cg * NT + (i - 1))
                    v.tensor_tensor(t_b[0:TT, i % 2, :], P[0:TT, i % 4, :], bkv[:, 0, :], ALU.add).then_inc(kv_evac, 1)
                    if i >= 1:
                        dve.wait_ge(er, cg * NT + i)
                        v.scalar_tensor_tensor(out=phik[:, i - 1, :], in0=e_b[0:TT, (i - 1) % 2, :], scalar=1.0,
                                               in1=t_b[0:TT, (i - 1) % 2, :], op0=ALU.min, op1=ALU.add).then_inc(phik_ok, 1)
                    if i == NT - 2:
                        split_lo(cg * 3 + 1, s0_hi, s0_lo)
                for i in range(NT):
                    dve.wait_ge(proj, cg * UNITS + (NT + i + 1))
                    if i >= 2:
                        dve.wait_ge(kv_mm, cg * NT + (i - 1))
                    v.tensor_tensor(vt[:, i % 2, :, 0:128], P[0:TT, (NT + i) % 4, :].rearrange("p (j c) -> p j c", j=PAIRS),
                                    bkv[:, 1, :].rearrange("p (j c) -> p j c", j=PAIRS), ALU.add).then_inc(kv_evac, 1)
                    if i == 0:
                        dve.wait_ge(er, cg * NT + NT)
                        v.scalar_tensor_tensor(out=phik[:, NT - 1, :], in0=e_b[0:TT, (NT - 1) % 2, :], scalar=1.0,
                                               in1=t_b[0:TT, (NT - 1) % 2, :], op0=ALU.min, op1=ALU.add).then_inc(phik_ok, 1)
                    if i >= 2:
                        if i >= 3:
                            records(cg, i - 3, st)
                        places(cg, i - 2, st)
                    if i == NT - 2:
                        split_lo(cg * 3 + 2, s0_hi, s0_lo)
                dve.wait_ge(kv_mm, cg * NT + NT)
                for h in range(2):
                    for a in range(2):
                        r = slice(64 * a, 64 * a + 64)
                        src = P[r, 4 + h, 0:2 * KVW].rearrange("p (j c) -> p j c", j=2)
                        v.tensor_copy(kvblk[r, 2 * h:2 * h + 2, 64 * a:64 * a + 64], src[:, :, 64 * a:64 * a + 64]).then_inc(kvblk_ok, 1)
                        v.tensor_copy(kvblk[r, 2 * h:2 * h + 2, 128 + a:129 + a], src[:, :, 128:129]).then_inc(kvblk_ok, 1)
                for q in range(3 * PAIRS):
                    j, a = q // 3, QCUT[q % 3]
                    n = QCUT[q % 3 + 1] - a
                    if q == 3 * PAIRS - 1:
                        split_lo(cg * 3 + 3, s0_hi, s0_lo)
                    dve.wait_ge(q_evac, cg * 12 + (q + 1))
                    if q % 3 == 0 and j >= 2:
                        dve.wait_ge(at_mm, cg * 20 + 5 * (j - 1))
                    ins = v.scalar_tensor_tensor(out=phiq[:, j % 2, a:a + n], in0=e_b[:, q % 2, 0:n], scalar=1.0,
                                                 in1=t_b[:, q % 2, 0:n], op0=ALU.min, op1=ALU.add)
                    ins.then_inc(phiq_ok, 1)
                    records(cg, q + 7, st)
                    places(cg, q + 8, st)
                    if q % 3 == 0 and j >= 1:
                        attention(cg, j - 1, st)
                records(cg, BPG - 1, st)
                attention(cg, PAIRS - 1, st)
                for c in range(2):
                    dve.wait_ge(sa_st[c], cg * 32 + 32)
                v.memset(mv[:, :], 0.0).then_inc(bias_free, 1)

            split_lo(7, s0_hi, s0_lo)
            step = NB * BW // 4
            for k in range(4):
                v.memset(adj[:, k * step:(k + 1) * step], 0.0)
            v.memset(rstd[:, 0:1], 0.0).then_inc(oh_free, 2)
            v.memset(rstd[:, 1:2], 0.0).then_inc(acc_free, 2)
            dve.wait_ge(acc_free, 2)
            dve.wait_ge(rl_in, 16)
            with dve.Fori(0, NCH // 2) as it:
                for c in range(2):
                    dve.wait_ge(oh_free, it * 2 + (c + 1))
                    v.tensor_scalar(ohs[:, c, 0:TT], iota[:, :], rl[:, bass.ds(it * 2 + c, 1), 0], None, ALU.is_equal)
                    v.tensor_scalar(ohd[:, c, 0:TT], iota[:, :], rl[:, bass.ds(it * 2 + c, 1), 1], None, ALU.is_equal).then_inc(oh_ok, 1)
                for c in range(2):
                    off = dve.value_load(offs[0:1, bass.ds(it * 2 + c, 1)], min_val=0, max_val=(NB - 1) * BW)
                    dve.wait_ge(ch_mm, it * 2 + (c + 1))
                    dve.wait_ge(acc_free, it * 2 + (c + 2))
                    blk = adj[:, bass.ds(off, BW)]
                    v.tensor_tensor(blk, blk, P[0:TT, 4 + c, 0:BW], ALU.add).then_inc(acc_free, 1)
            dve.wait_ge(acc_free, NCH + 2)
            a4 = adj[:, :].rearrange("p (d s c) -> p d s c", d=NT, s=NT)
            v.tensor_reduce(nrm[:, 0, :], a4[:, :, :, TT].rearrange("p d s -> p s d"), X, ALU.add)
            v.tensor_reduce(nrm[:, 1, :], a4[:, :, :, TT + 1].rearrange("p d s -> p s d"), X, ALU.add)
            v.tensor_reduce(nrm[:, 2, :], a4[:, :, :, TT + 2], X, ALU.add)
            steps.then(v.tensor_reduce(nrm[:, 3, :], a4[:, :, :, TT + 3], X, ALU.add))
            for k in range(4):
                ins = v.tensor_scalar(nrm[:, k, :], nrm[:, k, :], 1.0 if k % 2 else 1e-30, None, ALU.max)
            ins.then_inc(nrm_ok, 1)
            dve.wait_ge(nrm_sq, 1)
            for k in range(2):
                steps.then(v.tensor_tensor(nsc[:, k, :], nrm[:, 2 * k, :], nrm[:, 2 * k + 1, :], ALU.mult))
            v.reciprocal(nsc[:, :, :], nsc[:, :, :]).then_inc(nsc_ok, 1)
            dve.wait_ge(nsc_ok, 1)
            for j in range(NT):
                dve.wait_ge(yh_ok, j + 1)
                v.scalar_tensor_tensor(out=y_lo[:, j, :], in0=yraw[:, j % 4, :], scalar=nsc[:, 0, j:j + 1],
                                       in1=y_hi[:, j, :].bitcast(F32), op0=ALU.mult, op1=ALU.subtract).then_inc(yl_ok, 1)

            def adj_lo(i, h, k):
                dve.wait_ge(wh_ok, k)
                v.tensor_tensor(w_lo[:, 5 * h:5 * h + 5, :],
                                adj[:, bass.ds(i * (NT * BW) + h * (5 * BW), 5 * BW)].rearrange("p (j c) -> p j c", c=BW)[:, :, 0:TT],
                                w_hi[:, 5 * h:5 * h + 5, :].bitcast(F32), ALU.subtract).then_inc(wl_ok, 1)

            for h in range(2):
                adj_lo(0, h, h + 1)

            def adj_hi_dve(i, h, k):
                dve.wait_ge(wh_free, k)
                v.tensor_copy(w_hi[:, 5 * h:5 * h + 5, :],
                              adj[:, bass.ds(i * (NT * BW) + h * (5 * BW), 5 * BW)].rearrange("p (j c) -> p j c", c=BW)[:, :, 0:TT]).then_inc(wh_ok, 1)

            dve.wait_ge(bg_in, 16)

            def residual(i, c, n_res, st):
                dve.wait_ge(agg_mm, n_res)
                st.then(v.scalar_tensor_tensor(out=gt2[:, c, :], in0=P[0:TT, 2 * c:2 * c + 2, :].rearrange("p b n -> p (b n)"),
                                               scalar=nsc[:, 1, bass.ds(i, 1)], in1=bgb[:, :], op0=ALU.mult, op1=ALU.add))
                dve.wait_ge(res_ok, n_res)
                v.scalar_tensor_tensor(out=xt2[:, c, :], in0=gt2[:, c, :], scalar=0.0, in1=xt2[:, c, :],
                                       op0=ALU.max, op1=ALU.add).then_inc(x2_ok, 1)
                dve.wait_ge(x2_ok, n_res)
                normalize(st, xt2[:, c, :], at2[:, c, :], var2, std2, n_res).then_inc(h2_ok, 1)

            with dve.Fori(0, NT // 2 - 1) as it, steps.loop(it, NT // 2 - 1, 8) as st:
                for c in range(2):
                    for h in range(2):
                        adj_hi_dve(it * 2 + (c + 1), h, it * 4 + (2 * c + h + 1))
                        adj_lo(it * 2 + (c + 1), h, it * 4 + (2 * c + h + 3))
                    residual(it * 2 + c, c, it * 2 + (c + 1), st)
            for h in range(2):
                adj_hi_dve(NT - 1, h, 2 * (NT - 2) + h + 1)
                adj_lo(NT - 1, h, 2 * (NT - 1) + h + 1)
            for c in range(2):
                residual(NT - 2 + c, c, NT - 1 + c, steps)

            s = small
            with dve.Fori(0, NT // 2) as it:
                for c in range(2):
                    dve.wait_ge(lg_mm, it * 2 + (c + 1))
                    v.tensor_copy(s["lg"][:, bass.ds(it * 2 + c, 1), :], P[0:TT, 4 + c, None, 0:NX]).then_inc(lg_evac, 1)
            dve.wait_ge(lg_evac, NT)

            def per_token(a):
                return a[:, :, None].broadcast_to([TT, NT, NX])

            def per_expert(a):
                return a[:, None, :].broadcast_to([TT, NT, NX])

            steps.then(v.tensor_reduce(s["m1"][:, :], s["lg"][:, :, :], X, ALU.max))
            v.tensor_tensor(s["pr"][:, :, :], s["lg"][:, :, :], per_token(s["m1"]), ALU.subtract).then_inc(dmax_ok, 1)
            dve.wait_ge(exp_ok, 1)
            steps.then(v.tensor_reduce(s["den"][:, :], s["pr"][:, :, :], X, ALU.add))
            steps.then(v.reciprocal(s["den"][:, :], s["den"][:, :]))
            steps.then(v.tensor_tensor(s["pr"][:, :, :], s["pr"][:, :, :], per_token(s["den"]), ALU.mult))
            dve.wait_ge(const_ok, 12)
            for m, oh in (("m1", "ohe1"), ("m2", "ohe2")):
                steps.then(v.tensor_reduce(s[m][:, :], s["pr"][:, :, :], X, ALU.max))
                steps.then(v.tensor_tensor(s["cand"][:, :, :], s["pr"][:, :, :], per_token(s[m]), ALU.is_equal))
                steps.then(v.tensor_tensor(s["cand"][:, :, :], s["cand"][:, :, :], per_expert(io8), ALU.mult))
                steps.then(v.tensor_reduce(s["cm"][:, :], s["cand"][:, :, :], X, ALU.min))
                steps.then(v.tensor_tensor(s[oh][:, :, :], per_expert(io8), per_token(s["cm"]), ALU.is_equal))
                if m == "m1":
                    steps.then(v.scalar_tensor_tensor(out=s["pr"][:, :, :], in0=s[oh][:, :, :], scalar=-2.0, in1=s["pr"][:, :, :],
                                                      op0=ALU.mult, op1=ALU.add))
            steps.then(v.tensor_tensor(s["den"][:, :], s["m1"][:, :], s["m2"][:, :], ALU.add))
            steps.then(v.tensor_scalar(s["den"][:, :], s["den"][:, :], EPS, None, ALU.max))
            steps.then(v.reciprocal(s["den"][:, :], s["den"][:, :]))
            v.tensor_tensor(s["wk1"][:, :], s["m1"][:, :], s["den"][:, :], ALU.mult)
            steps.then(v.tensor_tensor(s["wk2"][:, :], s["m2"][:, :], s["den"][:, :], ALU.mult))
            steps.then(v.scalar_tensor_tensor(out=s["v"][:, :, :], in0=s["ohe1"][:, :, :], scalar=-1.0, in1=s["ohe2"][:, :, :],
                                              op0=ALU.add, op1=ALU.add))
            for w, oh in (("wk1", "ohe1"), ("wk2", "ohe2")):
                steps.then(v.tensor_tensor(s["cand"][:, :, :], s[oh][:, :, :], per_token(s[w]), ALU.mult))
                steps.then(v.tensor_tensor(s["v"][:, :, :], s["v"][:, :, :], s["cand"][:, :, :], ALU.add))
            with dve.Fori(0, NT // 2) as it:
                for c in range(2):
                    for h in range(2):
                        if h == 0:
                            dve.wait_ge(vb_ok, it * 2 + c) if False else None
                    v.tensor_tensor(diag[:, c, :, :], ident[0:TT, None, 0:TT].broadcast_to([TT, NX, TT]),
                                    s["v"][:, bass.ds(it * 2 + c, 1), :].rearrange("p a e -> p (a e)")[:, :, None].broadcast_to([TT, NX, TT]),
                                    ALU.mult).then_inc(diag_ok, 1)
                    dve.wait_ge(vb_mm, it * 2 + (c + 1))
            dve.wait_ge(vb_ok, NT)
            with dve.Fori(0, NX // 2) as it:
                for c in range(2):
                    e = it * 2 + c
                    if c == 0:
                        dve.wait_ge(cs_mm, it * 2 + 0) if False else None
                    at_ = 0
                    for i in range(NT):
                        vi = s["v"][:, i, bass.ds(e, 1)]
                        if i:
                            v.tensor_scalar(cmpm[:, c, at_:at_ + i * TT], vb[:, bass.ds(e, 1), 0:i * TT].rearrange("p a t -> p (a t)"),
                                            vi, None, ALU.is_ge, ALU.add, accum_out=s["r1"][:, i, bass.ds(e, 1)])
                        v.scalar_tensor_tensor(out=cmpm[:, c, at_ + i * TT:at_ + (i + 1) * TT],
                                               in0=vb[:, bass.ds(e, 1), i * TT:(i + 1) * TT].rearrange("p a t -> p (a t)"),
                                               scalar=vi, in1=lower[:, :], op0=ALU.is_ge, op1=ALU.mult,
                                               accum_out=s["r2"][:, i, bass.ds(e, 1)]).then_inc(cmp_ok, 1)
                        at_ += (i + 1) * TT
                    dve.wait_ge(cs_mm, e + 1)
            steps.then(v.memset(s["r1"][:, 0, :], 0.0))
            steps.then(v.tensor_tensor(s["rank"][:, :, :], s["r1"][:, :, :], s["r2"][:, :, :], ALU.add))
            steps.then(v.tensor_tensor(s["rank"][:, :, :], s["rank"][:, :, :],
                                       P[0:TT, 6, 0:NT * NX].rearrange("p (i e) -> p i e", e=NX), ALU.subtract))
            steps.then(v.tensor_tensor(s["rank"][:, :, :], s["rank"][:, :, :], per_token(s["left"]), ALU.add))
            v.tensor_scalar(s["keep"][:, :, :], s["rank"][:, :, :], float(CAP), None, ALU.is_lt)
            steps.then(v.tensor_scalar(s["rank"][:, :, :], s["rank"][:, :, :], float(CAP), None, ALU.min))
            steps.then(v.tensor_tensor(s["rank"][:, :, :], s["rank"][:, :, :], per_expert(io392), ALU.add))
            for k, (oh, sl, kp) in enumerate((("ohe1", "sl1", "kp1"), ("ohe2", "sl2", "kp2"))):
                steps.then(v.tensor_tensor(s["cand"][:, :, :], s[oh][:, :, :], s["rank"][:, :, :], ALU.mult))
                steps.then(v.tensor_reduce(s[sl][:, :], s["cand"][:, :, :], X, ALU.add))
                steps.then(v.tensor_tensor(s["cand"][:, :, :], s[oh][:, :, :], s["keep"][:, :, :], ALU.mult))
                steps.then(v.tensor_reduce(s[kp][:, :], s["cand"][:, :, :], X, ALU.add))
                steps.then(v.tensor_copy(gidx[:, k, :], s[sl][:, :]))
                steps.then(v.tensor_scalar(s["cm"][:, :], s[kp][:, :], -100000.0, 100000.0, ALU.mult, ALU.add))
                ins = v.tensor_tensor(sidx[:, k, :], s[sl][:, :], s["cm"][:, :], ALU.add)
                if k == 0:
                    steps.then(ins)
            ins.then_inc(sidx_ok, 1)
            v.tensor_tensor(s["wk1"][:, :], s["wk1"][:, :], s["kp1"][:, :], ALU.mult)
            steps.then(v.tensor_tensor(s["wk2"][:, :], s["wk2"][:, :], s["kp2"][:, :], ALU.mult))
            steps.then(v.tensor_tensor(s["den"][:, :], s["wk1"][:, :], s["wk2"][:, :], ALU.add))
            steps.then(v.tensor_scalar(s["den"][:, :], s["den"][:, :], EPS, None, ALU.max))
            steps.then(v.reciprocal(s["den"][:, :], s["den"][:, :]))
            v.tensor_tensor(s["wk1"][:, :], s["wk1"][:, :], s["den"][:, :], ALU.mult)
            steps.then(v.tensor_tensor(s["wk2"][:, :], s["wk2"][:, :], s["den"][:, :], ALU.mult))

            def ex_split_lo(e1):
                for h in range(HC):
                    dve.wait_ge(exh, e1 * 8 + (h + 1))
                    v.tensor_tensor(ex_lo[:, h, :], P[:, h % 2, 0:CAPR], ex_hi[:, h, :].bitcast(F32), ALU.subtract).then_inc(exl, 1)

            def moe_lo(e, k, hi, lo):
                for q in range(8):
                    dve.wait_ge(hi_ok, e * 24 + (MOE + 8 * k + q + 1))
                    v.tensor_tensor(lo[:, q, :], raw[:, q, :], hi[:, q, :].bitcast(F32), ALU.subtract).then_inc(lo_ok, 1)

            def swiglu(e, st):
                for m in range(FC):
                    dve.wait_ge(sg_ok, e * FC + (m + 1))
                    v.tensor_tensor(gf[:, m % 2, :], sg[:, m % 2, :], P[:, 2 + m % 2, 0:CAPR], ALU.mult).then_inc(gf_ok, 1)
                    dve.wait_ge(gh_ok, e * FC + (m + 1))
                    v.tensor_tensor(g_lo[:, m, :], gf[:, m % 2, :], g_hi[:, m, :].bitcast(F32), ALU.subtract).then_inc(gl_ok, 1)

            def results(e):
                for u in range(8):
                    dve.wait_ge(dn_mm, e * 8 + (u + 1))
                    if u >= 4:
                        dve.wait_ge(eo_st[u % 4], e * 32 + 16)
                    v.tensor_copy(eo[:, u % 4, :], P[0:CA, 6 + u % 2, :]).then_inc(eo_ok, 1)
                for c in range(4):
                    dve.wait_ge(eo_st[c], e * 32 + 32)

            moe_lo(0, 0, s0_hi, s0_lo)
            dve.wait_ge(ein_st, 16 * 2 * NT)
            dve.wait_ge(cs_mm, NX)
            moe_lo(0, 1, s1_hi, s1_lo)
            moe_lo(0, 2, s2_hi, s2_lo)
            ex_split_lo(0)
            with dve.Fori(0, NX - 1) as e:
                swiglu(e, None)
                moe_lo(e + 1, 0, s0_hi, s0_lo)
                moe_lo(e + 1, 1, s1_hi, s1_lo)
                ex_split_lo(e + 1)
                results(e)
                moe_lo(e + 1, 2, s2_hi, s2_lo)
            swiglu(NX - 1, None)
            results(NX - 1)
            for i in range(NT):
                c = i % 2
                dve.wait_ge(g1_in[c], 32 * (i // 2 + 1))
                dve.wait_ge(x2_in[c], 16 * (i // 2 + 1))
                steps.then(v.scalar_tensor_tensor(out=x2t[:, c, :], in0=r1t[:, c, :], scalar=s["wk1"][:, i:i + 1], in1=x2t[:, c, :],
                                                  op0=ALU.mult, op1=ALU.add))
                v.scalar_tensor_tensor(out=x2t[:, c, :], in0=r2t[:, c, :], scalar=s["wk2"][:, i:i + 1], in1=x2t[:, c, :],
                                       op0=ALU.mult, op1=ALU.add).then_inc(o_ok, 1)

        @block.tensor
        def _(pe):
            mm = nc.tensor.matmul

            def three(out, lh, ll, rh, rl_, first, last):
                mm(out, lh, rh, start=first, stop=False)
                mm(out, lh, rl_, start=False, stop=False)
                return mm(out, ll, rh, start=False, stop=last)

            pe.wait_ge(const_ok, 9)
            with pe.Fori(0, NT // 2) as it:
                for c in range(2):
                    pe.wait_ge(xn_ok, it * 2 + (c + 1))
                    for h in range(HC):
                        ins = nc.tensor.transpose(P[:, 2 * c + h // 4, (h % 4) * TT:(h % 4 + 1) * TT],
                                                  xin[:, c, h * 128:(h + 1) * 128], ident[0:TT, 0:TT])
                    ins.then_inc(tr_done, 1)
                    pe.wait_ge(lo_x, it * 2 + (c + 1))
            pe.wait_ge(ohb_ok, 2)
            for k in range(EC // 8):
                ins = mm(P[0:80, 7, 0:80], oh_d[:, 8 * k:8 * k + 8, :].rearrange("p a b -> p (a b)"),
                         oh_s[:, 8 * k:8 * k + 8, :].rearrange("p a b -> p (a b)"), start=(k == 0), stop=(k == EC // 8 - 1))
            ins.then_inc(graph_mm, 1)
            pe.wait_ge(gstep, 1)
            mm(P[0:NT, 7, 128:128 + NT], sel80[:, :], hs[:, :], start=True, stop=True).then_inc(graph_mm, 1)
            pe.wait_ge(gstep, 3)
            mm(P[0:NB, 7, 160:161], upper[:, :], nch[:, 0:1], start=True, stop=True).then_inc(graph_mm, 1)
            pe.wait_ge(gstep, 4)
            mm(P[0:1, 6, 0:NCH], ones[0:NB, 0:1], ge[:, :], start=True, stop=True).then_inc(graph_mm, 1)
            pe.wait_ge(gstep, 6)

            def positions(cg, b):
                pe.wait_ge(sm_ok, cg * BPG + (b + 1))
                for c in range(BC):
                    ins = mm(P[0:TT, 7, 256 + c:257 + c], sm[:, c * TT:(c + 1) * TT], ones[0:NB, 0:1], start=True, stop=True)
                ins.then_inc(graph_mm, 1)

            def row_tile(out, i, g, first, last):
                for s in range(8):
                    if first:
                        pe.wait_ge(lo_ok, g * 8 + (s + 1))
                    ins = three(out, xt_hi[:, s, i * TT:(i + 1) * TT], xt_lo[:, s, i * TT:(i + 1) * TT],
                                s0_hi[:, s, :], s0_lo[:, s, :], s == 0, s == 7)
                    if last and s < 7:
                        ins.then_inc(w_used, 1)
                return ins

            def kv_tile(cg, i):
                pe.wait_ge(kv_evac, cg * 20 + (NT + i + 1))
                pe.wait_ge(phik_ok, cg * NT + (i + 1))
                if i == 0:
                    pe.wait_ge(at_evac, cg * 20 + 1)
                for j in range(PAIRS):
                    ins = mm(P[:, 4 + j // 2, (j % 2) * KVW:(j % 2 + 1) * KVW], phik[:, i, j * 128:(j + 1) * 128],
                             vt[:, i % 2, j, :], start=(i == 0 and j % 2 == 0), stop=(i == NT - 1), skip_group_check=True)
                ins.then_inc(kv_mm, 1)

            def attend(cg, j):
                pe.wait_ge(phiq_ok, cg * 12 + 3 * (j + 1))
                if j == 0:
                    pe.wait_ge(kvblk_ok, cg * 8 + 8)
                for gg in range(5):
                    u = 5 * j + gg
                    if u >= 2:
                        pe.wait_ge(at_evac, cg * 20 + u)
                    for t in range(2):
                        i = 2 * gg + t
                        ins = mm(P[0:TT, 4 + u % 2, t * AW:(t + 1) * AW], phiq[:, j % 2, i * TT:(i + 1) * TT],
                                 kvblk[:, j, :], start=True, stop=True)
                    ins.then_inc(at_mm, 1)

            with pe.Fori(0, HG) as cg:
                for i in range(NT):
                    if i >= 4:
                        pe.wait_ge(kv_evac, cg * 20 + (i - 3))
                    ins = row_tile(P[0:TT, i % 4, :], i, cg * 3, i == 0, i == NT - 1)
                    ins.then_inc(proj, 1)
                    if i == NT - 1:
                        pe.wait_ge(proj, cg * UNITS + (i + 1))
                        pe.nop().then_inc(w_used, 1)
                for i in range(NT):
                    pe.wait_ge(kv_evac, cg * 20 + (NT + i - 3))
                    ins = row_tile(P[0:TT, (NT + i) % 4, :], i, cg * 3 + 1, i == 0, i == NT - 1)
                    ins.then_inc(proj, 1)
                    if i == NT - 1:
                        pe.wait_ge(proj, cg * UNITS + (NT + i + 1))
                        pe.nop().then_inc(w_used, 1)
                    if i >= 1:
                        kv_tile(cg, i - 1)
                    if i >= 3:
                        positions(cg, i - 3)
                kv_tile(cg, NT - 1)
                for q in range(3 * PAIRS):
                    j, a = q // 3, QCUT[q % 3]
                    n = QCUT[q % 3 + 1] - a
                    if q < 4:
                        pe.wait_ge(kv_evac, cg * 20 + (2 * NT - 3 + q))
                    else:
                        pe.wait_ge(q_evac, cg * 12 + (q - 3))
                    for s in range(8):
                        if q == 0:
                            pe.wait_ge(lo_ok, cg * 24 + (16 + s + 1))
                        ins = three(P[:, q % 4, 0:n], s0_hi[:, s, j * 128:(j + 1) * 128], s0_lo[:, s, j * 128:(j + 1) * 128],
                                    xt_hi[:, s, a:a + n], xt_lo[:, s, a:a + n], s == 0, s == 7)
                        if q == 3 * PAIRS - 1 and s < 7:
                            ins.then_inc(w_used, 1)
                    ins.then_inc(proj, 1)
                    if q == 3 * PAIRS - 1:
                        pe.wait_ge(proj, cg * UNITS + UNITS)
                        pe.nop().then_inc(w_used, 1)
                    positions(cg, q + 7)
                    if q % 3 == 0 and j >= 1:
                        attend(cg, j - 1)
                positions(cg, BPG - 1)
                attend(cg, PAIRS - 1)
            for g in range(2):
                for i in range(NT):
                    n = g * NT + i
                    if n >= 4:
                        pe.wait_ge(g_evac, n - 3)
                    ins = row_tile(P[0:TT, n % 4, :], i, 6 + g, i == 0, i == NT - 1)
                    ins.then_inc(proj, 1)
                    if i == NT - 1:
                        pe.wait_ge(proj, HG * UNITS + n + 1)
                        pe.nop().then_inc(w_used, 1)
            with pe.Fori(0, NCH // 2) as it:
                for c in range(2):
                    pe.wait_ge(mv_ok, it * 2 + (c + 1))
                    pe.wait_ge(acc_free, it * 2 + (c + 1))
                    mm(P[0:TT, 4 + c, 0:TT + 2], ohs[:, c, 0:TT], mvt[:, c, 0:TT + 2], start=True, stop=True)
                    mm(P[0:TT, 4 + c, TT + 2:TT + 4], ohd[:, c, 0:TT], mvt[:, c, TT:TT + 2], start=True, stop=True).then_inc(ch_mm, 1)
                    pe.wait_ge(ch_mm, it * 2 + (c + 1))
                    pe.nop().then_inc(oh_free, 1)
            def aggregate(c, it, h0):
                for j in range(NT):
                    pe.wait_ge(yl_ok, j + 1)
                    if j % 5 == 0:
                        pe.wait_ge(wl_ok, it * 4 + (2 * c + j // 5 + 1))
                    for h in range(2):
                        ins = three(P[0:TT, 2 * c + h, :], w_hi[:, j, :], w_lo[:, j, :], y_hi[:, j, h * SC:(h + 1) * SC],
                                    y_lo[:, j, h * SC:(h + 1) * SC], j == 0, j == NT - 1)
                    if j == 4:
                        ins.then_inc(wh_free, 1)
                ins.then_inc(agg_mm, 1)

            pe.wait_ge(g_evac, 2 * NT)
            with pe.Fori(0, NT // 2) as it:
                for c in range(2):
                    if c == 0:
                        pass
                    aggregate(c, it, 0)
                    pe.wait_ge(agg_mm, it * 2 + (c + 1))
                    pe.nop().then_inc(wh_free, 1)
                    pe.wait_ge(x2_ok, it * 2 + c) if False else None
            pe.wait_ge(x2_ok, NT)
            pe.wait_ge(h2_in, 16)
            pe.wait_ge(wr_in, 16)
            for i in range(NT):
                c = i % 2
                for h in range(HC):
                    ins = nc.tensor.transpose(P[:, 2 * c + h // 4, (h % 4) * TT:(h % 4 + 1) * TT],
                                              h2a[:, i, h * 128:(h + 1) * 128], ident[0:TT, 0:TT])
                ins.then_inc(tr2, 1)
                pe.wait_ge(h2t_ok, i + 1)
                for h in range(HC):
                    ins = mm(P[0:TT, 4 + c, 0:NX], h2t[:, c, h, :], wrt[:, h, :], start=(h == 0), stop=(h == HC - 1))
                ins.then_inc(lg_mm, 1)
                pe.wait_ge(lg_evac, i + 1)
            with pe.Fori(0, NT // 2) as it:
                for c in range(2):
                    pe.wait_ge(diag_ok, it * 2 + (c + 1))
                    for h in range(2):
                        ins = mm(P[0:TT, 2 * c + h, 0:500], ones[0:TT, 0:TT], diag[:, c, 4 * h:4 * h + 4, :].rearrange("p a b -> p (a b)"),
                                 start=True, stop=True)
                    ins.then_inc(vb_mm, 1)
                    pe.wait_ge(vb_ok, it * 2 + (c + 1))
            with pe.Fori(0, NX // 2) as it:
                for c in range(2):
                    at_ = 0
                    for i in range(NT):
                        pe.wait_ge(cmp_ok, it * 20 + (c * NT + i + 1))
                        for j in range(i + 1):
                            ins = mm(P[0:TT, 6, bass.ds(it * 2 + (c + j * NX), 1)], cmpm[:, c, at_ + j * TT:at_ + (j + 1) * TT],
                                     onesb[0:TT, 0:1], start=(i == 0), stop=(i == NT - 1), skip_group_check=True)
                        at_ += (i + 1) * TT
                    ins.then_inc(cs_mm, 1)

            def transposes(e1):
                pe.wait_ge(rows_in, e1 * 16 + 16)
                for h in range(HC):
                    if h >= 2:
                        pe.wait_ge(exl, e1 * 8 + (h - 1))
                    for a in range(4):
                        ins = nc.tensor.transpose(P[:, h % 2, a * CA:(a + 1) * CA], rows[:, a, h * 128:(h + 1) * 128], ident[0:CA, 0:CA])
                    ins.then_inc(etr, 1)

            def up(e):
                for m in range(FC):
                    ms = slice(m * 128, (m + 1) * 128)
                    if m >= 2:
                        pe.wait_ge(gf_ok, e * FC + (m - 1))
                    for k, (hi, lo) in enumerate(((s0_hi, s0_lo), (s1_hi, s1_lo))):
                        for h in range(HC):
                            if m == 0:
                                pe.wait_ge(lo_ok, e * 24 + (MOE + 8 * k + h + 1))
                                if k == 0:
                                    pe.wait_ge(exl, e * 8 + (h + 1))
                            ins = three(P[:, 2 + 2 * k + m % 2, 0:CAPR], hi[:, h, ms], lo[:, h, ms], ex_hi[:, h, :], ex_lo[:, h, :],
                                        h == 0, h == HC - 1)
                            if m == FC - 1 and not (k == 1 and h == HC - 1):
                                ins.then_inc(w_used, 1)
                    ins.then_inc(pg_mm, 1)
                pe.wait_ge(pg_mm, e * FC + FC)
                pe.nop().then_inc(w_used, 1)

            def down(e):
                for u in range(8):
                    a, h = u // 2, u % 2
                    if u >= 2:
                        pe.wait_ge(eo_ok, e * 8 + (u - 1))
                    for d in range(FC):
                        if u < 2:
                            pe.wait_ge(lo_ok, e * 24 + (MOE + 16 + 2 * d + h + 1))
                        if u == 0:
                            pe.wait_ge(gl_ok, e * FC + (d + 1))
                        ins = three(P[0:CA, 6 + u % 2, :], g_hi[:, d, a * CA:(a + 1) * CA], g_lo[:, d, a * CA:(a + 1) * CA],
                                    s2_hi[:, 2 * d + h, :], s2_lo[:, 2 * d + h, :], d == 0, d == FC - 1)
                    ins.then_inc(dn_mm, 1)
                pe.wait_ge(dn_mm, e * 8 + 8)
                pe.nop().then_inc(w_used, 8)

            transposes(0)
            with pe.Fori(0, NX - 1) as e:
                up(e)
                transposes(e + 1)
                down(e)
            up(NX - 1)
            down(NX - 1)


def kernel(x, src, dst, edge_weight, L0_gnn_W, L0_gnn_b, L0_mix_W_qkv, L0_mix_b_qkv, L0_mix_W_proj, L0_mix_b_proj,
           L0_ffn_router_weight, L0_ffn_ff_pre_act_weight, L0_ffn_gate_weight, L0_ffn_ff_post_act_weight):
    import numpy as np
    import concourse.bacc as bacc
    from concourse.bass_utils import run_bass_kernel_spmd as run

    n = np.asarray
    src, dst, qkv, gw = n(src), n(dst), n(L0_mix_W_qkv), n(L0_gnn_W)
    parts = []
    for g in range(HG):
        c = slice(g * SC, (g + 1) * SC)
        parts += [qkv[:, D:2 * D][:, c], qkv[:, 2 * D:][:, c], qkv[:, :D][:, c]]
    parts += [gw[:, :SC], gw[:, SC:]]
    pre, gate, post = n(L0_ffn_ff_pre_act_weight), n(L0_ffn_gate_weight), n(L0_ffn_ff_post_act_weight)
    arrays = {
        "x": n(x),
        "edges_n": np.stack([src.reshape(TT, EC), dst.reshape(TT, EC)]),
        "edges_c": np.stack([np.ascontiguousarray(src.reshape(EC, TT).T), np.ascontiguousarray(dst.reshape(EC, TT).T)]),
        "w_c": np.ascontiguousarray(n(edge_weight).reshape(EC, TT).T),
        "wmain": np.stack(parts),
        "bqkv": n(L0_mix_b_qkv),
        "bg": n(L0_gnn_b),
        "wr_t": np.ascontiguousarray(n(L0_ffn_router_weight).T.reshape(HC, 128, NX).transpose(1, 0, 2)).reshape(128, HC * NX),
        "wpre": np.ascontiguousarray(pre.transpose(0, 2, 1).reshape(NX, HC, 128, DFF).transpose(2, 0, 1, 3)),
        "wgate": np.ascontiguousarray(gate.transpose(0, 2, 1).reshape(NX, HC, 128, DFF).transpose(2, 0, 1, 3)),
        "wpost": np.ascontiguousarray(post.transpose(0, 2, 1).reshape(NX, FC, 128, 2, SC).transpose(2, 0, 1, 3, 4)).reshape(128, NX, 8, SC),
    }
    nc = bacc.Bacc("TRN2", target_bir_lowering=False, num_devices=1)
    args = [nc.dram_tensor(k, a.shape, mybir.dt.from_np(a.dtype), kind="ExternalInput").ap() for k, a in arrays.items()]
    out = nc.dram_tensor("out", [T, D], F32, kind="ExternalOutput").ap()
    build(nc, *args, out)
    r = run(nc, [arrays], core_ids=[0])
    return r.results[0]["out"]
```

```python
from contextlib import ExitStack, contextmanager

import concourse.bass as bass
from concourse import mybir

F32 = mybir.dt.float32
FR = mybir.dt.float32r
BF16 = mybir.dt.bfloat16
I32 = mybir.dt.int32
ALU = mybir.AluOpType
ACT = mybir.ActivationFunctionType
X = mybir.AxisListType.X

T = 1250
TT = 125
NT = T // TT
D = 1024
HC = D // 128
SC = 512
NG = 8
HG = 2
PAIRS = 4
KVW = 129
AW = 130
QCUT = [0, 418, 834, 1250]
UNITS = 2 * NT + 3 * PAIRS

NE = 40000
EC = NE // TT
BC = 8
EB = BC * TT
NBLK = EC // BC
BPG = NBLK // HG
NB = NT * NT
CHUNK = 128
CG = 4
NCH = -(-((NE + NB * (CHUNK - 1)) // CHUNK) // 8) * 8
NGR = NCH // CG
GT0 = 3
GL = (NGR - 2) // (2 * NT - GT0) // 2
BW = 129
MAGIC = 1.5 * 2.0**23

NX = 8
DFF = 512
FC = DFF // 128
CAP = 391
CAPR = CAP + 1
CA = CAPR // 4
ZP = 112
ZN = NX * CAPR // ZP // 4
EPS = 1.1920929e-07
LNEPS = 1e-05


class Count:

    def __init__(self, engine, sem):
        self.engine, self.sem, self.n = engine, sem, 0

    def then(self, instruction):
        instruction.then_inc(self.sem, 1)
        self.n = self.n + 1
        self.engine.wait_ge(self.sem, self.n)

    @contextmanager
    def loop(self, it, times, per):
        start = self.n
        self.n = start + it * per
        self.used = 0
        before = self.n
        inner = Body(self, before, per)
        yield inner
        assert inner.k == per, f"the body raises its semaphore {inner.k} times"
        self.n = start + times * per


class Body:
    def __init__(self, count, base, per):
        self.count, self.base, self.k = count, base, 0

    def then(self, instruction):
        instruction.then_inc(self.count.sem, 1)
        self.k += 1
        self.count.engine.wait_ge(self.count.sem, self.base + self.k)


def build(nc, x, edges_n, edges_c, w_c, wmain, bqkv, bg, wr_t, wpre, wgate, wpost, out, debug=None):
    with ExitStack() as ctx:
        names = [0]

        def at(off, shape, dt, name):
            t = nc.alloc_sbuf_tensor_at(name, shape, dt, offset=BASE + off)
            size = 4 if dt != BF16 else 2
            for n in shape[1:]:
                size *= n
            assert BASE + off + size <= nc.sbuf_usable_end, (name, BASE + off + size - nc.sbuf_usable_end)
            return t

        def sem(name):
            return ctx.enter_context(nc.semaphore(name))

        def dram(name, shape, dt=F32):
            return nc.dram_tensor(name, shape, dt).ap()

        BASE = -(-nc.sbuf_base // 32) * 32
        A = 0
        SL = A + 81920
        RAW = SL + 32768
        WR = RAW + 16384
        RR = WR + NB * BW * 4 + 16
        RR = -(-RR // 32) * 32
        xt_hi = at(A, [128, HC, T], FR, "xt_hi")
        xt_lo = at(A + 40000, [128, HC, T], FR, "xt_lo")
        s0_hi = at(SL, [128, 8, SC], FR, "s0_hi")
        s0_lo = at(SL + 16384, [128, 8, SC], FR, "s0_lo")
        raw = at(RAW, [128, 8, SC], F32, "raw")

        xin = at(WR, [TT, 2, D], F32, "xin")
        en = at(WR + 8192, [TT, 2, EC], I32, "en")
        ec = at(WR + 10752, [TT, 2, EC], I32, "ec")
        wc = at(WR + 13312, [TT, EC], F32, "wc")
        tn = at(WR + 14592, [TT, 3, EC], F32, "tn")
        tc = at(WR + 18432, [TT, 3, EC], F32, "tc")
        bkt = at(WR + 22272, [TT, EC], BF16, "bkt")
        oh_d = at(WR + 22912, [TT, EC, NT], BF16, "oh_d")
        oh_s = at(WR + 29312, [TT, EC, NT], BF16, "oh_s")
        hq = at(WR + 35712, [80, 8, NT], F32, "hq")
        mask80 = at(WR + 36032, [80, 8, NT], F32, "mask80")
        hs = at(WR + 36352, [80, NT], F32, "hs")
        sel80 = at(WR + 36416, [80, NT], F32, "sel80")
        hist10 = at(WR + 36480, [NT, NT], F32, "hist10")
        upper = at(WR + 36544, [NB, NB], F32, "upper")
        iotak = at(WR + 36960, [NB, NCH], F32, "iotak")
        ge = at(WR + 38624, [NB, NCH], F32, "ge")
        phik = at(WR, [TT, NT, SC], F32, "phik")
        vt = at(WR + 20480, [TT, 2, PAIRS, KVW], F32, "vt")
        phiq = at(WR + 24640, [128, 2, T], F32, "phiq")
        sa = at(WR + 34656, [TT, 2, NT, 128], F32, "sa")
        kvblk = at(WR + 44896, [128, PAIRS, AW], F32, "kvblk")
        bkv = at(WR + 46976, [TT, 2, SC], F32, "bkv")
        bq = at(WR + 51072, [128, PAIRS], F32, "bq")
        adj = at(WR, [TT, NB * BW], F32, "adj")
        h2a = at(WR, [TT, NT, D], F32, "h2a")
        s1_hi = at(WR, [128, 8, SC], FR, "s1_hi")
        s1_lo = at(WR + 16384, [128, 8, SC], FR, "s1_lo")
        g_hi = at(WR + 32768, [128, FC, CAPR], FR, "g_hi")
        g_lo = at(WR + 39040, [128, FC, CAPR], FR, "g_lo")

        o = RR
        def take(nbytes):
            nonlocal o
            r = o
            o += -(-nbytes // 32) * 32
            return r
        ident = at(take(512), [128, 128], F32, "ident")
        ones = at(take(512), [128, 128], F32, "ones")
        onesb = at(take(4), [128, 2], BF16, "onesb")
        iota = at(take(500), [128, TT], F32, "iota")
        iotap = at(take(4), [128, 1], F32, "iotap")
        lower = at(take(500), [TT, TT], F32, "lower")
        zero = at(take(2048), [128, SC], F32, "zero")
        offs = at(take(NCH * 4), [1, NCH], I32, "offs")
        stats = at(take(48), [TT, 2, 6], F32, "stats")
        mv = at(take(8), [TT, 2], F32, "mv")
        rstd = at(take(8), [TT, 2], F32, "rstd")
        nrm = at(take(160), [TT, 4, NT], F32, "nrm")
        nsc = at(take(80), [TT, 2, NT], F32, "nsc")
        hist = at(take(4), [NB, 1], F32, "hist")
        nch = at(take(8), [NB, 2], F32, "nch")
        incl = at(take(4), [NB, 1], F32, "incl")
        base1 = at(take(4), [NB, 1], F32, "base1")
        carry = at(take(4), [NB, 1], F32, "carry")
        zt = at(take(32), [TT, 2, 2, 2], F32, "zt")
        pw = at(take(4), [1, 1], F32, "pw")
        CST = o
        br = at(take(4000), [NB, 2, EB], BF16, "br")
        oht = at(take(2000), [NB, EB], BF16, "oht")
        sm = at(take(4000), [NB, EB], F32, "sm")
        RECO = o
        rec = at(take(EC * 16), [TT, EC, 4], F32, "rec")
        PKO = o
        pk = at(take(64), [TT, 2, BC], F32, "pk")
        idx = at(take(64), [TT, 2, BC], I32, "idx")
        rs = at(take(256), [TT, 2, BC, 4], F32, "rs")
        t_b = at(take(4096), [128, 2, SC], F32, "t_b")
        EBO = o
        e_b = at(take(4096), [128, 2, SC], F32, "e_b")
        rl = at(CST, [128, NCH, 4], F32, "rl")
        ohd = at(CST + 6656, [128, 2, CG, 128], F32, "ohd")
        ohs = at(CST + 10752, [128, 2, CG, 128], F32, "ohs")
        assert NCH * 16 <= 6656 and CST + 14848 <= PKO
        mvt = at(EBO, [128, 2, CG, 128], F32, "mvt")
        y_hi = at(A, [TT, NT, D], FR, "y_hi")
        y_lo = at(A + 40960, [TT, NT, D], FR, "y_lo")
        yraw = at(RAW, [TT, 4, D], F32, "yraw")
        w_hi = at(CST, [TT, NT, TT], FR, "w_hi")
        w_lo = at(CST + 5024, [TT, NT, TT], FR, "w_lo")
        bgb = at(SL, [TT, D], F32, "bgb")
        xt2 = at(SL + 4096, [TT, 2, D], F32, "xt2")
        at2 = at(SL + 12288, [TT, 2, D], F32, "at2")
        gt2 = at(SL + 20480, [TT, 2, D], F32, "gt2")
        h2t = at(SL + 28672, [128, HC, TT], F32, "h2t")
        diag = at(SL + 8320, [TT, 2, NX, TT], F32, "diag")
        vb = at(A, [TT, NX, T], F32, "vb")
        MW = TT * NT * (NT + 1) // 2
        cmpm = at(A + 40000, [TT, 2, MW], BF16, "cmpm")
        o = CST + 10080
        small = {}
        for name in ("lg", "pr", "ohe1", "ohe2", "cand", "v", "r1", "r2", "rank", "keep"):
            small[name] = at(take(320), [TT, NT, NX], F32, name)
        for name in ("m1", "m2", "den", "wk1", "wk2", "sl1", "sl2", "kp1", "kp2", "cm", "left"):
            small[name] = at(take(40), [TT, NT], F32, name)
        io8 = at(take(32), [TT, NX], F32, "io8")
        io392 = at(take(32), [TT, NX], F32, "io392")
        sidx = at(take(80), [TT, 2, NT], I32, "sidx")
        gidx = at(take(80), [TT, 2, NT], I32, "gidx")
        wrt = at(o, [128, HC, NX], F32, "wrt")
        ex_hi = at(A, [128, HC, CAPR], FR, "ex_hi")
        ex_lo = at(A + 12544, [128, HC, CAPR], FR, "ex_lo")
        s2_hi = at(A + 25088, [128, 8, SC], FR, "s2_hi")
        s2_lo = at(A + 41472, [128, 8, SC], FR, "s2_lo")
        rows = at(A + 57856, [CA, 4, D], F32, "rows")
        sg = at(CST, [128, 2, CAPR], F32, "sg")
        gf = at(CST + 3136, [128, 2, CAPR], F32, "gf")
        eo = at(o, [CA, 4, SC], F32, "eo")
        r1t = at(A, [TT, 2, D], F32, "r1t")
        r2t = at(A + 8192, [TT, 2, D], F32, "r2t")
        x2t = at(A + 16384, [TT, 2, D], F32, "x2t")

        P = ctx.enter_context(nc.psum_tensor("P", [128, 8, 512], F32))

        bkt_d = dram("bkt_d", [NE], BF16)
        hist_d = dram("hist_d", [NB])
        rec_d = dram("rec_d", [128 * NCH, 4])
        attn_d = dram("attn_d", [T, D])
        y_d = dram("y_d", [T, D])
        x2_d = dram("x2_d", [T, D])
        h2_d = dram("h2_d", [T, D])
        ein_d = dram("ein_d", [NX * CAPR, D])
        eo_d = dram("eo_d", [NX * CAPR, D])

        x_in = [sem(f"x_in{i}") for i in range(2)]
        edges_in = sem("edges_in")
        const_ok = sem("const_ok")
        dve_step = sem("dve_step")
        act_step = sem("act_step")
        pool_step = sem("pool_step")
        var_ok = sem("var_ok")
        std_ok = sem("std_ok")
        xn_ok = sem("xn_ok")
        tr_done = sem("tr_done")
        hi_x = sem("hi_x")
        lo_x = sem("lo_x")
        bkt_ok = sem("bkt_ok")
        bkt_st = sem("bkt_st")
        ohb_ok = sem("ohb_ok")
        graph_mm = sem("graph_mm")
        gstep = sem("gstep")
        hist_st = sem("hist_st")
        hist_in = sem("hist_in")
        raw_in = [sem(f"raw_in{i}") for i in range(4)]
        hi_ok = sem("hi_ok")
        lo_ok = sem("lo_ok")
        w_used = sem("w_used")
        bias_in = sem("bias_in")
        bias_free = sem("bias_free")
        proj = sem("proj")
        kv_evac = sem("kv_evac")
        er = sem("er")
        phik_ok = sem("phik_ok")
        kv_mm = sem("kv_mm")
        kvblk_ok = sem("kvblk_ok")
        q_evac = sem("q_evac")
        phiq_ok = sem("phiq_ok")
        at_mm = sem("at_mm")
        at_evac = sem("at_evac")
        sa_st = [sem(f"sa_st{i}") for i in range(2)]
        br_in = [sem(f"br_in{i}") for i in range(2)]
        br_free = sem("br_free")
        sm_ok = sem("sm_ok")
        rs_ok = sem("rs_ok")
        scat = [sem(f"scat{i}") for i in range(2)]
        ein_zero = sem("ein_zero")
        g_evac = sem("g_evac")
        y_st = [sem(f"y_st{i}") for i in range(2)]
        rl_in = sem("rl_in")
        ohd_ok = sem("ohd_ok")
        ohs_ok = sem("ohs_ok")
        mv_ok = sem("mv_ok")
        adj_sum = sem("adj_sum")
        ch_mm = sem("ch_mm")
        nrm_ok = sem("nrm_ok")
        nrm_sq = sem("nrm_sq")
        nsc_ok = sem("nsc_ok")
        y_in = [sem(f"y_in{i}") for i in range(4)]
        yh_ok = sem("yh_ok")
        yl_ok = sem("yl_ok")
        wh_ok = sem("wh_ok")
        wl_ok = sem("wl_ok")
        wh_free = sem("wh_free")
        agg_mm = sem("agg_mm")
        agg_evac = sem("agg_evac")
        bg_in = sem("bg_in")
        res_in = [sem(f"res_in{i}") for i in range(2)]
        res_ok = sem("res_ok")
        var2 = sem("var2")
        std2 = sem("std2")
        x2_ok = sem("x2_ok")
        h2_ok = sem("h2_ok")
        x2_st = [sem(f"x2_st{i}") for i in range(2)]
        h2_in = sem("h2_in")
        wr_in = sem("wr_in")
        tr2 = sem("tr2")
        h2t_ok = sem("h2t_ok")
        lg_mm = sem("lg_mm")
        lg_evac = sem("lg_evac")
        dmax_ok = sem("dmax_ok")
        exp_ok = sem("exp_ok")
        diag_ok = sem("diag_ok")
        vb_mm = sem("vb_mm")
        vb_ok = sem("vb_ok")
        cmp_ok = sem("cmp_ok")
        cs_mm = sem("cs_mm")
        sidx_ok = sem("sidx_ok")
        kw_ok = sem("kw_ok")
        ein_st = sem("ein_st")
        rows_in = sem("rows_in")
        rows_free = sem("rows_free")
        etr = sem("etr")
        exh = sem("exh")
        exl = sem("exl")
        pg_mm = sem("pg_mm")
        sg_ok = sem("sg_ok")
        gf_ok = sem("gf_ok")
        gh_ok = sem("gh_ok")
        gl_ok = sem("gl_ok")
        dn_mm = sem("dn_mm")
        eo_ok = sem("eo_ok")
        eo_st = [sem(f"eo_st{i}") for i in range(4)]
        g1_in = [sem(f"g1_in{i}") for i in range(2)]
        x2_in = [sem(f"x2_in{i}") for i in range(2)]
        o_ok = sem("o_ok")
        o_st = [sem(f"o_st{i}") for i in range(2)]

        MOE = 8 * NG
        GM0 = 4

        x_v = x.rearrange("(i p) d -> p i d", p=TT)
        attn_v = attn_d.rearrange("(i p) (g c) -> p i g c", p=TT, c=128)
        y_v = y_d.rearrange("(i p) (g c) -> p i g c", p=TT, c=SC)
        yt_v = y_d.rearrange("(i p) d -> p i d", p=TT)
        att_v = attn_d.rearrange("(i p) d -> p i d", p=TT)
        x2_v = x2_d.rearrange("(i p) d -> p i d", p=TT)
        h2_v = h2_d.rearrange("(i p) d -> p i d", p=TT)
        out_v = out.rearrange("(i p) d -> p i d", p=TT)
        wm_v = wmain.rearrange("g (s p) n -> p g s n", p=128)
        ein_v = ein_d.rearrange("(e a p) d -> p e a d", a=4, p=CA)
        eo_v = eo_d.rearrange("(e a p) (h n) -> p e a h n", a=4, p=CA, h=2)

        block = ctx.enter_context(nc.Block())

        @block.sync
        def _(sp):
            def load_group(g, first=False):
                for p in range(4):
                    if not first:
                        sp.wait_ge(lo_ok, g * 8 + 2 * p - 6)
                    sp.dma_start(raw[:, 2 * p:2 * p + 2, :], wm_v[:, g, 2 * p:2 * p + 2, :]).then_inc(raw_in[p], 16)

            for c in range(2):
                sp.dma_start(xin[:, c, :], x_v[:, c, :]).then_inc(x_in[c], 16)
            load_group(0, first=True)
            with sp.Fori(1, NT // 2) as it:
                for c in range(2):
                    sp.wait_ge(tr_done, it * 2 + c - 1)
                    sp.dma_start(xin[:, c, :], x_v[:, it * 2 + c, :]).then_inc(x_in[c], 16)
            with sp.Fori(0, HG) as cg:
                for k in range(1, 4):
                    load_group(cg * 3 + k)
                for j in range(PAIRS):
                    sp.wait_ge(at_evac, cg * 20 + 5 * j + 6)
                    sp.dma_start(attn_v[:, :, cg * PAIRS + j, :], sa[:, j % 2, :, :]).then_inc(sa_st[j % 2], 16)
            load_group(7)
            for g in range(2):
                with sp.Fori(0, NT // 2) as it:
                    for c in range(2):
                        sp.wait_ge(g_evac, it * 2 + (g * NT + c + 1))
                        sp.dma_start(y_v[:, it * 2 + c, g, :], t_b[0:TT, c, :]).then_inc(y_st[c], 16)
            sp.wait_ge(g_evac, 2 * NT)
            sp.wait_ge(ch_mm, NGR)
            sp.dma_start(wrt[:, :, :], wr_t.rearrange("p (h e) -> p h e", e=NX)).then_inc(wr_in, 16)
            sp.dma_start(bgb[:, :], bg.partition_broadcast(TT)).then_inc(bg_in, 16)
            for c in range(2):
                sp.wait_ge(y_st[c], 16 * NT)
                sp.wait_ge(sa_st[c], 64)
            for j in range(NT):
                if j >= 4:
                    sp.wait_ge(yl_ok, j - 3)
                sp.dma_start(yraw[:, j % 4, :], yt_v[:, j, :]).then_inc(y_in[j % 4], 16)
            for c in range(2):
                sp.dma_start(xt2[:, c, :], x_v[:, c, :]).then_inc(res_in[c], 16)
                sp.dma_start(at2[:, c, :], att_v[:, c, :]).then_inc(res_in[c], 16)
            with sp.Fori(0, NT // 2 - 1) as it:
                for c in range(2):
                    sp.wait_ge(x2_ok, it * 2 + c + 1)
                    sp.dma_start(x2_v[:, it * 2 + c, :], xt2[:, c, :]).then_inc(x2_st[c], 16)
                    sp.wait_ge(h2_ok, it * 2 + c + 1)
                    sp.dma_start(h2_v[:, it * 2 + c, :], at2[:, c, :]).then_inc(x2_st[c], 16)
                    sp.wait_ge(x2_st[c], it * 32 + 32)
                    sp.wait_ge(tr2, it * 2 + (c + 1))
                    sp.dma_start(xt2[:, c, :], x_v[:, it * 2 + (c + 2), :]).then_inc(res_in[c], 16)
                    sp.dma_start(at2[:, c, :], att_v[:, it * 2 + (c + 2), :]).then_inc(res_in[c], 16)
            for c in range(2):
                sp.wait_ge(x2_ok, NT - 1 + c)
                sp.dma_start(x2_v[:, NT - 2 + c, :], xt2[:, c, :]).then_inc(x2_st[c], 16)
                sp.wait_ge(h2_ok, NT - 1 + c)
                sp.dma_start(h2_v[:, NT - 2 + c, :], at2[:, c, :]).then_inc(x2_st[c], 16)
            for c in range(2):
                sp.wait_ge(x2_st[c], 16 * NT)
            sp.wait_ge(wl_ok, 2 * NT)
            sp.dma_start(h2a[:, :, :], h2_v).then_inc(h2_in, 16)

            def load_moe_part(e, k, src, p):
                sp.wait_ge(lo_ok, e * 24 + (MOE + 8 * k + 2 * p - 6))
                sp.dma_start(raw[:, 2 * p:2 * p + 2, :], src[:, 2 * p:2 * p + 2, :]).then_inc(raw_in[p], 16)

            def load_moe(e, k, src):
                for p in range(4):
                    load_moe_part(e, k, src, p)

            load_moe(0, 0, wpre[:, 0, :, :])
            load_moe(0, 1, wgate[:, 0, :, :])
            sp.wait_ge(ein_st, 16 * 2 * NT)
            sp.wait_ge(cs_mm, NX)
            sp.dma_start(rows[:, :, :], ein_v[:, 0, :, :]).then_inc(rows_in, 16)
            load_moe(0, 2, wpost[:, 0, :, :])
            with sp.Fori(0, NX - 1) as e:
                load_moe(e + 1, 0, wpre[:, e + 1, :, :])
                sp.wait_ge(etr, e * 8 + 8)
                sp.dma_start(rows[:, :, :], ein_v[:, e + 1, :, :]).then_inc(rows_in, 16)
                for u in range(9):
                    if u < 8:
                        load_moe_part(e + 1, 1 + u // 4, (wgate, wpost)[u // 4][:, e + 1, :, :], u % 4)
                    if u >= 1:
                        sp.wait_ge(eo_ok, e * 8 + u)
                        sp.dma_start(eo_v[:, e, (u - 1) // 2, (u - 1) % 2, :], eo[:, (u - 1) % 4, :]).then_inc(eo_st[(u - 1) % 4], 16)
            for u in range(8):
                sp.wait_ge(eo_ok, (NX - 1) * 8 + u + 1)
                sp.dma_start(eo_v[:, NX - 1, u // 2, u % 2, :], eo[:, u % 4, :]).then_inc(eo_st[u % 4], 16)
            sp.wait_ge(dn_mm, NX * 8)
            for i in range(NT):
                if i >= 2:
                    sp.wait_ge(o_ok, i - 1)
                    sp.dma_start(out_v[:, i - 2, :], x2t[:, i % 2, :]).then_inc(o_st[i % 2], 16)
                    sp.wait_ge(o_st[i % 2], 16 * (i // 2))
                sp.dma_start(x2t[:, i % 2, :], x2_v[:, i, :]).then_inc(x2_in[i % 2], 16)
            for i in range(NT - 2, NT):
                sp.wait_ge(o_ok, i + 1)
                sp.dma_start(out_v[:, i, :], x2t[:, i % 2, :]).then_inc(o_st[i % 2], 16)
            for c in range(2):
                sp.wait_ge(o_st[c], 16 * NT // 2)

        @block.scalar
        def _(act):
            act.dma_start(en[:, :, :], edges_n.rearrange("a p c -> p a c")).then_inc(edges_in, 16)
            act.dma_start(ec[:, :, :], edges_c.rearrange("a p c -> p a c")).then_inc(edges_in, 16)
            act.dma_start(wc[:, :], w_c).then_inc(edges_in, 16)
            act.wait_ge(bkt_ok, 1)
            act.dma_start(bkt_d.rearrange("(p c) -> p c", p=TT), bkt[:, :]).then_inc(bkt_st, 16)

            def split_hi(g, dst, first=False, src=None):
                for s in range(8):
                    act.wait_ge(raw_in[s // 2], g * 16 + 16)
                    if not first:
                        act.wait_ge(w_used, g * 8 + (s - 7))
                    act.copy(dst[:, s, :], raw[:, s, :]).then_inc(hi_ok, 1)

            split_hi(0, s0_hi, first=True)
            with act.Fori(0, NT // 2) as it:
                for c in range(2):
                    act.wait_ge(var_ok, it * 2 + (c + 1))
                    act.activation(rstd[:, 0:1], rstd[:, 1:2], ACT.Sqrt).then_inc(std_ok, 1)
                    act.wait_ge(tr_done, it * 2 + (c + 1))
                    act.copy(xt_hi[:, :, bass.ds(it * 250 + c * TT, TT)].rearrange("p (b h) t -> p b h t", b=2),
                             P[:, 2 * c:2 * c + 2, 0:500].rearrange("p b (h t) -> p b h t", h=4)).then_inc(hi_x, 1)
            act.wait_ge(gstep, 2)
            act.dma_start(hist_d.rearrange("(a b) -> a b", a=NT), hist10[:, :]).then_inc(hist_st, 16)
            act.wait_ge(hist_st, 16)
            act.dma_start(hist[:, :], hist_d.rearrange("(p o) -> p o", o=1)).then_inc(hist_in, 16)
            act.wait_ge(bkt_st, 16)
            act.wait_ge(gstep, 6)

            def load_rows(cg, b):
                act.wait_ge(br_free, cg * BPG + (b + 1))
                act.dma_start(br[:, b % 2, :],
                              bkt_d[bass.ds(cg * (BPG * EB) + b * EB, EB)].partition_broadcast(NB)).then_inc(br_in[b % 2], 16)

            with act.Fori(0, HG) as cg:
                act.wait_ge(bias_free, cg + 1)
                for k in range(2):
                    act.dma_start(bkv[:, k, :], bqkv[bass.ds(cg * SC + (k + 1) * D, SC)].partition_broadcast(TT)).then_inc(bias_in, 16)
                act.dma_start(bq[:, :], bqkv[bass.ds(cg * SC, SC)].rearrange("(j p) -> p j", p=128),
                              allow_slow_non_contiguous=True).then_inc(bias_in, 16)
                for i in range(NT):
                    act.wait_ge(kv_evac, cg * 20 + (i + 1))
                    if i >= 2:
                        act.wait_ge(phik_ok, cg * NT + (i - 1))
                    act.activation(e_b[0:TT, i % 2, :], t_b[0:TT, i % 2, :], ACT.Exp).then_inc(act_step, 1)
                    act.activation(t_b[0:TT, i % 2, :], t_b[0:TT, i % 2, :], ACT.Relu).then_inc(er, 1)
                    if i == NT - 2:
                        split_hi(cg * 3 + 1, s0_hi)
                load_rows(cg, 0)
                for i in range(NT):
                    if i >= 2:
                        load_rows(cg, i - 1)
                    if i == NT - 2:
                        split_hi(cg * 3 + 2, s0_hi)
                act.wait_ge(phik_ok, cg * NT + NT)
                act.wait_ge(bias_in, cg * 48 + 48)
                for q in range(3 * PAIRS):
                    j, n = q // 3, QCUT[q % 3 + 1] - QCUT[q % 3]
                    if q == 3 * PAIRS - 1:
                        split_hi(cg * 3 + 3, s0_hi)
                    act.wait_ge(proj, cg * UNITS + (2 * NT + q + 1))
                    if q >= 2:
                        act.wait_ge(phiq_ok, cg * 12 + (q - 1))
                    act.activation(e_b[:, q % 2, 0:n], P[:, q % 4, 0:n], ACT.Exp, bias=bq[:, j:j + 1]).then_inc(act_step, 1)
                    act.activation(t_b[:, q % 2, 0:n], P[:, q % 4, 0:n], ACT.Relu, bias=bq[:, j:j + 1]).then_inc(q_evac, 1)
                    if q + 9 < BPG:
                        load_rows(cg, q + 9)
            def weighted(p, n):
                for c in range(CG):
                    if c % 2 == 0:
                        act.wait_ge(ohd_ok, n * 2 + (1 + c // 2))
                        act.copy(mvt[:, p, c:c + 2, TT:TT + 2], rl[:, bass.ds(n * CG + c, 2), 2:4]).then_inc(act_step, 1)
                    act.activation(mvt[:, p, c, 0:TT], ohd[:, p, c, 0:TT], ACT.Copy,
                                   scale=rl[:, bass.ds(n * CG + c, 1), 2]).then_inc(mv_ok, 1)

            act.wait_ge(phiq_ok, 24)
            zv = ein_d.rearrange("(p r) (h n) -> p (r h) n", p=ZP, h=2)
            for n in range(2 * NT):
                if GT0 < n <= GT0 + ZN:
                    z = n - GT0 - 1
                    act.dma_start(zv[:, 8 * z:8 * z + 8, :], zero[0:ZP, None, :].broadcast_to([ZP, 8, SC])).then_inc(ein_zero, 16)
                if n >= GT0:
                    with act.Fori(0, GL) as it:
                        for p in range(2):
                            weighted(p, it * 2 + (2 * GL * (n - GT0) + 2 + p))
                if n == NT - 1:
                    split_hi(7, s0_hi)
                act.wait_ge(proj, HG * UNITS + n + 1)
                if n >= 2:
                    act.wait_ge(y_st[n % 2], 16 * (n // 2))
                act.copy(t_b[0:TT, n % 2, :], P[0:TT, n % 4, :]).then_inc(g_evac, 1)
                if n == GT0 - 1:
                    for p in range(2):
                        weighted(p, p)
            act.wait_ge(adj_sum, NCH + 2 * CG)

            def adj_hi(i, h):
                act.copy(w_hi[:, 5 * h:5 * h + 5, :],
                         adj[:, bass.ds(i * (NT * BW) + h * (5 * BW), 5 * BW)].rearrange("p (j c) -> p j c", c=BW)[:, :, 0:TT]).then_inc(wh_ok, 1)

            for h in range(2):
                adj_hi(0, h)
            act.wait_ge(nrm_ok, 1)
            act.activation(nrm[:, :, :], nrm[:, :, :], ACT.Sqrt).then_inc(nrm_sq, 1)
            act.wait_ge(nsc_ok, 1)
            act.wait_ge(w_used, 8 * NG)
            for j in range(NT):
                act.wait_ge(y_in[j % 4], 16 * (j // 4 + 1))
                act.activation(y_hi[:, j, :], yraw[:, j % 4, :], ACT.Copy, scale=nsc[:, 0, j:j + 1]).then_inc(yh_ok, 1)

            def h2_out(i):
                act.wait_ge(tr2, i + 1)
                act.copy(h2t[:, :, :].rearrange("p (b h) t -> p b (h t)", b=2), P[:, 4:6, 0:500]).then_inc(h2t_ok, 1)

            def root(i):
                act.wait_ge(var2, i + 1)
                act.activation(rstd[:, 0:1], rstd[:, 1:2], ACT.Sqrt).then_inc(std2, 1)

            root(0)
            with act.Fori(0, NT - 1) as i:
                h2_out(i)
                root(i + 1)
            h2_out(NT - 1)
            act.wait_ge(dmax_ok, 1)
            act.activation(small["pr"][:, :, :], small["pr"][:, :, :], ACT.Exp).then_inc(exp_ok, 1)
            for i in range(NT):
                c = i % 2
                act.wait_ge(vb_mm, i + 1)
                act.copy(vb[:, :, i * TT:(i + 1) * TT].rearrange("p (b e) t -> p b e t", b=2),
                         P[0:TT, 2 * c:2 * c + 2, 0:500].rearrange("p b (e t) -> p b e t", e=4)).then_inc(vb_ok, 1)

            def split_moe(e, k, dst, slots=range(8)):
                for s in slots:
                    act.wait_ge(raw_in[s // 2], e * 48 + 16 * (NG + k + 1))
                    if k == 0:
                        act.wait_ge(w_used, e * 24 + (MOE - 24 + s + 1 + 0))
                    else:
                        act.wait_ge(w_used, e * 24 + (MOE - 24 + 8 * k + s + 1))
                    act.copy(dst[:, s, :], raw[:, s, :]).then_inc(hi_ok, 1)

            def ex_split_hi(e1, chunks=range(HC)):
                for h in chunks:
                    act.wait_ge(etr, e1 * 8 + (h + 1))
                    act.copy(ex_hi[:, h, :], P[:, h % 2, 0:CAPR]).then_inc(exh, 1)

            act.wait_ge(lg_evac, 1)
            act.wait_ge(vb_mm, NT)
            split_moe(0, 0, s0_hi)
            act.wait_ge(ein_st, 16 * 2 * NT)
            act.wait_ge(cs_mm, NX)
            split_moe(0, 1, s1_hi)
            ex_split_hi(0)
            split_moe(0, 2, s2_hi)

            def swiglu(e):
                for m in range(FC):
                    act.wait_ge(pg_mm, e * FC + (m + 1))
                    if m >= 2:
                        act.wait_ge(gf_ok, e * FC + (m - 1))
                    act.activation(sg[:, m % 2, :], P[:, 4 + m % 2, 0:CAPR], ACT.Silu).then_inc(sg_ok, 1)
                    act.wait_ge(gf_ok, e * FC + (m + 1))
                    act.copy(g_hi[:, m, :], gf[:, m % 2, :]).then_inc(gh_ok, 1)

            def results(e):
                for u in range(0, 8, 2):
                    act.wait_ge(dn_mm, e * 8 + (u + 1))
                    act.wait_ge(eo_st[u % 4], e * 32 + 16 * (u // 4))
                    act.copy(eo[:, u % 4, :], P[0:CA, 6 + u % 2, :]).then_inc(eo_ok, 1)

            with act.Fori(0, NX - 1) as e:
                swiglu(e)
                for u in range(8):
                    ex_split_hi(e + 1, (u,))
                    a = 2 * (u % 4)
                    split_moe(e + 1, u // 4, (s0_hi, s1_hi)[u // 4], (a, a + 1))
                act.wait_ge(sg_ok, e * FC + FC)
                split_moe(e + 1, 2, s2_hi)
            swiglu(NX - 1)

        @block.gpsimd
        def _(pool):
            steps = Count(pool, pool_step)
            nc.gpsimd.memset(zero[:, :], 0.0).then_inc(const_ok, 1)
            steps.then(nc.gpsimd.memset(ident[:, :], 0.0))
            steps.then(nc.gpsimd.memset(ones[:, :], 1.0))
            nc.gpsimd.memset(onesb[:, :], 1.0).then_inc(const_ok, 1)
            nc.gpsimd.affine_select(out=ident[:, :], in_=ident[:, :], compare_op=ALU.not_equal, fill=1.0, base=0,
                                    pattern=[[-1, 128]], channel_multiplier=1).then_inc(const_ok, 1)
            nc.gpsimd.iota(iota[:, :], [[1, TT]], base=0, channel_multiplier=0,
                           allow_small_or_imprecise_dtypes=True).then_inc(const_ok, 1)
            nc.gpsimd.iota(iotap[:, :], [[1, 1]], base=0, channel_multiplier=1,
                           allow_small_or_imprecise_dtypes=True).then_inc(const_ok, 1)
            nc.gpsimd.iota(iotak[:, :], [[1, NCH]], base=0, channel_multiplier=0,
                           allow_small_or_imprecise_dtypes=True).then_inc(const_ok, 1)
            nc.gpsimd.affine_select(out=upper[:, :], in_=ones[0:NB, 0:NB], compare_op=ALU.is_ge, fill=0.0, base=0,
                                    pattern=[[1, NB]], channel_multiplier=-1).then_inc(const_ok, 1)
            nc.gpsimd.affine_select(out=lower[:, :], in_=ones[0:TT, 0:TT], compare_op=ALU.is_ge, fill=0.0, base=-1,
                                    pattern=[[-1, TT]], channel_multiplier=1).then_inc(const_ok, 1)
            o80 = ones[0:80, 0:80].rearrange("p (a b) -> p a b", a=8)
            steps.then(nc.gpsimd.affine_select(out=mask80[:, :, :], in_=o80, compare_op=ALU.is_ge, fill=0.0, base=0,
                                               pattern=[[-10, 8], [0, 10]], channel_multiplier=1))
            nc.gpsimd.affine_select(out=mask80[:, :, :], in_=mask80[:, :, :], compare_op=ALU.is_ge, fill=0.0, base=9,
                                    pattern=[[10, 8], [0, 10]], channel_multiplier=-1).then_inc(const_ok, 1)
            pool.wait_ge(const_ok, 1)
            rz = rec_d.rearrange("(p k) f -> p (k f)", p=128).rearrange("p (r n) -> p r n", r=4)
            for c in range(2):
                pool.dma_start(rz[:, 2 * c:2 * c + 2, :],
                               zero[:, None, 0:NCH].broadcast_to([128, 2, NCH])).then_inc(scat[c], 16)
            for c in range(2):
                pool.wait_ge(scat[c], 16)
            with pool.Fori(0, NBLK // 2) as it:
                for c in range(2):
                    pool.wait_ge(rs_ok, it * 2 + (c + 1))
                    pool.wait_ge(pool_step, it * 2 + (steps.n + c))
                    nc.gpsimd.tensor_tensor(pw[:, :], ones[0:1, 0:1], ones[0:1, 0:1], ALU.add).then_inc(pool_step, 1)
                    for k in range(BC):
                        pool.indirect_dma_start(out=rec_d, out_offset=bass.IndirectOffsetOnAxis(ap=idx[:, c, k:k + 1], axis=0),
                                                in_=rs[:, c, k, :], in_offset=None, bounds_check=128 * NCH - 1,
                                                oob_is_err=True).then_inc(scat[c], 16)
            for c in range(2):
                pool.wait_ge(scat[c], 16 + 16 * BC * NBLK // 2)
            pool.dma_start(rl[:, :, :], rec_d.rearrange("(p k) f -> p k f", p=128)).then_inc(rl_in, 16)
            with pool.Fori(0, NT // 2) as it:
                for c in range(2):
                    pool.wait_ge(res_in[c], it * 32 + 32)
                    nc.gpsimd.tensor_tensor(xt2[:, c, :], xt2[:, c, :], at2[:, c, :], ALU.add).then_inc(res_ok, 1)
            pool.wait_ge(x2_ok, NT)
            nc.gpsimd.iota(io8[:, :], [[1, NX]], base=-NX, channel_multiplier=0,
                           allow_small_or_imprecise_dtypes=True).then_inc(const_ok, 1)
            nc.gpsimd.iota(io392[:, :], [[CAPR, NX]], base=0, channel_multiplier=0,
                           allow_small_or_imprecise_dtypes=True).then_inc(const_ok, 1)
            nc.gpsimd.iota(small["left"][:, :], [[-TT, NT]], base=T - 1, channel_multiplier=-1,
                           allow_small_or_imprecise_dtypes=True).then_inc(const_ok, 1)
            pool.wait_ge(ein_zero, 16 * ZN)
            pool.wait_ge(sidx_ok, 1)
            pool.wait_ge(h2_in, 16)
            for i in range(NT):
                for k in range(2):
                    pool.indirect_dma_start(out=ein_d, out_offset=bass.IndirectOffsetOnAxis(ap=sidx[:, k, i:i + 1], axis=0),
                                            in_=h2a[:, i, :], in_offset=None, bounds_check=NX * CAPR - 1,
                                            oob_is_err=False).then_inc(ein_st, 16)
            pool.wait_ge(dn_mm, NX * 8)
            for c in range(4):
                pool.wait_ge(eo_st[c], 16 * 2 * NX)
            for i in range(NT):
                if i >= 2:
                    pool.wait_ge(o_ok, i - 1)
                for k, dst in ((0, r1t), (1, r2t)):
                    pool.indirect_dma_start(out=dst[:, i % 2, :], out_offset=None, in_=eo_d,
                                            in_offset=bass.IndirectOffsetOnAxis(ap=gidx[:, k, i:i + 1], axis=0),
                                            bounds_check=NX * CAPR - 1, oob_is_err=True).then_inc(g1_in[i % 2], 16)

        @block.vector
        def _(dve):
            v = nc.vector
            steps = Count(dve, dve_step)

            def floor_div(dst, src, by, add=0.0):
                steps.then(v.tensor_scalar(dst, src, 1.0 / by, add / by - 0.498, ALU.mult, ALU.add))
                steps.then(v.tensor_scalar(dst, dst, MAGIC, MAGIC, ALU.add, ALU.subtract))

            dve.wait_ge(edges_in, 48)
            for a in range(2):
                floor_div(tn[:, a, :], en[:, a, :], TT)
            v.scalar_tensor_tensor(out=bkt[:, :], in0=tn[:, 1, :], scalar=float(NT), in1=tn[:, 0, :],
                                   op0=ALU.mult, op1=ALU.add).then_inc(bkt_ok, 1)
            for a in range(2):
                floor_div(tc[:, a, :], ec[:, a, :], TT)
                v.scalar_tensor_tensor(out=rec[:, :, a], in0=tc[:, a, :], scalar=-float(TT), in1=ec[:, a, :],
                                       op0=ALU.mult, op1=ALU.add)
            v.tensor_copy(rec[:, :, 2], wc[:, :])
            v.memset(rec[:, :, 3:4], 1.0)
            dve.wait_ge(const_ok, 9)
            for a, oh in ((0, oh_s), (1, oh_d)):
                v.tensor_tensor(oh[:, :, :], iota[0:TT, None, 0:NT].broadcast_to([TT, EC, NT]),
                                tc[:, a, :, None].broadcast_to([TT, EC, NT]), ALU.is_equal).then_inc(ohb_ok, 1)

            def split_lo(g, hi, lo):
                for s in range(8):
                    dve.wait_ge(hi_ok, g * 8 + (s + 1))
                    v.tensor_tensor(lo[:, s, :], raw[:, s, :], hi[:, s, :].bitcast(F32), ALU.subtract).then_inc(lo_ok, 1)

            def normalize(st, src, dst, var, std, n):
                for h in range(2):
                    ins = v.bn_stats(stats[:, h, :], src[:, h * SC:(h + 1) * SC])
                st.then(ins)
                v.memset(rstd[:, 0:1], 0.0)
                st.then(v.bn_aggr(mv[:, :], stats[:, :, :]))
                v.tensor_scalar(rstd[:, 1:2], mv[:, 1:2], LNEPS, None, ALU.add).then_inc(var, 1)
                dve.wait_ge(std, n)
                st.then(v.reciprocal(rstd[:, 0:1], rstd[:, 0:1]))
                return v.tensor_scalar(dst, src, mv[:, 0:1], rstd[:, 0:1], ALU.subtract, ALU.mult)

            with dve.Fori(0, NT // 2) as it, steps.loop(it, NT // 2, 6) as st:
                for c in range(2):
                    dve.wait_ge(x_in[c], it * 16 + 16)
                    normalize(st, xin[:, c, :], xin[:, c, :], var_ok, std_ok, it * 2 + (c + 1)).then_inc(xn_ok, 1)
                    dve.wait_ge(hi_x, it * 2 + (c + 1))
                    sl = bass.ds(it * 250 + c * TT, TT)
                    v.tensor_tensor(xt_lo[:, :, sl].rearrange("p (b h) t -> p b h t", b=2),
                                    P[:, 2 * c:2 * c + 2, 0:500].rearrange("p b (h t) -> p b h t", h=4),
                                    xt_hi[:, :, sl].bitcast(F32).rearrange("p (b h) t -> p b h t", b=2),
                                    ALU.subtract).then_inc(lo_x, 1)
            split_lo(0, s0_hi, s0_lo)

            dve.wait_ge(graph_mm, 1)
            steps.then(v.tensor_tensor(hq[:, :, :], P[0:80, 7, 0:80].rearrange("p (a b) -> p a b", a=8), mask80[:, :, :], ALU.mult))
            v.tensor_reduce(sel80[:, :], ident[0:80, 0:80].rearrange("p (a b) -> p b a", a=8), X, ALU.add)
            v.tensor_reduce(hs[:, :], hq[:, :, :].rearrange("p a b -> p b a"), X, ALU.add).then_inc(gstep, 1)
            dve.wait_ge(graph_mm, 2)
            v.tensor_copy(hist10[:, :], P[0:NT, 7, 128:128 + NT]).then_inc(gstep, 1)
            dve.wait_ge(hist_in, 16)
            floor_div(nch[:, 0:1], hist[:, :], CHUNK, CHUNK - 1.0)
            v.tensor_copy(nch[:, 1:2], nch[:, 0:1]).then_inc(gstep, 1)
            dve.wait_ge(graph_mm, 3)
            steps.then(v.tensor_copy(incl[:, :], P[0:NB, 7, 160:161]))
            v.tensor_scalar(ge[:, :], iotak[:, :], incl[:, 0:1], None, ALU.is_ge).then_inc(gstep, 1)
            steps.then(v.tensor_tensor(base1[:, :], incl[:, :], nch[:, 0:1], ALU.subtract))
            steps.then(v.tensor_scalar(base1[:, :], base1[:, :], float(CHUNK), -1.0, ALU.mult, ALU.add))
            dve.wait_ge(graph_mm, 4)
            v.tensor_scalar(offs[:, :], P[0:1, 6, 0:NCH], float(NB - 1), float(BW), ALU.min, ALU.mult).then_inc(gstep, 1)
            v.memset(carry[:, :], 0.0).then_inc(br_free, 2)
            dve.wait_ge(bkt_st, 16)
            v.memset(vt[:, :, :, 128:129], 1.0).then_inc(at_evac, 1)
            v.memset(kvblk[:, :, :], 0.0).then_inc(bias_free, 1)
            v.memset(zt[:, :, :, :], 0.0).then_inc(gstep, 1)

            def places(cg, b, st):
                dve.wait_ge(br_in[b % 2], cg * (8 * BPG) + 16 * (b // 2 + 1))
                v.tensor_scalar(oht[:, :], br[:, b % 2, :], iotap[0:NB, 0:1], None, ALU.is_equal).then_inc(br_free, 1)
                dve.wait_ge(br_free, cg * BPG + (b + 3))
                dve.wait_ge(graph_mm, cg * BPG + (GM0 + b))
                st.then(v.tensor_tensor_scan(sm[:, :], oht[:, :], oht[:, :], carry[:, 0:1], ALU.add, ALU.max))
                st.then(v.tensor_copy(carry[:, :], sm[:, EB - 1:EB]))
                v.scalar_tensor_tensor(out=sm[:, :], in0=sm[:, :], scalar=base1[:, 0:1], in1=oht[:, :],
                                       op0=ALU.add, op1=ALU.mult).then_inc(sm_ok, 1)

            def records(cg, b, st):
                c = b % 2
                dve.wait_ge(graph_mm, cg * BPG + (GM0 + b + 1))
                pos = P[0:TT, 7, 256:256 + BC]
                st.then(v.tensor_scalar(pk[:, 0, :], pos, 1.0 / CHUNK, -0.498, ALU.mult, ALU.add))
                st.then(v.tensor_scalar(pk[:, 0, :], pk[:, 0, :], MAGIC, MAGIC, ALU.add, ALU.subtract))
                st.then(v.scalar_tensor_tensor(out=pk[:, 1, :], in0=pk[:, 0, :], scalar=-float(CHUNK), in1=pos,
                                               op0=ALU.mult, op1=ALU.add))
                dve.wait_ge(scat[c], cg * (8 * BPG * BC) + (16 + 16 * BC * (b // 2)))
                st.then(v.scalar_tensor_tensor(out=idx[:, c, :], in0=pk[:, 1, :], scalar=float(NCH), in1=pk[:, 0, :],
                                               op0=ALU.mult, op1=ALU.add))
                v.tensor_copy(rs[:, c, :, :], rec[:, bass.ds(cg * (BPG * BC) + b * BC, BC), :]).then_inc(rs_ok, 1)

            def attention(cg, j, st):
                for gg in range(5):
                    u = 5 * j + gg
                    dve.wait_ge(at_mm, cg * 20 + (u + 1))
                    pv = P[0:TT, 4 + u % 2, 0:2 * AW].rearrange("p (t c) -> p t c", t=2)
                    z = zt[:, u % 2, :, :]
                    st.then(v.tensor_scalar(z, pv[:, :, 128:130], 1e-6, None, ALU.add))
                    st.then(v.reciprocal(z, z))
                    if gg == 0 and j >= 2:
                        dve.wait_ge(sa_st[j % 2], cg * 32 + 16)
                    for t in range(2):
                        ins = v.tensor_tensor(sa[:, j % 2, 2 * gg + t, :].rearrange("p (h m) -> p h m", h=2),
                                              pv[:, t, 0:128].rearrange("p (h m) -> p h m", h=2),
                                              z[:, t, :, None].broadcast_to([TT, 2, 64]), ALU.mult)
                    ins.then_inc(at_evac, 1)

            with dve.Fori(0, HG) as cg, steps.loop(cg, HG, 2 * BPG + 4 * BPG + 2 * 20) as st:
                dve.wait_ge(bias_in, cg * 48 + 48)
                for i in range(NT):
                    dve.wait_ge(proj, cg * UNITS + (i + 1))
                    if i >= 2:
                        dve.wait_ge(phik_ok, cg * NT + (i - 1))
                    v.tensor_tensor(t_b[0:TT, i % 2, :], P[0:TT, i % 4, :], bkv[:, 0, :], ALU.add).then_inc(kv_evac, 1)
                    if i >= 1:
                        dve.wait_ge(er, cg * NT + i)
                        v.scalar_tensor_tensor(out=phik[:, i - 1, :], in0=e_b[0:TT, (i - 1) % 2, :], scalar=1.0,
                                               in1=t_b[0:TT, (i - 1) % 2, :], op0=ALU.min, op1=ALU.add).then_inc(phik_ok, 1)
                    if i == NT - 2:
                        split_lo(cg * 3 + 1, s0_hi, s0_lo)
                for i in range(NT):
                    dve.wait_ge(proj, cg * UNITS + (NT + i + 1))
                    if i >= 2:
                        dve.wait_ge(kv_mm, cg * NT + (i - 1))
                    v.tensor_tensor(vt[:, i % 2, :, 0:128], P[0:TT, (NT + i) % 4, :].rearrange("p (j c) -> p j c", j=PAIRS),
                                    bkv[:, 1, :].rearrange("p (j c) -> p j c", j=PAIRS), ALU.add).then_inc(kv_evac, 1)
                    if i == 0:
                        dve.wait_ge(er, cg * NT + NT)
                        v.scalar_tensor_tensor(out=phik[:, NT - 1, :], in0=e_b[0:TT, (NT - 1) % 2, :], scalar=1.0,
                                               in1=t_b[0:TT, (NT - 1) % 2, :], op0=ALU.min, op1=ALU.add).then_inc(phik_ok, 1)
                    if i >= 2:
                        if i >= 3:
                            records(cg, i - 3, st)
                        places(cg, i - 2, st)
                    if i == NT - 2:
                        split_lo(cg * 3 + 2, s0_hi, s0_lo)
                dve.wait_ge(kv_mm, cg * NT + NT)
                for h in range(2):
                    for a in range(2):
                        r = slice(64 * a, 64 * a + 64)
                        src = P[r, 4 + h, 0:2 * KVW].rearrange("p (j c) -> p j c", j=2)
                        v.tensor_copy(kvblk[r, 2 * h:2 * h + 2, 64 * a:64 * a + 64], src[:, :, 64 * a:64 * a + 64]).then_inc(kvblk_ok, 1)
                        v.tensor_copy(kvblk[r, 2 * h:2 * h + 2, 128 + a:129 + a], src[:, :, 128:129]).then_inc(kvblk_ok, 1)
                for q in range(3 * PAIRS):
                    j, a = q // 3, QCUT[q % 3]
                    n = QCUT[q % 3 + 1] - a
                    if q == 3 * PAIRS - 1:
                        split_lo(cg * 3 + 3, s0_hi, s0_lo)
                    dve.wait_ge(q_evac, cg * 12 + (q + 1))
                    if q % 3 == 0 and j >= 2:
                        dve.wait_ge(at_mm, cg * 20 + 5 * (j - 1))
                    ins = v.scalar_tensor_tensor(out=phiq[:, j % 2, a:a + n], in0=e_b[:, q % 2, 0:n], scalar=1.0,
                                                 in1=t_b[:, q % 2, 0:n], op0=ALU.min, op1=ALU.add)
                    ins.then_inc(phiq_ok, 1)
                    if q % 3 == 0 and j >= 1:
                        attention(cg, j - 1, st)
                    records(cg, q + 7, st)
                    places(cg, q + 8, st)
                records(cg, BPG - 1, st)
                attention(cg, PAIRS - 1, st)
                for c in range(2):
                    dve.wait_ge(sa_st[c], cg * 32 + 32)
                v.memset(mv[:, :], 0.0).then_inc(bias_free, 1)

            step = NB * BW // 4
            for k in range(4):
                v.memset(adj[:, k * step:(k + 1) * step], 0.0)
            v.memset(rstd[:, 0:1], 0.0).then_inc(adj_sum, 2 * CG)
            dve.wait_ge(rl_in, 16)

            def one_hots(p, n, k):
                a, oh, done = ((1, ohd, ohd_ok), (0, ohs, ohs_ok))[k // 2]
                h = k % 2
                v.tensor_tensor(oh[:, p, 2 * h:2 * h + 2, 0:TT], iota[:, None, :].broadcast_to([128, 2, TT]),
                                rl[:, bass.ds(n * CG + 2 * h, 2), a:a + 1].broadcast_to([128, 2, TT]), ALU.is_equal).then_inc(done, 1)

            off_regs = [dve.alloc_register(f"off{k}") for k in range(2 * CG)]

            def offsets(n):
                dve.reg_load(off_regs, offs[0:1, bass.ds(n * CG, 2 * CG)])
                return [nc.snap(r, min_val=0, max_val=(NB - 1) * BW) for r in off_regs]

            def add_blocks(p, n, at_, more=True):
                dve.wait_ge(ch_mm, n + 1)
                for c in range(CG):
                    blk = adj[:, bass.ds(at_[CG * p + c], BW)]
                    dve.wait_ge(adj_sum, n * CG + (2 * CG + c))
                    v.tensor_tensor(blk, blk, P[0:TT, 4 + 2 * p + c // 2, (c % 2) * BW:(c % 2 + 1) * BW], ALU.add).then_inc(adj_sum, 1)
                    if more:
                        one_hots(p, n + 2, c)

            for p in range(2):
                for k in range(4):
                    one_hots(p, p, k)
            for k in range(2 * NT - GT0):
                if k + GT0 == NT:
                    split_lo(7, s0_hi, s0_lo)
                with dve.Fori(0, GL) as it:
                    at_ = offsets(it * 2 + 2 * GL * k)
                    for p in range(2):
                        add_blocks(p, it * 2 + (2 * GL * k + p), at_)
            at_ = offsets(NGR - 2)
            for p in range(2):
                add_blocks(p, NGR - 2 + p, at_, more=False)
            dve.wait_ge(adj_sum, NCH + 2 * CG)
            a4 = adj[:, :].rearrange("p (d s c) -> p d s c", d=NT, s=NT)
            v.tensor_reduce(nrm[:, 0, :], a4[:, :, :, TT].rearrange("p d s -> p s d"), X, ALU.add)
            v.tensor_reduce(nrm[:, 1, :], a4[:, :, :, TT + 1].rearrange("p d s -> p s d"), X, ALU.add)
            v.tensor_reduce(nrm[:, 2, :], a4[:, :, :, TT + 2], X, ALU.add)
            steps.then(v.tensor_reduce(nrm[:, 3, :], a4[:, :, :, TT + 3], X, ALU.add))
            for k in range(4):
                ins = v.tensor_scalar(nrm[:, k, :], nrm[:, k, :], 1.0 if k % 2 else 1e-30, None, ALU.max)
            ins.then_inc(nrm_ok, 1)

            def adj_lo(i, h, k):
                dve.wait_ge(wh_ok, k)
                v.tensor_tensor(w_lo[:, 5 * h:5 * h + 5, :],
                                adj[:, bass.ds(i * (NT * BW) + h * (5 * BW), 5 * BW)].rearrange("p (j c) -> p j c", c=BW)[:, :, 0:TT],
                                w_hi[:, 5 * h:5 * h + 5, :].bitcast(F32), ALU.subtract).then_inc(wl_ok, 1)

            for h in range(2):
                adj_lo(0, h, h + 1)
            dve.wait_ge(nrm_sq, 1)
            for k in range(2):
                steps.then(v.tensor_tensor(nsc[:, k, :], nrm[:, 2 * k, :], nrm[:, 2 * k + 1, :], ALU.mult))
            v.reciprocal(nsc[:, :, :], nsc[:, :, :]).then_inc(nsc_ok, 1)
            dve.wait_ge(nsc_ok, 1)
            for j in range(NT):
                dve.wait_ge(yh_ok, j + 1)
                v.scalar_tensor_tensor(out=y_lo[:, j, :], in0=yraw[:, j % 4, :], scalar=nsc[:, 0, j:j + 1],
                                       in1=y_hi[:, j, :].bitcast(F32), op0=ALU.mult, op1=ALU.subtract).then_inc(yl_ok, 1)

            def adj_hi_dve(i, h, k):
                dve.wait_ge(wh_free, k)
                v.tensor_copy(w_hi[:, 5 * h:5 * h + 5, :],
                              adj[:, bass.ds(i * (NT * BW) + h * (5 * BW), 5 * BW)].rearrange("p (j c) -> p j c", c=BW)[:, :, 0:TT]).then_inc(wh_ok, 1)

            dve.wait_ge(bg_in, 16)

            def residual(i, c, n_res, st):
                dve.wait_ge(agg_mm, n_res)
                st.then(v.scalar_tensor_tensor(out=gt2[:, c, :], in0=P[0:TT, 2 * c:2 * c + 2, :].rearrange("p b n -> p (b n)"),
                                               scalar=nsc[:, 1, bass.ds(i, 1)], in1=bgb[:, :], op0=ALU.mult, op1=ALU.add))
                dve.wait_ge(res_ok, n_res)
                v.scalar_tensor_tensor(out=xt2[:, c, :], in0=gt2[:, c, :], scalar=0.0, in1=xt2[:, c, :],
                                       op0=ALU.max, op1=ALU.add).then_inc(x2_ok, 1)
                dve.wait_ge(x2_ok, n_res)
                normalize(st, xt2[:, c, :], at2[:, c, :], var2, std2, n_res).then_inc(h2_ok, 1)

            with dve.Fori(0, NT // 2 - 1) as it, steps.loop(it, NT // 2 - 1, 8) as st:
                for c in range(2):
                    for h in range(2):
                        adj_hi_dve(it * 2 + (c + 1), h, it * 4 + (2 * c + h + 1))
                        adj_lo(it * 2 + (c + 1), h, it * 4 + (2 * c + h + 3))
                    residual(it * 2 + c, c, it * 2 + (c + 1), st)
            for h in range(2):
                adj_hi_dve(NT - 1, h, 2 * (NT - 2) + h + 1)
                adj_lo(NT - 1, h, 2 * (NT - 1) + h + 1)
            for c in range(2):
                residual(NT - 2 + c, c, NT - 1 + c, steps)

            s = small
            dve.wait_ge(lg_mm, NT)
            v.tensor_copy(s["lg"][:, :, :], P[0:TT, 6, 0:NT * NX].rearrange("p (i e) -> p i e", e=NX)).then_inc(lg_evac, 1)
            dve.wait_ge(lg_evac, 1)

            def per_token(a):
                return a[:, :, None].broadcast_to([TT, NT, NX])

            def per_expert(a):
                return a[:, None, :].broadcast_to([TT, NT, NX])

            steps.then(v.tensor_reduce(s["m1"][:, :], s["lg"][:, :, :], X, ALU.max))
            v.tensor_tensor(s["pr"][:, :, :], s["lg"][:, :, :], per_token(s["m1"]), ALU.subtract).then_inc(dmax_ok, 1)
            dve.wait_ge(exp_ok, 1)
            steps.then(v.tensor_reduce(s["den"][:, :], s["pr"][:, :, :], X, ALU.add))
            steps.then(v.reciprocal(s["den"][:, :], s["den"][:, :]))
            steps.then(v.tensor_tensor(s["pr"][:, :, :], s["pr"][:, :, :], per_token(s["den"]), ALU.mult))
            dve.wait_ge(const_ok, 12)
            for m, oh in (("m1", "ohe1"), ("m2", "ohe2")):
                steps.then(v.tensor_reduce(s[m][:, :], s["pr"][:, :, :], X, ALU.max))
                steps.then(v.tensor_tensor(s["cand"][:, :, :], s["pr"][:, :, :], per_token(s[m]), ALU.is_equal))
                steps.then(v.tensor_tensor(s["cand"][:, :, :], s["cand"][:, :, :], per_expert(io8), ALU.mult))
                steps.then(v.tensor_reduce(s["cm"][:, :], s["cand"][:, :, :], X, ALU.min))
                steps.then(v.tensor_tensor(s[oh][:, :, :], per_expert(io8), per_token(s["cm"]), ALU.is_equal))
                if m == "m1":
                    steps.then(v.scalar_tensor_tensor(out=s["pr"][:, :, :], in0=s[oh][:, :, :], scalar=-2.0, in1=s["pr"][:, :, :],
                                                      op0=ALU.mult, op1=ALU.add))
            steps.then(v.tensor_tensor(s["den"][:, :], s["m1"][:, :], s["m2"][:, :], ALU.add))
            steps.then(v.tensor_scalar(s["den"][:, :], s["den"][:, :], EPS, None, ALU.max))
            steps.then(v.reciprocal(s["den"][:, :], s["den"][:, :]))
            v.tensor_tensor(s["wk1"][:, :], s["m1"][:, :], s["den"][:, :], ALU.mult)
            steps.then(v.tensor_tensor(s["wk2"][:, :], s["m2"][:, :], s["den"][:, :], ALU.mult))
            steps.then(v.scalar_tensor_tensor(out=s["v"][:, :, :], in0=s["ohe1"][:, :, :], scalar=-1.0, in1=s["ohe2"][:, :, :],
                                              op0=ALU.add, op1=ALU.add))
            for w, oh in (("wk1", "ohe1"), ("wk2", "ohe2")):
                steps.then(v.tensor_tensor(s["cand"][:, :, :], s[oh][:, :, :], per_token(s[w]), ALU.mult))
                steps.then(v.tensor_tensor(s["v"][:, :, :], s["v"][:, :, :], s["cand"][:, :, :], ALU.add))
            for c in range(2):
                dve.wait_ge(x2_st[c], 16 * NT)
            for i in range(NT):
                if i >= 2:
                    dve.wait_ge(vb_mm, i - 1)
                v.tensor_tensor(diag[:, i % 2, :, :], ident[0:TT, None, 0:TT].broadcast_to([TT, NX, TT]),
                                s["v"][:, i, :, None].broadcast_to([TT, NX, TT]), ALU.mult).then_inc(diag_ok, 1)
            dve.wait_ge(vb_ok, NT)
            with dve.Fori(0, NX // 2) as it:
                for c in range(2):
                    e = it * 2 + c
                    if c == 0:
                        dve.wait_ge(cs_mm, it * 2 + 0) if False else None
                    at_ = 0
                    for i in range(NT):
                        vi = s["v"][:, i, bass.ds(e, 1)]
                        if i:
                            v.tensor_scalar(cmpm[:, c, at_:at_ + i * TT], vb[:, bass.ds(e, 1), 0:i * TT].rearrange("p a t -> p (a t)"),
                                            vi, None, ALU.is_ge, ALU.add, accum_out=s["r1"][:, i, bass.ds(e, 1)])
                        v.scalar_tensor_tensor(out=cmpm[:, c, at_ + i * TT:at_ + (i + 1) * TT],
                                               in0=vb[:, bass.ds(e, 1), i * TT:(i + 1) * TT].rearrange("p a t -> p (a t)"),
                                               scalar=vi, in1=lower[:, :], op0=ALU.is_ge, op1=ALU.mult,
                                               accum_out=s["r2"][:, i, bass.ds(e, 1)]).then_inc(cmp_ok, 1)
                        at_ += (i + 1) * TT
                    dve.wait_ge(cs_mm, e + 1)
            steps.then(v.memset(s["r1"][:, 0, :], 0.0))
            steps.then(v.tensor_tensor(s["rank"][:, :, :], s["r1"][:, :, :], s["r2"][:, :, :], ALU.add))
            steps.then(v.tensor_tensor(s["rank"][:, :, :], s["rank"][:, :, :],
                                       P[0:TT, 6, 0:NT * NX].rearrange("p (i e) -> p i e", e=NX), ALU.subtract))
            steps.then(v.tensor_tensor(s["rank"][:, :, :], s["rank"][:, :, :], per_token(s["left"]), ALU.add))
            v.tensor_scalar(s["keep"][:, :, :], s["rank"][:, :, :], float(CAP), None, ALU.is_lt)
            steps.then(v.tensor_scalar(s["rank"][:, :, :], s["rank"][:, :, :], float(CAP), None, ALU.min))
            steps.then(v.tensor_tensor(s["rank"][:, :, :], s["rank"][:, :, :], per_expert(io392), ALU.add))
            for k, (oh, sl, kp) in enumerate((("ohe1", "sl1", "kp1"), ("ohe2", "sl2", "kp2"))):
                steps.then(v.tensor_tensor(s["cand"][:, :, :], s[oh][:, :, :], s["rank"][:, :, :], ALU.mult))
                steps.then(v.tensor_reduce(s[sl][:, :], s["cand"][:, :, :], X, ALU.add))
                steps.then(v.tensor_tensor(s["cand"][:, :, :], s[oh][:, :, :], s["keep"][:, :, :], ALU.mult))
                steps.then(v.tensor_reduce(s[kp][:, :], s["cand"][:, :, :], X, ALU.add))
                steps.then(v.tensor_copy(gidx[:, k, :], s[sl][:, :]))
                steps.then(v.tensor_scalar(s["cm"][:, :], s[kp][:, :], -100000.0, 100000.0, ALU.mult, ALU.add))
                ins = v.tensor_tensor(sidx[:, k, :], s[sl][:, :], s["cm"][:, :], ALU.add)
                if k == 0:
                    steps.then(ins)
            ins.then_inc(sidx_ok, 1)
            v.tensor_tensor(s["wk1"][:, :], s["wk1"][:, :], s["kp1"][:, :], ALU.mult)
            steps.then(v.tensor_tensor(s["wk2"][:, :], s["wk2"][:, :], s["kp2"][:, :], ALU.mult))
            steps.then(v.tensor_tensor(s["den"][:, :], s["wk1"][:, :], s["wk2"][:, :], ALU.add))
            steps.then(v.tensor_scalar(s["den"][:, :], s["den"][:, :], EPS, None, ALU.max))
            steps.then(v.reciprocal(s["den"][:, :], s["den"][:, :]))
            v.tensor_tensor(s["wk1"][:, :], s["wk1"][:, :], s["den"][:, :], ALU.mult)
            steps.then(v.tensor_tensor(s["wk2"][:, :], s["wk2"][:, :], s["den"][:, :], ALU.mult))

            def ex_split_lo(e1, chunks=range(HC)):
                for h in chunks:
                    dve.wait_ge(exh, e1 * 8 + (h + 1))
                    v.tensor_tensor(ex_lo[:, h, :], P[:, h % 2, 0:CAPR], ex_hi[:, h, :].bitcast(F32), ALU.subtract).then_inc(exl, 1)

            def moe_lo(e, k, hi, lo, slots=range(8)):
                for q in slots:
                    dve.wait_ge(hi_ok, e * 24 + (MOE + 8 * k + q + 1))
                    v.tensor_tensor(lo[:, q, :], raw[:, q, :], hi[:, q, :].bitcast(F32), ALU.subtract).then_inc(lo_ok, 1)

            def swiglu(e, st):
                for m in range(FC):
                    dve.wait_ge(sg_ok, e * FC + (m + 1))
                    v.tensor_tensor(gf[:, m % 2, :], sg[:, m % 2, :], P[:, 2 + m % 2, 0:CAPR], ALU.mult).then_inc(gf_ok, 1)
                    dve.wait_ge(gh_ok, e * FC + (m + 1))
                    v.tensor_tensor(g_lo[:, m, :], gf[:, m % 2, :], g_hi[:, m, :].bitcast(F32), ALU.subtract).then_inc(gl_ok, 1)

            def result(e, u):
                dve.wait_ge(dn_mm, e * 8 + (u + 1))
                if u >= 4:
                    dve.wait_ge(eo_st[u % 4], e * 32 + 16)
                v.tensor_copy(eo[:, u % 4, :], P[0:CA, 6 + u % 2, :]).then_inc(eo_ok, 1)

            def results_stored(e):
                for c in range(4):
                    dve.wait_ge(eo_st[c], e * 32 + 32)

            moe_lo(0, 0, s0_hi, s0_lo)
            dve.wait_ge(ein_st, 16 * 2 * NT)
            dve.wait_ge(cs_mm, NX)
            moe_lo(0, 1, s1_hi, s1_lo)
            ex_split_lo(0)
            moe_lo(0, 2, s2_hi, s2_lo)
            with dve.Fori(0, NX - 1) as e:
                swiglu(e, None)
                for u in range(9):
                    if u < 8:
                        ex_split_lo(e + 1, (u,))
                        hi, lo = ((s0_hi, s0_lo), (s1_hi, s1_lo))[u // 4]
                        moe_lo(e + 1, u // 4, hi, lo, (2 * (u % 4), 2 * (u % 4) + 1))
                    if u >= 1:
                        result(e, u - 1)
                results_stored(e)
                moe_lo(e + 1, 2, s2_hi, s2_lo)
            swiglu(NX - 1, None)
            for u in range(8):
                result(NX - 1, u)
            results_stored(NX - 1)
            for i in range(NT):
                c = i % 2
                dve.wait_ge(g1_in[c], 32 * (i // 2 + 1))
                dve.wait_ge(x2_in[c], 16 * (i // 2 + 1))
                steps.then(v.scalar_tensor_tensor(out=x2t[:, c, :], in0=r1t[:, c, :], scalar=s["wk1"][:, i:i + 1], in1=x2t[:, c, :],
                                                  op0=ALU.mult, op1=ALU.add))
                v.scalar_tensor_tensor(out=x2t[:, c, :], in0=r2t[:, c, :], scalar=s["wk2"][:, i:i + 1], in1=x2t[:, c, :],
                                       op0=ALU.mult, op1=ALU.add).then_inc(o_ok, 1)

        @block.tensor
        def _(pe):
            mm = nc.tensor.matmul

            def three(out, lh, ll, rh, rl_, first, last):
                mm(out, lh, rh, start=first, stop=False)
                mm(out, lh, rl_, start=False, stop=False)
                return mm(out, ll, rh, start=False, stop=last)

            pe.wait_ge(const_ok, 9)
            with pe.Fori(0, NT // 2) as it:
                for c in range(2):
                    pe.wait_ge(xn_ok, it * 2 + (c + 1))
                    for h in range(HC):
                        ins = nc.tensor.transpose(P[:, 2 * c + h // 4, (h % 4) * TT:(h % 4 + 1) * TT],
                                                  xin[:, c, h * 128:(h + 1) * 128], ident[0:TT, 0:TT])
                    ins.then_inc(tr_done, 1)
                    pe.wait_ge(lo_x, it * 2 + (c + 1))
            pe.wait_ge(ohb_ok, 2)
            for k in range(EC // 8):
                ins = mm(P[0:80, 7, 0:80], oh_d[:, 8 * k:8 * k + 8, :].rearrange("p a b -> p (a b)"),
                         oh_s[:, 8 * k:8 * k + 8, :].rearrange("p a b -> p (a b)"), start=(k == 0), stop=(k == EC // 8 - 1))
            ins.then_inc(graph_mm, 1)
            pe.wait_ge(gstep, 1)
            mm(P[0:NT, 7, 128:128 + NT], sel80[:, :], hs[:, :], start=True, stop=True).then_inc(graph_mm, 1)
            pe.wait_ge(gstep, 3)
            mm(P[0:NB, 7, 160:161], upper[:, :], nch[:, 0:1], start=True, stop=True).then_inc(graph_mm, 1)
            pe.wait_ge(gstep, 4)
            mm(P[0:1, 6, 0:NCH], ones[0:NB, 0:1], ge[:, :], start=True, stop=True).then_inc(graph_mm, 1)
            pe.wait_ge(gstep, 6)

            def positions(cg, b):
                pe.wait_ge(sm_ok, cg * BPG + (b + 1))
                for c in range(BC):
                    ins = mm(P[0:TT, 7, 256 + c:257 + c], sm[:, c * TT:(c + 1) * TT], ones[0:NB, 0:1], start=True, stop=True)
                ins.then_inc(graph_mm, 1)

            def row_tile(out, i, g, first, last, between=None):
                for s in range(8):
                    if first:
                        pe.wait_ge(lo_ok, g * 8 + (s + 1))
                    ins = three(out, xt_hi[:, s, i * TT:(i + 1) * TT], xt_lo[:, s, i * TT:(i + 1) * TT],
                                s0_hi[:, s, :], s0_lo[:, s, :], s == 0, s == 7)
                    if last and s < 7:
                        ins.then_inc(w_used, 1)
                    if between:
                        between(s)
                return ins

            def kv_tile(cg, i):
                pe.wait_ge(kv_evac, cg * 20 + (NT + i + 1))
                pe.wait_ge(phik_ok, cg * NT + (i + 1))
                if i == 0:
                    pe.wait_ge(at_evac, cg * 20 + 1)
                for j in range(PAIRS):
                    ins = mm(P[:, 4 + j // 2, (j % 2) * KVW:(j % 2 + 1) * KVW], phik[:, i, j * 128:(j + 1) * 128],
                             vt[:, i % 2, j, :], start=(i == 0 and j % 2 == 0), stop=(i == NT - 1), skip_group_check=True)
                ins.then_inc(kv_mm, 1)

            def attend(cg, j):
                pe.wait_ge(phiq_ok, cg * 12 + 3 * (j + 1))
                if j == 0:
                    pe.wait_ge(kvblk_ok, cg * 8 + 8)
                for gg in range(5):
                    u = 5 * j + gg
                    if u >= 2:
                        pe.wait_ge(at_evac, cg * 20 + u)
                    for t in range(2):
                        i = 2 * gg + t
                        ins = mm(P[0:TT, 4 + u % 2, t * AW:(t + 1) * AW], phiq[:, j % 2, i * TT:(i + 1) * TT],
                                 kvblk[:, j, :], start=True, stop=True)
                    ins.then_inc(at_mm, 1)

            with pe.Fori(0, HG) as cg:
                for i in range(NT):
                    if i >= 4:
                        pe.wait_ge(kv_evac, cg * 20 + (i - 3))
                    ins = row_tile(P[0:TT, i % 4, :], i, cg * 3, i == 0, i == NT - 1)
                    ins.then_inc(proj, 1)
                    if i == NT - 1:
                        pe.wait_ge(proj, cg * UNITS + (i + 1))
                        pe.nop().then_inc(w_used, 1)
                for i in range(NT):
                    pe.wait_ge(kv_evac, cg * 20 + (NT + i - 3))
                    ins = row_tile(P[0:TT, (NT + i) % 4, :], i, cg * 3 + 1, i == 0, i == NT - 1)
                    ins.then_inc(proj, 1)
                    if i == NT - 1:
                        pe.wait_ge(proj, cg * UNITS + (NT + i + 1))
                        pe.nop().then_inc(w_used, 1)
                    if i >= 1:
                        kv_tile(cg, i - 1)
                    if i >= 3:
                        positions(cg, i - 3)
                kv_tile(cg, NT - 1)
                for q in range(3 * PAIRS):
                    j, a = q // 3, QCUT[q % 3]
                    n = QCUT[q % 3 + 1] - a
                    if q < 4:
                        pe.wait_ge(kv_evac, cg * 20 + (2 * NT - 3 + q))
                    else:
                        pe.wait_ge(q_evac, cg * 12 + (q - 3))
                    for s in range(8):
                        if q == 0:
                            pe.wait_ge(lo_ok, cg * 24 + (16 + s + 1))
                        ins = three(P[:, q % 4, 0:n], s0_hi[:, s, j * 128:(j + 1) * 128], s0_lo[:, s, j * 128:(j + 1) * 128],
                                    xt_hi[:, s, a:a + n], xt_lo[:, s, a:a + n], s == 0, s == 7)
                        if q == 3 * PAIRS - 1 and s < 7:
                            ins.then_inc(w_used, 1)
                    ins.then_inc(proj, 1)
                    if q == 3 * PAIRS - 1:
                        pe.wait_ge(proj, cg * UNITS + UNITS)
                        pe.nop().then_inc(w_used, 1)
                    positions(cg, q + 7)
                    if q % 3 == 0 and j >= 1:
                        attend(cg, j - 1)
                positions(cg, BPG - 1)
                attend(cg, PAIRS - 1)
            def chunk_group(p, n):
                pe.wait_ge(adj_sum, n * CG + CG)
                for c in range(CG):
                    pe.wait_ge(ohs_ok, n * 2 + (1 + c // 2))
                    pe.wait_ge(mv_ok, n * CG + (c + 1))
                    b, a = 4 + 2 * p + c // 2, (c % 2) * BW
                    mm(P[0:TT, b, a:a + TT + 2], ohs[:, p, c, 0:TT], mvt[:, p, c, 0:TT + 2], start=True, stop=True)
                    ins = mm(P[0:TT, b, a + TT + 2:a + BW], ohd[:, p, c, 0:TT], mvt[:, p, c, TT:TT + 2], start=True, stop=True)
                ins.then_inc(ch_mm, 1)

            for n in range(2 * NT):
                g, i = n // NT, n % NT
                if n >= 4:
                    pe.wait_ge(g_evac, n - 3)
                def between(s, n=n):
                    if n >= GT0 and 1 <= s <= 2 * GL:
                        k = 2 * GL * (n - GT0) + s - 1
                        chunk_group(k % 2, k)
                ins = row_tile(P[0:TT, n % 4, :], i, 6 + g, i == 0, i == NT - 1, between)
                ins.then_inc(proj, 1)
                if i == NT - 1:
                    pe.wait_ge(proj, HG * UNITS + n + 1)
                    pe.nop().then_inc(w_used, 1)
            for p in range(2):
                chunk_group(p, NGR - 2 + p)
            def aggregate(c, i):
                for j in range(NT):
                    pe.wait_ge(yl_ok, j + 1)
                    if j % 5 == 0:
                        pe.wait_ge(wl_ok, i * 2 + (j // 5 + 1))
                    for h in range(2):
                        ins = three(P[0:TT, 2 * c + h, :], w_hi[:, j, :], w_lo[:, j, :], y_hi[:, j, h * SC:(h + 1) * SC],
                                    y_lo[:, j, h * SC:(h + 1) * SC], j == 0, j == NT - 1)
                    if j == 4:
                        ins.then_inc(wh_free, 1)
                ins.then_inc(agg_mm, 1)
                pe.wait_ge(agg_mm, i + 1)
                pe.nop().then_inc(wh_free, 1)

            def h2_transposes(c, i):
                pe.wait_ge(h2_ok, i + 1)
                for h in range(HC):
                    ins = nc.tensor.transpose(P[:, 4 + h // 4, (h % 4) * TT:(h % 4 + 1) * TT],
                                              at2[:, c, h * 128:(h + 1) * 128], ident[0:TT, 0:TT])
                ins.then_inc(tr2, 1)

            def logits(i):
                pe.wait_ge(h2t_ok, i + 1)
                for h in range(HC):
                    ins = mm(P[0:TT, 6, bass.ds(i * NX, NX)], h2t[:, h, :], wrt[:, h, :], start=(h == 0), stop=(h == HC - 1))
                ins.then_inc(lg_mm, 1)

            pe.wait_ge(g_evac, 2 * NT)
            aggregate(0, 0)
            aggregate(1, 1)
            h2_transposes(0, 0)
            pe.wait_ge(wr_in, 16)
            with pe.Fori(0, NT // 2 - 1) as it:
                for c in range(2):
                    aggregate(c, it * 2 + (c + 2))
                    logits(it * 2 + c)
                    h2_transposes(1 - c, it * 2 + (c + 1))
            logits(NT - 2)
            h2_transposes((NT - 1) % 2, NT - 1)
            logits(NT - 1)
            for i in range(NT):
                c = i % 2
                pe.wait_ge(diag_ok, i + 1)
                if i >= 2:
                    pe.wait_ge(vb_ok, i - 1)
                for h in range(2):
                    ins = mm(P[0:TT, 2 * c + h, 0:500], ones[0:TT, 0:TT], diag[:, c, 4 * h:4 * h + 4, :].rearrange("p a b -> p (a b)"),
                             start=True, stop=True)
                ins.then_inc(vb_mm, 1)
            with pe.Fori(0, NX // 2) as it:
                for c in range(2):
                    at_ = 0
                    for i in range(NT):
                        pe.wait_ge(cmp_ok, it * 20 + (c * NT + i + 1))
                        for j in range(i + 1):
                            ins = mm(P[0:TT, 6, bass.ds(it * 2 + (c + j * NX), 1)], cmpm[:, c, at_ + j * TT:at_ + (j + 1) * TT],
                                     onesb[0:TT, 0:1], start=(i == 0), stop=(i == NT - 1), skip_group_check=True)
                        at_ += (i + 1) * TT
                    ins.then_inc(cs_mm, 1)

            def transposes(e1, chunks=range(HC)):
                pe.wait_ge(rows_in, e1 * 16 + 16)
                for h in chunks:
                    if h >= 2:
                        pe.wait_ge(exl, e1 * 8 + (h - 1))
                    for a in range(4):
                        ins = nc.tensor.transpose(P[:, h % 2, a * CA:(a + 1) * CA], rows[:, a, h * 128:(h + 1) * 128], ident[0:CA, 0:CA])
                    ins.then_inc(etr, 1)

            def up(e):
                for m in range(FC):
                    ms = slice(m * 128, (m + 1) * 128)
                    if m >= 2:
                        pe.wait_ge(gf_ok, e * FC + (m - 1))
                    for k, (hi, lo) in enumerate(((s0_hi, s0_lo), (s1_hi, s1_lo))):
                        for h in range(HC):
                            if m == 0:
                                pe.wait_ge(lo_ok, e * 24 + (MOE + 8 * k + h + 1))
                                if k == 0:
                                    pe.wait_ge(exl, e * 8 + (h + 1))
                            ins = three(P[:, 2 + 2 * k + m % 2, 0:CAPR], hi[:, h, ms], lo[:, h, ms], ex_hi[:, h, :], ex_lo[:, h, :],
                                        h == 0, h == HC - 1)
                            if m == FC - 1 and not (k == 1 and h == HC - 1):
                                ins.then_inc(w_used, 1)
                    ins.then_inc(pg_mm, 1)
                pe.wait_ge(pg_mm, e * FC + FC)
                pe.nop().then_inc(w_used, 1)

            def down(e, parts=range(8)):
                for u in parts:
                    a, h = u // 2, u % 2
                    if u >= 2:
                        pe.wait_ge(eo_ok, e * 8 + (u - 1))
                    for d in range(FC):
                        if u < 2:
                            pe.wait_ge(lo_ok, e * 24 + (MOE + 16 + 2 * d + h + 1))
                        if u == 0:
                            pe.wait_ge(gl_ok, e * FC + (d + 1))
                        ins = three(P[0:CA, 6 + u % 2, :], g_hi[:, d, a * CA:(a + 1) * CA], g_lo[:, d, a * CA:(a + 1) * CA],
                                    s2_hi[:, 2 * d + h, :], s2_lo[:, 2 * d + h, :], d == 0, d == FC - 1)
                    ins.then_inc(dn_mm, 1)
                    if u == 7:
                        pe.wait_ge(dn_mm, e * 8 + 8)
                        pe.nop().then_inc(w_used, 8)

            transposes(0)
            with pe.Fori(0, NX - 1) as e:
                up(e)
                transposes(e + 1, (0, 1))
                for u in range(8):
                    down(e, (u,))
                    if u + 2 < HC:
                        transposes(e + 1, (u + 2,))
            up(NX - 1)
            down(NX - 1)


def kernel(x, src, dst, edge_weight, L0_gnn_W, L0_gnn_b, L0_mix_W_qkv, L0_mix_b_qkv, L0_mix_W_proj, L0_mix_b_proj,
           L0_ffn_router_weight, L0_ffn_ff_pre_act_weight, L0_ffn_gate_weight, L0_ffn_ff_post_act_weight):
    import numpy as np
    import concourse.bacc as bacc
    from concourse.bass_utils import run_bass_kernel_spmd as run

    n = np.asarray
    src, dst, qkv, gw = n(src), n(dst), n(L0_mix_W_qkv), n(L0_gnn_W)
    parts = []
    for g in range(HG):
        c = slice(g * SC, (g + 1) * SC)
        parts += [qkv[:, D:2 * D][:, c], qkv[:, 2 * D:][:, c], qkv[:, :D][:, c]]
    parts += [gw[:, :SC], gw[:, SC:]]
    pre, gate, post = n(L0_ffn_ff_pre_act_weight), n(L0_ffn_gate_weight), n(L0_ffn_ff_post_act_weight)
    arrays = {
        "x": n(x),
        "edges_n": np.stack([src.reshape(TT, EC), dst.reshape(TT, EC)]),
        "edges_c": np.stack([np.ascontiguousarray(src.reshape(EC, TT).T), np.ascontiguousarray(dst.reshape(EC, TT).T)]),
        "w_c": np.ascontiguousarray(n(edge_weight).reshape(EC, TT).T),
        "wmain": np.stack(parts),
        "bqkv": n(L0_mix_b_qkv),
        "bg": n(L0_gnn_b),
        "wr_t": np.ascontiguousarray(n(L0_ffn_router_weight).T.reshape(HC, 128, NX).transpose(1, 0, 2)).reshape(128, HC * NX),
        "wpre": np.ascontiguousarray(pre.transpose(0, 2, 1).reshape(NX, HC, 128, DFF).transpose(2, 0, 1, 3)),
        "wgate": np.ascontiguousarray(gate.transpose(0, 2, 1).reshape(NX, HC, 128, DFF).transpose(2, 0, 1, 3)),
        "wpost": np.ascontiguousarray(post.transpose(0, 2, 1).reshape(NX, FC, 128, 2, SC).transpose(2, 0, 1, 3, 4)).reshape(128, NX, 8, SC),
    }
    nc = bacc.Bacc("TRN2", target_bir_lowering=False, num_devices=1)
    args = [nc.dram_tensor(k, a.shape, mybir.dt.from_np(a.dtype), kind="ExternalInput").ap() for k, a in arrays.items()]
    out = nc.dram_tensor("out", [T, D], F32, kind="ExternalOutput").ap()
    build(nc, *args, out)
    r = run(nc, [arrays], core_ids=[0])
    return r.results[0]["out"]
```

```python
from contextlib import ExitStack, contextmanager

import concourse.bass as bass
from concourse import mybir

F32 = mybir.dt.float32
FR = mybir.dt.float32r
BF16 = mybir.dt.bfloat16
I32 = mybir.dt.int32
ALU = mybir.AluOpType
ACT = mybir.ActivationFunctionType
X = mybir.AxisListType.X

T = 1250
TT = 125
NT = T // TT
D = 1024
HC = D // 128
SC = 512
NG = 8
HG = 2
PAIRS = 4
KVW = 129
AW = 130
QCUT = [0, 418, 834, 1250]
UNITS = 2 * NT + 3 * PAIRS

NE = 40000
EC = NE // TT
BC = 8
EB = BC * TT
NBLK = EC // BC
BPG = NBLK // HG
NB = NT * NT
CHUNK = 128
CG = 4
NCH = -(-((NE + NB * (CHUNK - 1)) // CHUNK) // 8) * 8
NGR = NCH // CG
GT0 = 3
GL = (NGR - 2) // (2 * NT - GT0) // 2
BW = 129
MAGIC = 1.5 * 2.0**23

NX = 8
DFF = 512
FC = DFF // 128
CAP = 391
CAPR = CAP + 1
CA = CAPR // 4
EPS = 1.1920929e-07
LNEPS = 1e-05


class Count:

    def __init__(self, engine, sem):
        self.engine, self.sem, self.n = engine, sem, 0

    def then(self, instruction):
        instruction.then_inc(self.sem, 1)
        self.n = self.n + 1
        self.engine.wait_ge(self.sem, self.n)

    @contextmanager
    def loop(self, it, times, per):
        start = self.n
        inner = Body(self, start + it * per, per)
        yield inner
        assert inner.k == per, f"the body raises its semaphore {inner.k} times"
        self.n = start + times * per


class Body:

    def __init__(self, count, base, per):
        self.count, self.base, self.k = count, base, 0

    def then(self, instruction):
        instruction.then_inc(self.count.sem, 1)
        self.k += 1
        self.count.engine.wait_ge(self.count.sem, self.base + self.k)


def build(nc, x, edges_n, edges_c, w_c, wmain, bqkv, bg, wr_t, wpre, wgate, wpost, out):
    with ExitStack() as ctx:
        names = [0]

        def at(off, shape, dt, name):
            t = nc.alloc_sbuf_tensor_at(name, shape, dt, offset=BASE + off)
            size = 4 if dt != BF16 else 2
            for n in shape[1:]:
                size *= n
            assert BASE + off + size <= nc.sbuf_usable_end, (name, BASE + off + size - nc.sbuf_usable_end)
            return t

        def sem(name):
            return ctx.enter_context(nc.semaphore(name))

        def dram(name, shape, dt=F32):
            return nc.dram_tensor(name, shape, dt).ap()

        BASE = -(-nc.sbuf_base // 32) * 32
        A = 0
        SL = A + 81920
        RAW = SL + 32768
        WR = RAW + 16384
        RR = WR + NB * BW * 4 + 16
        RR = -(-RR // 32) * 32
        xt_hi = at(A, [128, HC, T], FR, "xt_hi")
        xt_lo = at(A + 40000, [128, HC, T], FR, "xt_lo")
        s0_hi = at(SL, [128, 8, SC], FR, "s0_hi")
        s0_lo = at(SL + 16384, [128, 8, SC], FR, "s0_lo")
        raw = at(RAW, [128, 8, SC], F32, "raw")

        xin = at(WR, [TT, 2, D], F32, "xin")
        en = at(WR + 8192, [TT, 2, EC], I32, "en")
        ec = at(WR + 10752, [TT, 2, EC], I32, "ec")
        wc = at(WR + 13312, [TT, EC], F32, "wc")
        tn = at(WR + 14592, [TT, 3, EC], F32, "tn")
        tc = at(WR + 18432, [TT, 3, EC], F32, "tc")
        bkt = at(WR + 22272, [TT, EC], BF16, "bkt")
        oh_d = at(WR + 22912, [TT, EC, NT], BF16, "oh_d")
        oh_s = at(WR + 29312, [TT, EC, NT], BF16, "oh_s")
        hq = at(WR + 35712, [80, 8, NT], F32, "hq")
        mask80 = at(WR + 36032, [80, 8, NT], F32, "mask80")
        hs = at(WR + 36352, [80, NT], F32, "hs")
        sel80 = at(WR + 36416, [80, NT], F32, "sel80")
        hist10 = at(WR + 36480, [NT, NT], F32, "hist10")
        upper = at(WR + 36544, [NB, NB], F32, "upper")
        iotak = at(WR + 36960, [NB, NCH], F32, "iotak")
        ge = at(WR + 38624, [NB, NCH], F32, "ge")
        phik = at(WR, [TT, NT, SC], F32, "phik")
        vt = at(WR + 20480, [TT, 2, PAIRS, KVW], F32, "vt")
        phiq = at(WR + 24640, [128, 2, T], F32, "phiq")
        sa = at(WR + 34656, [TT, 2, NT, 128], F32, "sa")
        kvblk = at(WR + 44896, [128, PAIRS, AW], F32, "kvblk")
        bkv = at(WR + 46976, [TT, 2, SC], F32, "bkv")
        bq = at(WR + 51072, [128, PAIRS], F32, "bq")
        adj = at(WR, [TT, NB * BW], F32, "adj")
        junk = at(WR + 40960, [TT, 4, T], BF16, "junk")
        s1_hi = at(WR, [128, 8, SC], FR, "s1_hi")
        s1_lo = at(WR + 16384, [128, 8, SC], FR, "s1_lo")
        g_hi = at(WR + 32768, [128, FC, CAPR], FR, "g_hi")
        g_lo = at(WR + 39040, [128, FC, CAPR], FR, "g_lo")

        o = RR
        def take(nbytes):
            nonlocal o
            r = o
            o += -(-nbytes // 32) * 32
            return r
        ident = at(take(512), [128, 128], F32, "ident")
        ones = at(take(512), [128, 128], F32, "ones")
        onesb = at(take(4), [128, 2], BF16, "onesb")
        iota = at(take(500), [128, TT], F32, "iota")
        iotap = at(take(4), [128, 1], F32, "iotap")
        lower = at(take(500), [TT, TT], F32, "lower")
        zero = at(take(2048), [128, SC], F32, "zero")
        offs = at(take(NCH * 4), [1, NCH], I32, "offs")
        stats = at(take(48), [TT, 2, 6], F32, "stats")
        mv = at(take(8), [TT, 2], F32, "mv")
        rstd = at(take(8), [TT, 2], F32, "rstd")
        nrm = at(take(160), [TT, 4, NT], F32, "nrm")
        nsc = at(take(80), [TT, 2, NT], F32, "nsc")
        hist = at(take(4), [NB, 1], F32, "hist")
        nch = at(take(8), [NB, 2], F32, "nch")
        incl = at(take(4), [NB, 1], F32, "incl")
        base1 = at(take(4), [NB, 1], F32, "base1")
        carry = at(take(4), [NB, 1], F32, "carry")
        zt = at(take(32), [TT, 2, 2, 2], F32, "zt")
        pw = at(take(4), [1, 1], F32, "pw")
        CST = o
        br = at(take(4000), [NB, 2, EB], BF16, "br")
        oht = at(take(2000), [NB, EB], BF16, "oht")
        sm = at(take(4000), [NB, EB], F32, "sm")
        RECO = o
        rec = at(take(EC * 16), [TT, EC, 4], F32, "rec")
        PKO = o
        pk = at(take(64), [TT, 2, BC], F32, "pk")
        idx = at(take(64), [TT, 2, BC], I32, "idx")
        rs = at(take(256), [TT, 2, BC, 4], F32, "rs")
        t_b = at(take(4096), [128, 2, SC], F32, "t_b")
        EBO = o
        e_b = at(take(4096), [128, 2, SC], F32, "e_b")
        rl = at(CST, [128, NCH, 4], F32, "rl")
        ohd = at(CST + 6656, [128, 2, CG, 128], F32, "ohd")
        ohs = at(CST + 10752, [128, 2, CG, 128], F32, "ohs")
        assert NCH * 16 <= 6656 and CST + 14848 <= PKO
        mvt = at(EBO, [128, 2, CG, 128], F32, "mvt")
        y_hi = at(A, [TT, NT, D], FR, "y_hi")
        y_lo = at(A + 40960, [TT, NT, D], FR, "y_lo")
        yraw = at(RAW, [TT, 4, D], F32, "yraw")
        w_hi = at(CST, [TT, NT, TT], FR, "w_hi")
        w_lo = at(CST + 5024, [TT, NT, TT], FR, "w_lo")
        bgb = at(SL, [TT, D], F32, "bgb")
        xt2 = at(SL + 4096, [TT, 2, D], F32, "xt2")
        at2 = at(SL + 12288, [TT, 2, D], F32, "at2")
        gt2 = at(SL + 20480, [TT, 2, D], F32, "gt2")
        h2t = at(SL + 28672, [128, HC, TT], F32, "h2t")
        diag = at(SL + 8320, [TT, 2, NX, TT], F32, "diag")
        vb = at(A, [TT, NX, T], F32, "vb")
        RS = 3
        RA = NT - RS
        MW = TT * NT * (NT + 1) // 2
        cmpm = at(A + 40000, [TT, 2, MW], BF16, "cmpm")
        o = CST + 10080
        small = {}
        for name in ("lg", "pr", "ohe1", "ohe2", "cand", "v", "rank", "keep"):
            small[name] = at(take(320), [TT, NT, NX], F32, name)
        for name in ("m1", "m2", "den", "wk1", "wk2", "sl1", "sl2", "kp1", "kp2", "cm", "left"):
            small[name] = at(take(40), [TT, NT], F32, name)
        racc = at(take(80), [TT, 2, NT], F32, "racc")
        io8 = at(take(32), [TT, NX], F32, "io8")
        io392 = at(take(32), [TT, NX], F32, "io392")
        sidx = at(take(80), [TT, 2, NT], I32, "sidx")
        gidx = at(take(80), [TT, 2, NT], I32, "gidx")
        lowx = at(take(RS * TT * 4), [TT, RS * TT], F32, "lowx")
        tok = at(take(40), [TT, NT], I32, "tok")
        places_tok = at(take(128), [CA, NX, 4], I32, "places_tok")
        rowi = at(take(16), [CA, 4], I32, "rowi")
        wrt = at(o, [128, HC, NX], F32, "wrt")
        ex_hi = at(A, [128, HC, CAPR], FR, "ex_hi")
        ex_lo = at(A + 12544, [128, HC, CAPR], FR, "ex_lo")
        s2_hi = at(A + 25088, [128, 8, SC], FR, "s2_hi")
        s2_lo = at(A + 41472, [128, 8, SC], FR, "s2_lo")
        rows = at(A + 57856, [CA, 4, D], F32, "rows")
        sg = at(CST, [128, 2, CAPR], F32, "sg")
        gf = at(CST + 3136, [128, 2, CAPR], F32, "gf")
        eo = at(o, [CA, 4, SC], F32, "eo")
        r1t = at(A, [TT, NT, D], F32, "r1t")
        r2t = at(A + 40960, [TT, NT, D], F32, "r2t")
        x2t = at(SL, [TT, NT, D], F32, "x2t")

        P = ctx.enter_context(nc.psum_tensor("P", [128, 8, 512], F32))

        bkt_d = dram("bkt_d", [NE], BF16)
        hist_d = dram("hist_d", [NB])
        rec_d = dram("rec_d", [128 * NCH, 4])
        attn_d = dram("attn_d", [T, D])
        y_d = dram("y_d", [T, D])
        x2_d = dram("x2_d", [T, D])
        h2_d = dram("h2_d", [T, D])
        tok_d = dram("tok_d", [NX * CAPR, 1], I32)
        eo_d = dram("eo_d", [NX * CAPR, D])

        x_in = [sem(f"x_in{i}") for i in range(2)]
        edges_in = sem("edges_in")
        const_ok = sem("const_ok")
        dve_step = sem("dve_step")
        act_step = sem("act_step")
        pool_step = sem("pool_step")
        var_ok = sem("var_ok")
        std_ok = sem("std_ok")
        xn_ok = sem("xn_ok")
        tr_done = sem("tr_done")
        hi_x = sem("hi_x")
        lo_x = sem("lo_x")
        bkt_ok = sem("bkt_ok")
        bkt_st = sem("bkt_st")
        ohb_ok = sem("ohb_ok")
        graph_mm = sem("graph_mm")
        gstep = sem("gstep")
        hist_st = sem("hist_st")
        hist_in = sem("hist_in")
        raw_in = [sem(f"raw_in{i}") for i in range(4)]
        hi_ok = sem("hi_ok")
        lo_ok = sem("lo_ok")
        w_used = sem("w_used")
        bias_in = sem("bias_in")
        bias_free = sem("bias_free")
        proj = sem("proj")
        kv_evac = sem("kv_evac")
        er = sem("er")
        phik_ok = sem("phik_ok")
        kv_mm = sem("kv_mm")
        kvblk_ok = sem("kvblk_ok")
        q_evac = sem("q_evac")
        phiq_ok = sem("phiq_ok")
        at_mm = sem("at_mm")
        at_evac = sem("at_evac")
        sa_st = [sem(f"sa_st{i}") for i in range(2)]
        br_in = [sem(f"br_in{i}") for i in range(2)]
        br_free = sem("br_free")
        sm_ok = sem("sm_ok")
        rs_ok = sem("rs_ok")
        scat = [sem(f"scat{i}") for i in range(2)]
        tok_zero = sem("tok_zero")
        g_evac = sem("g_evac")
        y_st = [sem(f"y_st{i}") for i in range(2)]
        rl_in = sem("rl_in")
        ohd_ok = sem("ohd_ok")
        ohs_ok = sem("ohs_ok")
        mv_ok = sem("mv_ok")
        adj_sum = sem("adj_sum")
        ch_mm = sem("ch_mm")
        nrm_ok = sem("nrm_ok")
        nrm_sq = sem("nrm_sq")
        nsc_ok = sem("nsc_ok")
        y_in = [sem(f"y_in{i}") for i in range(4)]
        yh_ok = sem("yh_ok")
        yl_ok = sem("yl_ok")
        wh_ok = sem("wh_ok")
        wl_ok = sem("wl_ok")
        wh_free = sem("wh_free")
        agg_mm = sem("agg_mm")
        bg_in = sem("bg_in")
        res_in = [sem(f"res_in{i}") for i in range(2)]
        res_ok = sem("res_ok")
        var2 = sem("var2")
        std2 = sem("std2")
        x2_ok = sem("x2_ok")
        h2_ok = sem("h2_ok")
        x2_st = [sem(f"x2_st{i}") for i in range(2)]
        wr_in = sem("wr_in")
        tr2 = sem("tr2")
        h2t_ok = sem("h2t_ok")
        lg_mm = sem("lg_mm")
        lg_evac = sem("lg_evac")
        dmax_ok = sem("dmax_ok")
        exp_ok = sem("exp_ok")
        diag_ok = sem("diag_ok")
        vb_mm = sem("vb_mm")
        vb_ok = sem("vb_ok")
        cmp_ok = sem("cmp_ok")
        cs_mm = sem("cs_mm")
        racc_ok = sem("racc_ok")
        row_sum = sem("row_sum")
        sidx_ok = sem("sidx_ok")
        tok_st = sem("tok_st")
        tok_in = sem("tok_in")
        rowi_ok = sem("rowi_ok")
        rows_in = sem("rows_in")
        etr = sem("etr")
        exh = sem("exh")
        exl = sem("exl")
        pg_mm = sem("pg_mm")
        sg_ok = sem("sg_ok")
        gf_ok = sem("gf_ok")
        gh_ok = sem("gh_ok")
        gl_ok = sem("gl_ok")
        dn_mm = sem("dn_mm")
        eo_ok = sem("eo_ok")
        eo_st = [sem(f"eo_st{i}") for i in range(4)]
        g1_in = [sem(f"g1_in{i}") for i in range(NT)]
        x2_in = sem("x2_in")
        o_ok = sem("o_ok")
        o_st = sem("o_st")

        MOE = 8 * NG
        GM0 = 4

        x_v = x.rearrange("(i p) d -> p i d", p=TT)
        attn_v = attn_d.rearrange("(i p) (g c) -> p i g c", p=TT, c=128)
        y_v = y_d.rearrange("(i p) (g c) -> p i g c", p=TT, c=SC)
        yt_v = y_d.rearrange("(i p) d -> p i d", p=TT)
        att_v = attn_d.rearrange("(i p) d -> p i d", p=TT)
        x2_v = x2_d.rearrange("(i p) d -> p i d", p=TT)
        h2_v = h2_d.rearrange("(i p) d -> p i d", p=TT)
        out_v = out.rearrange("(i p) d -> p i d", p=TT)
        wm_v = wmain.rearrange("g (s p) n -> p g s n", p=128)
        tok_v = tok_d.rearrange("(e p a) o -> p e (a o)", a=4, p=CA)
        eo_v = eo_d.rearrange("(e p a) (h n) -> p e a h n", a=4, p=CA, h=2)

        block = ctx.enter_context(nc.Block())

        @block.sync
        def _(sp):
            def load_group(g, first=False):
                for p in range(4):
                    if not first:
                        sp.wait_ge(lo_ok, g * 8 + 2 * p - 6)
                    sp.dma_start(raw[:, 2 * p:2 * p + 2, :], wm_v[:, g, 2 * p:2 * p + 2, :]).then_inc(raw_in[p], 16)

            for c in range(2):
                sp.dma_start(xin[:, c, :], x_v[:, c, :]).then_inc(x_in[c], 16)
            load_group(0, first=True)
            with sp.Fori(1, NT // 2) as it:
                for c in range(2):
                    sp.wait_ge(tr_done, it * 2 + c - 1)
                    sp.dma_start(xin[:, c, :], x_v[:, it * 2 + c, :]).then_inc(x_in[c], 16)
            with sp.Fori(0, HG) as cg:
                for k in range(1, 4):
                    load_group(cg * 3 + k)
                for j in range(PAIRS):
                    sp.wait_ge(at_evac, cg * 20 + 5 * j + 6)
                    sp.dma_start(attn_v[:, :, cg * PAIRS + j, :], sa[:, j % 2, :, :]).then_inc(sa_st[j % 2], 16)
            load_group(7)
            for g in range(2):
                with sp.Fori(0, NT // 2) as it:
                    for c in range(2):
                        sp.wait_ge(g_evac, it * 2 + (g * NT + c + 1))
                        sp.dma_start(y_v[:, it * 2 + c, g, :], t_b[0:TT, c, :]).then_inc(y_st[c], 16)
            sp.wait_ge(g_evac, 2 * NT)
            sp.dma_start(bgb[:, :], bg.partition_broadcast(TT)).then_inc(bg_in, 16)
            for c in range(2):
                sp.wait_ge(y_st[c], 16 * NT)
                sp.wait_ge(sa_st[c], 64)
            for j in range(NT):
                if j >= 4:
                    sp.wait_ge(yl_ok, j - 3)
                sp.dma_start(yraw[:, j % 4, :], yt_v[:, j, :]).then_inc(y_in[j % 4], 16)
            for c in range(2):
                sp.dma_start(xt2[:, c, :], x_v[:, c, :]).then_inc(res_in[c], 16)
                sp.dma_start(at2[:, c, :], att_v[:, c, :]).then_inc(res_in[c], 16)
            sp.wait_ge(ch_mm, NGR)
            sp.dma_start(wrt[:, :, :], wr_t.rearrange("p (h e) -> p h e", e=NX)).then_inc(wr_in, 16)
            with sp.Fori(0, NT // 2 - 1) as it:
                for c in range(2):
                    sp.wait_ge(x2_ok, it * 2 + c + 1)
                    sp.dma_start(x2_v[:, it * 2 + c, :], xt2[:, c, :]).then_inc(x2_st[c], 16)
                    sp.wait_ge(h2_ok, it * 2 + c + 1)
                    sp.dma_start(h2_v[:, it * 2 + c, :], at2[:, c, :]).then_inc(x2_st[c], 16)
                    sp.wait_ge(x2_st[c], it * 32 + 32)
                    sp.wait_ge(tr2, it * 2 + (c + 1))
                    sp.dma_start(xt2[:, c, :], x_v[:, it * 2 + (c + 2), :]).then_inc(res_in[c], 16)
                    sp.dma_start(at2[:, c, :], att_v[:, it * 2 + (c + 2), :]).then_inc(res_in[c], 16)
            for c in range(2):
                sp.wait_ge(x2_ok, NT - 1 + c)
                sp.dma_start(x2_v[:, NT - 2 + c, :], xt2[:, c, :]).then_inc(x2_st[c], 16)
                sp.wait_ge(h2_ok, NT - 1 + c)
                sp.dma_start(h2_v[:, NT - 2 + c, :], at2[:, c, :]).then_inc(x2_st[c], 16)
            def load_moe_part(e, k, src, p):
                sp.wait_ge(lo_ok, e * 24 + (MOE + 8 * k + 2 * p - 6))
                sp.dma_start(raw[:, 2 * p:2 * p + 2, :], src[:, 2 * p:2 * p + 2, :]).then_inc(raw_in[p], 16)

            def load_moe(e, k, src):
                for p in range(4):
                    load_moe_part(e, k, src, p)

            load_moe(0, 0, wpre[:, 0, :, :])
            load_moe(0, 1, wgate[:, 0, :, :])
            load_moe(0, 2, wpost[:, 0, :, :])
            with sp.Fori(0, NX - 1) as e:
                load_moe(e + 1, 0, wpre[:, e + 1, :, :])
                for u in range(9):
                    if u < 8:
                        load_moe_part(e + 1, 1 + u // 4, (wgate, wpost)[u // 4][:, e + 1, :, :], u % 4)
                    if u >= 1:
                        sp.wait_ge(eo_ok, e * 8 + u)
                        sp.dma_start(eo_v[:, e, (u - 1) // 2, (u - 1) % 2, :], eo[:, (u - 1) % 4, :]).then_inc(eo_st[(u - 1) % 4], 16)
            sp.wait_ge(w_used, MOE + 24 * (NX - 1) + 16)
            sp.wait_ge(lo_ok, MOE + 24 * NX)
            for i in range(NT):
                sp.dma_start(x2t[:, i, :], x2_v[:, i, :]).then_inc(x2_in, 16)
                if i < 8:
                    sp.wait_ge(eo_ok, (NX - 1) * 8 + i + 1)
                    sp.dma_start(eo_v[:, NX - 1, i // 2, i % 2, :], eo[:, i % 4, :]).then_inc(eo_st[i % 4], 16)
            for i in range(NT):
                sp.wait_ge(o_ok, i + 1)
                sp.dma_start(out_v[:, i, :], x2t[:, i, :]).then_inc(o_st, 16)
            sp.wait_ge(o_st, 16 * NT)

        @block.scalar
        def _(act):
            act.dma_start(en[:, :, :], edges_n.rearrange("a p c -> p a c")).then_inc(edges_in, 16)
            act.dma_start(ec[:, :, :], edges_c.rearrange("a p c -> p a c")).then_inc(edges_in, 16)
            act.dma_start(wc[:, :], w_c).then_inc(edges_in, 16)
            act.wait_ge(bkt_ok, 1)
            act.dma_start(bkt_d.rearrange("(p c) -> p c", p=TT), bkt[:, :]).then_inc(bkt_st, 16)

            def split_hi(g, dst, first=False, src=None):
                for s in range(8):
                    act.wait_ge(raw_in[s // 2], g * 16 + 16)
                    if not first:
                        act.wait_ge(w_used, g * 8 + (s - 7))
                    act.copy(dst[:, s, :], raw[:, s, :]).then_inc(hi_ok, 1)

            split_hi(0, s0_hi, first=True)
            def norm_root(i):
                act.wait_ge(var_ok, i + 1)
                act.activation(rstd[:, 0:1], rstd[:, 1:2], ACT.Sqrt).then_inc(std_ok, 1)

            def norm_hi(c, i):
                act.wait_ge(tr_done, i + 1)
                act.copy(xt_hi[:, :, bass.ds(i * TT, TT)].rearrange("p (b h) t -> p b h t", b=2),
                         P[:, 2 * c:2 * c + 2, 0:500].rearrange("p b (h t) -> p b h t", h=4)).then_inc(hi_x, 1)

            norm_root(0)
            with act.Fori(0, NT // 2 - 1) as it:
                for c in range(2):
                    norm_root(it * 2 + (c + 1))
                    norm_hi(c, it * 2 + c)
            norm_root(NT - 1)
            norm_hi(0, NT - 2)
            norm_hi(1, NT - 1)
            act.wait_ge(bkt_st, 16)
            act.wait_ge(gstep, 6)

            def load_rows(cg, b):
                act.wait_ge(br_free, cg * BPG + (b + 1))
                act.dma_start(br[:, b % 2, :],
                              bkt_d[bass.ds(cg * (BPG * EB) + b * EB, EB)].partition_broadcast(NB)).then_inc(br_in[b % 2], 16)

            with act.Fori(0, HG) as cg:
                act.wait_ge(bias_free, cg + 1)
                for k in range(2):
                    act.dma_start(bkv[:, k, :], bqkv[bass.ds(cg * SC + (k + 1) * D, SC)].partition_broadcast(TT)).then_inc(bias_in, 16)
                act.dma_start(bq[:, :], bqkv[bass.ds(cg * SC, SC)].rearrange("(j p) -> p j", p=128),
                              allow_slow_non_contiguous=True).then_inc(bias_in, 16)
                for i in range(NT):
                    act.wait_ge(kv_evac, cg * 20 + (i + 1))
                    if i >= 2:
                        act.wait_ge(phik_ok, cg * NT + (i - 1))
                    act.activation(e_b[0:TT, i % 2, :], t_b[0:TT, i % 2, :], ACT.Exp).then_inc(act_step, 1)
                    act.activation(t_b[0:TT, i % 2, :], t_b[0:TT, i % 2, :], ACT.Relu).then_inc(er, 1)
                    if i == NT - 2:
                        split_hi(cg * 3 + 1, s0_hi)
                load_rows(cg, 0)
                for i in range(NT):
                    if i >= 1:
                        load_rows(cg, i)
                    if i == NT - 2:
                        split_hi(cg * 3 + 2, s0_hi)
                act.wait_ge(phik_ok, cg * NT + NT)
                act.wait_ge(bias_in, cg * 48 + 48)
                for q in range(3 * PAIRS):
                    j, n = q // 3, QCUT[q % 3 + 1] - QCUT[q % 3]
                    if q == 3 * PAIRS - 1:
                        split_hi(cg * 3 + 3, s0_hi)
                    act.wait_ge(proj, cg * UNITS + (2 * NT + q + 1))
                    if q >= 2:
                        act.wait_ge(phiq_ok, cg * 12 + (q - 1))
                    act.activation(e_b[:, q % 2, 0:n], P[:, q % 4, 0:n], ACT.Exp, bias=bq[:, j:j + 1]).then_inc(act_step, 1)
                    act.activation(t_b[:, q % 2, 0:n], P[:, q % 4, 0:n], ACT.Relu, bias=bq[:, j:j + 1]).then_inc(q_evac, 1)
                    if q + 10 < BPG:
                        load_rows(cg, q + 10)
            def weighted(p, n):
                for c in range(CG):
                    if c % 2 == 0:
                        act.wait_ge(ohd_ok, n * 2 + (1 + c // 2))
                        act.copy(mvt[:, p, c:c + 2, TT:TT + 2], rl[:, bass.ds(n * CG + c, 2), 2:4]).then_inc(act_step, 1)
                    act.activation(mvt[:, p, c, 0:TT], ohd[:, p, c, 0:TT], ACT.Copy,
                                   scale=rl[:, bass.ds(n * CG + c, 1), 2]).then_inc(mv_ok, 1)

            act.wait_ge(phiq_ok, 24)
            for n in range(2 * NT):
                if n >= GT0:
                    with act.Fori(0, GL) as it:
                        for p in range(2):
                            weighted(p, it * 2 + (2 * GL * (n - GT0) + 2 + p))
                if n == NT - 1:
                    split_hi(7, s0_hi)
                act.wait_ge(proj, HG * UNITS + n + 1)
                if n >= 2:
                    act.wait_ge(y_st[n % 2], 16 * (n // 2))
                act.copy(t_b[0:TT, n % 2, :], P[0:TT, n % 4, :]).then_inc(g_evac, 1)
                if n == GT0 - 1:
                    for p in range(2):
                        weighted(p, p)
            act.activation(rstd[:, 0:1], ones[0:TT, 0:1], ACT.Sqrt).then_inc(act_step, 1)
            act.wait_ge(adj_sum, NCH + 2 * CG)

            def adj_hi(i, h):
                act.copy(w_hi[:, 5 * h:5 * h + 5, :],
                         adj[:, bass.ds(i * (NT * BW) + h * (5 * BW), 5 * BW)].rearrange("p (j c) -> p j c", c=BW)[:, :, 0:TT]).then_inc(wh_ok, 1)

            for h in range(2):
                adj_hi(0, h)
            act.wait_ge(nrm_ok, 1)
            act.activation(nrm[:, :, :], nrm[:, :, :], ACT.Sqrt).then_inc(nrm_sq, 1)
            act.wait_ge(nsc_ok, 1)
            act.wait_ge(w_used, 8 * NG)
            for j in range(NT):
                act.wait_ge(y_in[j % 4], 16 * (j // 4 + 1))
                act.activation(y_hi[:, j, :], yraw[:, j % 4, :], ACT.Copy, scale=nsc[:, 0, j:j + 1]).then_inc(yh_ok, 1)

            def h2_out(i):
                act.wait_ge(tr2, i + 1)
                act.copy(h2t[:, :, :].rearrange("p (b h) t -> p b (h t)", b=2), P[:, 4:6, 0:500]).then_inc(h2t_ok, 1)

            def root(i):
                act.wait_ge(var2, i + 1)
                act.activation(rstd[:, 0:1], rstd[:, 1:2], ACT.Sqrt).then_inc(std2, 1)

            root(0)
            with act.Fori(0, NT - 1) as i:
                h2_out(i)
                root(i + 1)
            h2_out(NT - 1)
            s = small
            act.wait_ge(dmax_ok, 1)
            act.activation(small["pr"][:, :, :], small["pr"][:, :, :], ACT.Exp).then_inc(exp_ok, 1)
            for i in range(NT):
                c = i % 2
                act.wait_ge(vb_mm, i + 1)
                act.copy(vb[:, :, i * TT:(i + 1) * TT].rearrange("p (b e) t -> p b e t", b=2),
                         P[0:TT, 2 * c:2 * c + 2, 0:500].rearrange("p b (e t) -> p b e t", e=4)).then_inc(vb_ok, 1)

            def row_sums():
                with act.Fori(0, NX // 2) as it:
                    for c in range(2):
                        e, at_ = it * 2 + c, TT * RS * (RS + 1) // 2
                        for i in range(RS, NT):
                            act.wait_ge(cmp_ok, it * 20 + (c * NT + i + 1))
                            if i >= RS + 4:
                                act.wait_ge(racc_ok, it * (2 * RA) + (c * RA + i - RS - 3))
                            act.activation(junk[:, i % 4, 0:(i + 1) * TT], cmpm[:, c, at_:at_ + (i + 1) * TT], ACT.Copy,
                                           accum_out=racc[:, c, i:i + 1]).then_inc(racc_ok, 1)
                            at_ += (i + 1) * TT
                        act.wait_ge(cs_mm, e + 1)
                        act.wait_ge(racc_ok, it * (2 * RA) + (c + 1) * RA)
                        act.copy(s["rank"][:, RS:, bass.ds(e, 1)], racc[:, c, RS:, None]).then_inc(row_sum, 1)

            def split_moe(e, k, dst, slots=range(8)):
                for s in slots:
                    act.wait_ge(raw_in[s // 2], e * 48 + 16 * (NG + k + 1))
                    if k == 0:
                        act.wait_ge(w_used, e * 24 + (MOE - 24 + s + 1))
                    else:
                        act.wait_ge(w_used, e * 24 + (MOE - 24 + 8 * k + s + 1))
                    act.copy(dst[:, s, :], raw[:, s, :]).then_inc(hi_ok, 1)

            def ex_split_hi(e1, chunks=range(HC)):
                for h in chunks:
                    act.wait_ge(etr, e1 * 8 + (h + 1))
                    act.copy(ex_hi[:, h, :], P[:, h % 2, 0:CAPR]).then_inc(exh, 1)

            act.wait_ge(lg_evac, 1)
            act.wait_ge(vb_mm, NT)
            row_sums()
            split_moe(0, 0, s0_hi)
            split_moe(0, 1, s1_hi)
            split_moe(0, 2, s2_hi)
            ex_split_hi(0)

            def swiglu(e):
                for m in range(FC):
                    act.wait_ge(pg_mm, e * FC + (m + 1))
                    if m >= 2:
                        act.wait_ge(gf_ok, e * FC + (m - 1))
                    act.activation(sg[:, m % 2, :], P[:, 4 + m % 2, 0:CAPR], ACT.Silu).then_inc(sg_ok, 1)
                    act.wait_ge(gf_ok, e * FC + (m + 1))
                    act.copy(g_hi[:, m, :], gf[:, m % 2, :]).then_inc(gh_ok, 1)

            def results(e):
                for u in range(0, 8, 2):
                    act.wait_ge(dn_mm, e * 8 + (u + 1))
                    act.wait_ge(eo_st[u % 4], e * 32 + 16 * (u // 4))
                    act.copy(eo[:, u % 4, :], P[0:CA, 6 + u % 2, :]).then_inc(eo_ok, 1)

            with act.Fori(0, NX - 1) as e:
                swiglu(e)
                for u in range(8):
                    ex_split_hi(e + 1, (u,))
                    a = 2 * (u % 4)
                    split_moe(e + 1, u // 4, (s0_hi, s1_hi)[u // 4], (a, a + 1))
                act.wait_ge(sg_ok, e * FC + FC)
                split_moe(e + 1, 2, s2_hi)
            swiglu(NX - 1)

        @block.gpsimd
        def _(pool):
            steps = Count(pool, pool_step)
            nc.gpsimd.memset(zero[:, :], 0.0).then_inc(const_ok, 1)
            steps.then(nc.gpsimd.memset(ident[:, :], 0.0))
            steps.then(nc.gpsimd.memset(ones[:, :], 1.0))
            nc.gpsimd.memset(onesb[:, :], 1.0).then_inc(const_ok, 1)
            nc.gpsimd.affine_select(out=ident[:, :], in_=ident[:, :], compare_op=ALU.not_equal, fill=1.0, base=0,
                                    pattern=[[-1, 128]], channel_multiplier=1).then_inc(const_ok, 1)
            nc.gpsimd.iota(iota[:, :], [[1, TT]], base=0, channel_multiplier=0,
                           allow_small_or_imprecise_dtypes=True).then_inc(const_ok, 1)
            nc.gpsimd.iota(iotap[:, :], [[1, 1]], base=0, channel_multiplier=1,
                           allow_small_or_imprecise_dtypes=True).then_inc(const_ok, 1)
            nc.gpsimd.iota(iotak[:, :], [[1, NCH]], base=0, channel_multiplier=0,
                           allow_small_or_imprecise_dtypes=True).then_inc(const_ok, 1)
            nc.gpsimd.affine_select(out=upper[:, :], in_=ones[0:NB, 0:NB], compare_op=ALU.is_ge, fill=0.0, base=0,
                                    pattern=[[1, NB]], channel_multiplier=-1).then_inc(const_ok, 1)
            nc.gpsimd.affine_select(out=lower[:, :], in_=ones[0:TT, 0:TT], compare_op=ALU.is_ge, fill=0.0, base=-1,
                                    pattern=[[-1, TT]], channel_multiplier=1).then_inc(const_ok, 1)
            o80 = ones[0:80, 0:80].rearrange("p (a b) -> p a b", a=8)
            steps.then(nc.gpsimd.affine_select(out=mask80[:, :, :], in_=o80, compare_op=ALU.is_ge, fill=0.0, base=0,
                                               pattern=[[-10, 8], [0, 10]], channel_multiplier=1))
            nc.gpsimd.affine_select(out=mask80[:, :, :], in_=mask80[:, :, :], compare_op=ALU.is_ge, fill=0.0, base=9,
                                    pattern=[[10, 8], [0, 10]], channel_multiplier=-1).then_inc(const_ok, 1)
            pool.wait_ge(const_ok, 1)
            pool.dma_start(tok_d.rearrange("(p n) o -> p (n o)", p=CA), zero[0:CA, 0:NX * 4].bitcast(I32)).then_inc(tok_zero, 16)
            rz = rec_d.rearrange("(p k) f -> p (k f)", p=128).rearrange("p (r n) -> p r n", r=4)
            for c in range(2):
                pool.dma_start(rz[:, 2 * c:2 * c + 2, :],
                               zero[:, None, 0:NCH].broadcast_to([128, 2, NCH])).then_inc(scat[c], 16)
            pool.wait_ge(gstep, 2)
            pool.dma_start(hist_d.rearrange("(a b) -> a b", a=NT), hist10[:, :]).then_inc(hist_st, 16)
            pool.wait_ge(hist_st, 16)
            pool.dma_start(hist[:, :], hist_d.rearrange("(p o) -> p o", o=1)).then_inc(hist_in, 16)
            for c in range(2):
                pool.wait_ge(scat[c], 16)
            with pool.Fori(0, NBLK // 2) as it:
                for c in range(2):
                    pool.wait_ge(rs_ok, it * 2 + (c + 1))
                    pool.wait_ge(pool_step, it * 2 + (steps.n + c))
                    nc.gpsimd.tensor_tensor(pw[:, :], ones[0:1, 0:1], ones[0:1, 0:1], ALU.add).then_inc(pool_step, 1)
                    for k in range(BC):
                        pool.indirect_dma_start(out=rec_d, out_offset=bass.IndirectOffsetOnAxis(ap=idx[:, c, k:k + 1], axis=0),
                                                in_=rs[:, c, k, :], in_offset=None, bounds_check=128 * NCH - 1,
                                                oob_is_err=True).then_inc(scat[c], 16)
            for c in range(2):
                pool.wait_ge(scat[c], 16 + 16 * BC * NBLK // 2)
            pool.dma_start(rl[:, :, :], rec_d.rearrange("(p k) f -> p k f", p=128)).then_inc(rl_in, 16)
            with pool.Fori(0, NT // 2) as it:
                for c in range(2):
                    pool.wait_ge(res_in[c], it * 32 + 32)
                    nc.gpsimd.tensor_tensor(xt2[:, c, :], xt2[:, c, :], at2[:, c, :], ALU.add).then_inc(res_ok, 1)
            pool.wait_ge(x2_ok, NT)
            nc.gpsimd.iota(io8[:, :], [[1, NX]], base=-NX, channel_multiplier=0,
                           allow_small_or_imprecise_dtypes=True).then_inc(const_ok, 1)
            nc.gpsimd.iota(io392[:, :], [[CAPR, NX]], base=0, channel_multiplier=0,
                           allow_small_or_imprecise_dtypes=True).then_inc(const_ok, 1)
            nc.gpsimd.iota(small["left"][:, :], [[-TT, NT]], base=T - 1, channel_multiplier=-1,
                           allow_small_or_imprecise_dtypes=True).then_inc(const_ok, 1)
            nc.gpsimd.iota(tok[:, :], [[TT, NT]], base=0, channel_multiplier=1).then_inc(const_ok, 1)
            nc.gpsimd.memset(lowx[:, :], 1.0).then_inc(const_ok, 1)
            pool.wait_ge(const_ok, 14)
            nc.gpsimd.affine_select(out=lowx[:, (RS - 1) * TT:], in_=lowx[:, (RS - 1) * TT:], compare_op=ALU.is_ge, fill=0.0, base=-1,
                                    pattern=[[-1, TT]], channel_multiplier=1).then_inc(const_ok, 1)
            pool.wait_ge(tok_zero, 16)
            pool.wait_ge(const_ok, 13)
            pool.wait_ge(sidx_ok, 1)
            for i in range(NT):
                for k in range(2):
                    pool.indirect_dma_start(out=tok_d, out_offset=bass.IndirectOffsetOnAxis(ap=sidx[:, k, i:i + 1], axis=0),
                                            in_=tok[:, i:i + 1], in_offset=None, bounds_check=NX * CAPR - 1,
                                            oob_is_err=False).then_inc(tok_st, 16)
            pool.wait_ge(tok_st, 16 * 2 * NT)
            pool.dma_start(places_tok[:, :, :], tok_v).then_inc(tok_in, 16)

            def gather_rows():
                for a in range(4):
                    pool.indirect_dma_start(out=rows[:, a, :], out_offset=None, in_=h2_d,
                                            in_offset=bass.IndirectOffsetOnAxis(ap=rowi[:, a:a + 1], axis=0),
                                            bounds_check=T - 1, oob_is_err=True).then_inc(rows_in, 16)

            for c in range(2):
                pool.wait_ge(x2_st[c], 16 * NT)
            pool.wait_ge(rowi_ok, 1)
            gather_rows()
            with pool.Fori(0, NX - 1) as e:
                pool.wait_ge(rowi_ok, e + 2)
                pool.wait_ge(etr, e * 8 + 8)
                pool.wait_ge(pool_step, e + (steps.n + NBLK))
                nc.gpsimd.tensor_tensor(pw[:, :], ones[0:1, 0:1], ones[0:1, 0:1], ALU.add).then_inc(pool_step, 1)
                gather_rows()
            pool.wait_ge(dn_mm, NX * 8)
            for c in range(4):
                pool.wait_ge(eo_st[c], 16 * 2 * NX)
            for i in range(NT):
                for k, dst in ((0, r1t), (1, r2t)):
                    pool.indirect_dma_start(out=dst[:, i, :], out_offset=None, in_=eo_d,
                                            in_offset=bass.IndirectOffsetOnAxis(ap=gidx[:, k, i:i + 1], axis=0),
                                            bounds_check=NX * CAPR - 1, oob_is_err=True).then_inc(g1_in[i], 16)

        @block.vector
        def _(dve):
            v = nc.vector
            steps = Count(dve, dve_step)

            def floor_div(dst, src, by, add=0.0):
                steps.then(v.tensor_scalar(dst, src, 1.0 / by, add / by - 0.498, ALU.mult, ALU.add))
                steps.then(v.tensor_scalar(dst, dst, MAGIC, MAGIC, ALU.add, ALU.subtract))

            dve.wait_ge(edges_in, 48)
            for a in range(2):
                floor_div(tn[:, a, :], en[:, a, :], TT)
            v.scalar_tensor_tensor(out=bkt[:, :], in0=tn[:, 1, :], scalar=float(NT), in1=tn[:, 0, :],
                                   op0=ALU.mult, op1=ALU.add).then_inc(bkt_ok, 1)
            for a in range(2):
                floor_div(tc[:, a, :], ec[:, a, :], TT)
                v.scalar_tensor_tensor(out=rec[:, :, a], in0=tc[:, a, :], scalar=-float(TT), in1=ec[:, a, :],
                                       op0=ALU.mult, op1=ALU.add)
            v.tensor_copy(rec[:, :, 2], wc[:, :])
            v.memset(rec[:, :, 3:4], 1.0)
            dve.wait_ge(const_ok, 9)
            for a, oh in ((0, oh_s), (1, oh_d)):
                v.tensor_tensor(oh[:, :, :], iota[0:TT, None, 0:NT].broadcast_to([TT, EC, NT]),
                                tc[:, a, :, None].broadcast_to([TT, EC, NT]), ALU.is_equal).then_inc(ohb_ok, 1)

            def split_lo(g, hi, lo, slots=range(8)):
                for s in slots:
                    dve.wait_ge(hi_ok, g * 8 + (s + 1))
                    v.tensor_tensor(lo[:, s, :], raw[:, s, :], hi[:, s, :].bitcast(F32), ALU.subtract).then_inc(lo_ok, 1)

            def moments(st, src, var):
                for h in range(2):
                    ins = v.bn_stats(stats[:, h, :], src[:, h * SC:(h + 1) * SC])
                st.then(ins)
                v.memset(rstd[:, 0:1], 0.0)
                st.then(v.bn_aggr(mv[:, :], stats[:, :, :]))
                v.tensor_scalar(rstd[:, 1:2], mv[:, 1:2], LNEPS, None, ALU.add).then_inc(var, 1)

            def scaled(st, src, dst, std, n):
                dve.wait_ge(std, n)
                st.then(v.reciprocal(rstd[:, 0:1], rstd[:, 0:1]))
                return v.tensor_scalar(dst, src, mv[:, 0:1], rstd[:, 0:1], ALU.subtract, ALU.mult)

            def norm_lo(c, i):
                dve.wait_ge(hi_x, i + 1)
                sl = bass.ds(i * TT, TT)
                v.tensor_tensor(xt_lo[:, :, sl].rearrange("p (b h) t -> p b h t", b=2),
                                P[:, 2 * c:2 * c + 2, 0:500].rearrange("p b (h t) -> p b h t", h=4),
                                xt_hi[:, :, sl].bitcast(F32).rearrange("p (b h) t -> p b h t", b=2),
                                ALU.subtract).then_inc(lo_x, 1)

            def norm_tile(st, c, i, arrived):
                dve.wait_ge(x_in[c], arrived)
                moments(st, xin[:, c, :], var_ok)
                scaled(st, xin[:, c, :], xin[:, c, :], std_ok, i + 1).then_inc(xn_ok, 1)
                norm_lo(1 - c, i - 1)

            dve.wait_ge(x_in[0], 16)
            moments(steps, xin[:, 0, :], var_ok)
            scaled(steps, xin[:, 0, :], xin[:, 0, :], std_ok, 1).then_inc(xn_ok, 1)
            dve.wait_ge(graph_mm, 1)
            steps.then(v.tensor_tensor(hq[:, :, :], P[0:80, 7, 0:80].rearrange("p (a b) -> p a b", a=8), mask80[:, :, :], ALU.mult))
            v.tensor_reduce(sel80[:, :], ident[0:80, 0:80].rearrange("p (a b) -> p b a", a=8), X, ALU.add)
            v.tensor_reduce(hs[:, :], hq[:, :, :].rearrange("p a b -> p b a"), X, ALU.add).then_inc(gstep, 1)
            dve.wait_ge(graph_mm, 2)
            v.tensor_copy(hist10[:, :], P[0:NT, 7, 128:128 + NT]).then_inc(gstep, 1)
            with dve.Fori(0, NT // 2 - 1) as it, steps.loop(it, NT // 2 - 1, 6) as st:
                for k in range(1, 3):
                    norm_tile(st, k % 2, it * 2 + k, it * 16 + 16 * (k // 2 + 1))
            norm_tile(steps, 1, NT - 1, 16 * (NT // 2))
            norm_lo(1, NT - 1)
            dve.wait_ge(hist_in, 16)
            floor_div(nch[:, 0:1], hist[:, :], CHUNK, CHUNK - 1.0)
            v.tensor_copy(nch[:, 1:2], nch[:, 0:1]).then_inc(gstep, 1)
            split_lo(0, s0_hi, s0_lo, range(0, 4))
            dve.wait_ge(graph_mm, 3)
            steps.then(v.tensor_copy(incl[:, :], P[0:NB, 7, 160:161]))
            v.tensor_scalar(ge[:, :], iotak[:, :], incl[:, 0:1], None, ALU.is_ge).then_inc(gstep, 1)
            split_lo(0, s0_hi, s0_lo, range(4, 8))
            steps.then(v.tensor_tensor(base1[:, :], incl[:, :], nch[:, 0:1], ALU.subtract))
            steps.then(v.tensor_scalar(base1[:, :], base1[:, :], float(CHUNK), -1.0, ALU.mult, ALU.add))
            dve.wait_ge(graph_mm, 4)
            v.tensor_scalar(offs[:, :], P[0:1, 6, 0:NCH], float(NB - 1), float(BW), ALU.min, ALU.mult).then_inc(gstep, 1)
            v.memset(carry[:, :], 0.0).then_inc(br_free, 2)
            dve.wait_ge(bkt_st, 16)
            v.memset(vt[:, :, :, 128:129], 1.0).then_inc(at_evac, 1)
            v.memset(kvblk[:, :, :], 0.0).then_inc(bias_free, 1)
            v.memset(zt[:, :, :, :], 0.0).then_inc(gstep, 1)

            def places(cg, b, st):
                dve.wait_ge(br_in[b % 2], cg * (8 * BPG) + 16 * (b // 2 + 1))
                v.tensor_scalar(oht[:, :], br[:, b % 2, :], iotap[0:NB, 0:1], None, ALU.is_equal).then_inc(br_free, 1)
                dve.wait_ge(br_free, cg * BPG + (b + 3))
                dve.wait_ge(graph_mm, cg * BPG + (GM0 + b))
                st.then(v.tensor_tensor_scan(sm[:, :], oht[:, :], oht[:, :], carry[:, 0:1], ALU.add, ALU.max))
                st.then(v.tensor_copy(carry[:, :], sm[:, EB - 1:EB]))
                v.scalar_tensor_tensor(out=sm[:, :], in0=sm[:, :], scalar=base1[:, 0:1], in1=oht[:, :],
                                       op0=ALU.add, op1=ALU.mult).then_inc(sm_ok, 1)

            def records(cg, b, st):
                c = b % 2
                dve.wait_ge(graph_mm, cg * BPG + (GM0 + b + 1))
                pos = P[0:TT, 7, 256:256 + BC]
                st.then(v.tensor_scalar(pk[:, 0, :], pos, 1.0 / CHUNK, -0.498, ALU.mult, ALU.add))
                st.then(v.tensor_scalar(pk[:, 0, :], pk[:, 0, :], MAGIC, MAGIC, ALU.add, ALU.subtract))
                st.then(v.scalar_tensor_tensor(out=pk[:, 1, :], in0=pk[:, 0, :], scalar=-float(CHUNK), in1=pos,
                                               op0=ALU.mult, op1=ALU.add))
                dve.wait_ge(scat[c], cg * (8 * BPG * BC) + (16 + 16 * BC * (b // 2)))
                st.then(v.scalar_tensor_tensor(out=idx[:, c, :], in0=pk[:, 1, :], scalar=float(NCH), in1=pk[:, 0, :],
                                               op0=ALU.mult, op1=ALU.add))
                v.tensor_copy(rs[:, c, :, :], rec[:, bass.ds(cg * (BPG * BC) + b * BC, BC), :]).then_inc(rs_ok, 1)

            def attention(cg, j, st):
                for gg in range(5):
                    u = 5 * j + gg
                    dve.wait_ge(at_mm, cg * 20 + (u + 1))
                    pv = P[0:TT, 4 + u % 2, 0:2 * AW].rearrange("p (t c) -> p t c", t=2)
                    z = zt[:, u % 2, :, :]
                    st.then(v.tensor_scalar(z, pv[:, :, 128:130], 1e-6, None, ALU.add))
                    st.then(v.reciprocal(z, z))
                    if gg == 0 and j >= 2:
                        dve.wait_ge(sa_st[j % 2], cg * 32 + 16)
                    for t in range(2):
                        ins = v.tensor_tensor(sa[:, j % 2, 2 * gg + t, :].rearrange("p (h m) -> p h m", h=2),
                                              pv[:, t, 0:128].rearrange("p (h m) -> p h m", h=2),
                                              z[:, t, :, None].broadcast_to([TT, 2, 64]), ALU.mult)
                    ins.then_inc(at_evac, 1)

            with dve.Fori(0, HG) as cg, steps.loop(cg, HG, 2 * BPG + 4 * BPG + 2 * 20) as st:
                dve.wait_ge(bias_in, cg * 48 + 48)
                for i in range(NT):
                    dve.wait_ge(proj, cg * UNITS + (i + 1))
                    if i >= 2:
                        dve.wait_ge(phik_ok, cg * NT + (i - 1))
                    v.tensor_tensor(t_b[0:TT, i % 2, :], P[0:TT, i % 4, :], bkv[:, 0, :], ALU.add).then_inc(kv_evac, 1)
                    if i >= 1:
                        dve.wait_ge(er, cg * NT + i)
                        v.scalar_tensor_tensor(out=phik[:, i - 1, :], in0=e_b[0:TT, (i - 1) % 2, :], scalar=1.0,
                                               in1=t_b[0:TT, (i - 1) % 2, :], op0=ALU.min, op1=ALU.add).then_inc(phik_ok, 1)
                    if i == NT - 2:
                        split_lo(cg * 3 + 1, s0_hi, s0_lo)
                for i in range(NT):
                    dve.wait_ge(proj, cg * UNITS + (NT + i + 1))
                    if i >= 2:
                        dve.wait_ge(kv_mm, cg * NT + (i - 1))
                    v.tensor_tensor(vt[:, i % 2, :, 0:128], P[0:TT, (NT + i) % 4, :].rearrange("p (j c) -> p j c", j=PAIRS),
                                    bkv[:, 1, :].rearrange("p (j c) -> p j c", j=PAIRS), ALU.add).then_inc(kv_evac, 1)
                    if i == 0:
                        dve.wait_ge(er, cg * NT + NT)
                        v.scalar_tensor_tensor(out=phik[:, NT - 1, :], in0=e_b[0:TT, (NT - 1) % 2, :], scalar=1.0,
                                               in1=t_b[0:TT, (NT - 1) % 2, :], op0=ALU.min, op1=ALU.add).then_inc(phik_ok, 1)
                    if i >= 1:
                        if i >= 2:
                            records(cg, i - 2, st)
                        places(cg, i - 1, st)
                    if i == NT - 2:
                        split_lo(cg * 3 + 2, s0_hi, s0_lo)
                dve.wait_ge(kv_mm, cg * NT + NT)
                for h in range(2):
                    for a in range(2):
                        r = slice(64 * a, 64 * a + 64)
                        src = P[r, 4 + h, 0:2 * KVW].rearrange("p (j c) -> p j c", j=2)
                        v.tensor_copy(kvblk[r, 2 * h:2 * h + 2, 64 * a:64 * a + 64], src[:, :, 64 * a:64 * a + 64]).then_inc(kvblk_ok, 1)
                        v.tensor_copy(kvblk[r, 2 * h:2 * h + 2, 128 + a:129 + a], src[:, :, 128:129]).then_inc(kvblk_ok, 1)
                for q in range(3 * PAIRS):
                    j, a = q // 3, QCUT[q % 3]
                    n = QCUT[q % 3 + 1] - a
                    if q == 3 * PAIRS - 1:
                        split_lo(cg * 3 + 3, s0_hi, s0_lo, range(0, 4))
                    dve.wait_ge(q_evac, cg * 12 + (q + 1))
                    if q % 3 == 0 and j >= 2:
                        dve.wait_ge(at_mm, cg * 20 + 5 * (j - 1))
                    ins = v.scalar_tensor_tensor(out=phiq[:, j % 2, a:a + n], in0=e_b[:, q % 2, 0:n], scalar=1.0,
                                                 in1=t_b[:, q % 2, 0:n], op0=ALU.min, op1=ALU.add)
                    ins.then_inc(phiq_ok, 1)
                    if q % 3 == 0 and j >= 1:
                        attention(cg, j - 1, st)
                    records(cg, q + 8, st)
                    if q + 9 < BPG:
                        places(cg, q + 9, st)
                attention(cg, PAIRS - 1, st)
                split_lo(cg * 3 + 3, s0_hi, s0_lo, range(4, 8))
                for c in range(2):
                    dve.wait_ge(sa_st[c], cg * 32 + 32)
                v.memset(mv[:, :], 0.0).then_inc(bias_free, 1)

            step = NB * BW // 4
            for k in range(4):
                v.memset(adj[:, k * step:(k + 1) * step], 0.0)
            v.memset(rstd[:, 0:1], 0.0).then_inc(adj_sum, 2 * CG)
            dve.wait_ge(rl_in, 16)

            def one_hots(p, n, k):
                a, oh, done = ((1, ohd, ohd_ok), (0, ohs, ohs_ok))[k // 2]
                h = k % 2
                v.tensor_tensor(oh[:, p, 2 * h:2 * h + 2, 0:TT], iota[:, None, :].broadcast_to([128, 2, TT]),
                                rl[:, bass.ds(n * CG + 2 * h, 2), a:a + 1].broadcast_to([128, 2, TT]), ALU.is_equal).then_inc(done, 1)

            off_regs = [dve.alloc_register(f"off{k}") for k in range(2 * CG)]

            def offsets(n):
                dve.reg_load(off_regs, offs[0:1, bass.ds(n * CG, 2 * CG)])
                return [nc.snap(r, min_val=0, max_val=(NB - 1) * BW) for r in off_regs]

            def add_blocks(p, n, at_, more=True):
                dve.wait_ge(ch_mm, n + 1)
                for c in range(CG):
                    blk = adj[:, bass.ds(at_[CG * p + c], BW)]
                    dve.wait_ge(adj_sum, n * CG + (2 * CG + c))
                    v.tensor_tensor(blk, blk, P[0:TT, 4 + 2 * p + c // 2, (c % 2) * BW:(c % 2 + 1) * BW], ALU.add).then_inc(adj_sum, 1)
                    if more:
                        one_hots(p, n + 2, c)

            for p in range(2):
                for k in range(4):
                    one_hots(p, p, k)
            for k in range(2 * NT - GT0):
                if k + GT0 == NT:
                    split_lo(7, s0_hi, s0_lo)
                with dve.Fori(0, GL) as it:
                    at_ = offsets(it * 2 + 2 * GL * k)
                    for p in range(2):
                        add_blocks(p, it * 2 + (2 * GL * k + p), at_)
            at_ = offsets(NGR - 2)
            for p in range(2):
                add_blocks(p, NGR - 2 + p, at_, more=False)
            dve.wait_ge(adj_sum, NCH + 2 * CG)
            a4 = adj[:, :].rearrange("p (d s c) -> p d s c", d=NT, s=NT)
            v.tensor_reduce(nrm[:, 0, :], a4[:, :, :, TT].rearrange("p d s -> p s d"), X, ALU.add)
            v.tensor_reduce(nrm[:, 1, :], a4[:, :, :, TT + 1].rearrange("p d s -> p s d"), X, ALU.add)
            v.tensor_reduce(nrm[:, 2, :], a4[:, :, :, TT + 2], X, ALU.add)
            steps.then(v.tensor_reduce(nrm[:, 3, :], a4[:, :, :, TT + 3], X, ALU.add))
            for k in range(4):
                ins = v.tensor_scalar(nrm[:, k, :], nrm[:, k, :], 1.0 if k % 2 else 1e-30, None, ALU.max)
            ins.then_inc(nrm_ok, 1)

            def adj_lo(i, h, k):
                dve.wait_ge(wh_ok, k)
                v.tensor_tensor(w_lo[:, 5 * h:5 * h + 5, :],
                                adj[:, bass.ds(i * (NT * BW) + h * (5 * BW), 5 * BW)].rearrange("p (j c) -> p j c", c=BW)[:, :, 0:TT],
                                w_hi[:, 5 * h:5 * h + 5, :].bitcast(F32), ALU.subtract).then_inc(wl_ok, 1)

            for h in range(2):
                adj_lo(0, h, h + 1)
            dve.wait_ge(nrm_sq, 1)
            for k in range(2):
                steps.then(v.tensor_tensor(nsc[:, k, :], nrm[:, 2 * k, :], nrm[:, 2 * k + 1, :], ALU.mult))
            v.reciprocal(nsc[:, :, :], nsc[:, :, :]).then_inc(nsc_ok, 1)
            dve.wait_ge(nsc_ok, 1)
            for j in range(NT):
                dve.wait_ge(yh_ok, j + 1)
                v.scalar_tensor_tensor(out=y_lo[:, j, :], in0=yraw[:, j % 4, :], scalar=nsc[:, 0, j:j + 1],
                                       in1=y_hi[:, j, :].bitcast(F32), op0=ALU.mult, op1=ALU.subtract).then_inc(yl_ok, 1)

            def adj_hi_dve(i, h, k):
                dve.wait_ge(wh_free, k)
                v.tensor_copy(w_hi[:, 5 * h:5 * h + 5, :],
                              adj[:, bass.ds(i * (NT * BW) + h * (5 * BW), 5 * BW)].rearrange("p (j c) -> p j c", c=BW)[:, :, 0:TT]).then_inc(wh_ok, 1)

            dve.wait_ge(bg_in, 16)

            def residual(i, c, n_res, st):
                dve.wait_ge(agg_mm, n_res)
                st.then(v.scalar_tensor_tensor(out=gt2[:, c, :], in0=P[0:TT, 2 * c:2 * c + 2, :].rearrange("p b n -> p (b n)"),
                                               scalar=nsc[:, 1, bass.ds(i, 1)], in1=bgb[:, :], op0=ALU.mult, op1=ALU.add))
                dve.wait_ge(res_ok, n_res)
                v.scalar_tensor_tensor(out=xt2[:, c, :], in0=gt2[:, c, :], scalar=0.0, in1=xt2[:, c, :],
                                       op0=ALU.max, op1=ALU.add).then_inc(x2_ok, 1)
                dve.wait_ge(x2_ok, n_res)
                moments(st, xt2[:, c, :], var2)
                scaled(st, xt2[:, c, :], at2[:, c, :], std2, n_res).then_inc(h2_ok, 1)

            with dve.Fori(0, NT // 2 - 1) as it, steps.loop(it, NT // 2 - 1, 8) as st:
                for c in range(2):
                    for h in range(2):
                        adj_hi_dve(it * 2 + (c + 1), h, it * 4 + (2 * c + h + 1))
                        adj_lo(it * 2 + (c + 1), h, it * 4 + (2 * c + h + 3))
                    residual(it * 2 + c, c, it * 2 + (c + 1), st)
            for h in range(2):
                adj_hi_dve(NT - 1, h, 2 * (NT - 2) + h + 1)
                adj_lo(NT - 1, h, 2 * (NT - 1) + h + 1)
            for c in range(2):
                residual(NT - 2 + c, c, NT - 1 + c, steps)

            s = small
            dve.wait_ge(lg_mm, NT)
            v.tensor_copy(s["lg"][:, :, :], P[0:TT, 6, 0:NT * NX].rearrange("p (i e) -> p i e", e=NX)).then_inc(lg_evac, 1)
            dve.wait_ge(lg_evac, 1)

            def per_token(a):
                return a[:, :, None].broadcast_to([TT, NT, NX])

            def per_expert(a):
                return a[:, None, :].broadcast_to([TT, NT, NX])

            steps.then(v.tensor_reduce(s["m1"][:, :], s["lg"][:, :, :], X, ALU.max))
            v.tensor_tensor(s["pr"][:, :, :], s["lg"][:, :, :], per_token(s["m1"]), ALU.subtract).then_inc(dmax_ok, 1)
            dve.wait_ge(exp_ok, 1)
            steps.then(v.tensor_reduce(s["den"][:, :], s["pr"][:, :, :], X, ALU.add))
            steps.then(v.reciprocal(s["den"][:, :], s["den"][:, :]))
            steps.then(v.tensor_tensor(s["pr"][:, :, :], s["pr"][:, :, :], per_token(s["den"]), ALU.mult))
            dve.wait_ge(const_ok, 12)
            for m, oh in (("m1", "ohe1"), ("m2", "ohe2")):
                steps.then(v.tensor_reduce(s[m][:, :], s["pr"][:, :, :], X, ALU.max))
                steps.then(v.tensor_tensor(s["cand"][:, :, :], s["pr"][:, :, :], per_token(s[m]), ALU.is_equal))
                steps.then(v.tensor_tensor(s["cand"][:, :, :], s["cand"][:, :, :], per_expert(io8), ALU.mult))
                steps.then(v.tensor_reduce(s["cm"][:, :], s["cand"][:, :, :], X, ALU.min))
                steps.then(v.tensor_tensor(s[oh][:, :, :], per_expert(io8), per_token(s["cm"]), ALU.is_equal))
                if m == "m1":
                    steps.then(v.scalar_tensor_tensor(out=s["pr"][:, :, :], in0=s[oh][:, :, :], scalar=-2.0, in1=s["pr"][:, :, :],
                                                      op0=ALU.mult, op1=ALU.add))
            steps.then(v.tensor_tensor(s["den"][:, :], s["m1"][:, :], s["m2"][:, :], ALU.add))
            steps.then(v.tensor_scalar(s["den"][:, :], s["den"][:, :], EPS, None, ALU.max))
            steps.then(v.reciprocal(s["den"][:, :], s["den"][:, :]))
            v.tensor_tensor(s["wk1"][:, :], s["m1"][:, :], s["den"][:, :], ALU.mult)
            steps.then(v.tensor_tensor(s["wk2"][:, :], s["m2"][:, :], s["den"][:, :], ALU.mult))
            steps.then(v.scalar_tensor_tensor(out=s["v"][:, :, :], in0=s["ohe1"][:, :, :], scalar=-1.0, in1=s["ohe2"][:, :, :],
                                              op0=ALU.add, op1=ALU.add))
            for w, oh in (("wk1", "ohe1"), ("wk2", "ohe2")):
                steps.then(v.tensor_tensor(s["cand"][:, :, :], s[oh][:, :, :], per_token(s[w]), ALU.mult))
                steps.then(v.tensor_tensor(s["v"][:, :, :], s["v"][:, :, :], s["cand"][:, :, :], ALU.add))
            for c in range(2):
                dve.wait_ge(x2_st[c], 16 * NT)
            for i in range(NT):
                if i >= 2:
                    dve.wait_ge(vb_mm, i - 1)
                v.tensor_tensor(diag[:, i % 2, :, :], ident[0:TT, None, 0:TT].broadcast_to([TT, NX, TT]),
                                s["v"][:, i, :, None].broadcast_to([TT, NX, TT]), ALU.mult).then_inc(diag_ok, 1)
            dve.wait_ge(vb_ok, NT)
            dve.wait_ge(const_ok, 15)
            v.memset(s["cand"][:, :, :], 0.0).then_inc(row_sum, 2)
            with dve.Fori(0, NX // 2) as it:
                for c in range(2):
                    e = it * 2 + c
                    dve.wait_ge(row_sum, e + 1)
                    at_ = 0
                    for i in range(NT):
                        vi = s["v"][:, i, bass.ds(e, 1)]
                        if i < RS:
                            v.scalar_tensor_tensor(out=cmpm[:, c, at_:at_ + (i + 1) * TT],
                                                   in0=vb[:, bass.ds(e, 1), 0:(i + 1) * TT].rearrange("p a t -> p (a t)"),
                                                   scalar=vi, in1=lowx[:, (RS - 1 - i) * TT:], op0=ALU.is_ge, op1=ALU.mult,
                                                   accum_out=s["rank"][:, i, bass.ds(e, 1)]).then_inc(cmp_ok, 1)
                            at_ += (i + 1) * TT
                            continue
                        if i:
                            v.tensor_scalar(cmpm[:, c, at_:at_ + i * TT], vb[:, bass.ds(e, 1), 0:i * TT].rearrange("p a t -> p (a t)"),
                                            vi, None, ALU.is_ge)
                        v.scalar_tensor_tensor(out=cmpm[:, c, at_ + i * TT:at_ + (i + 1) * TT],
                                               in0=vb[:, bass.ds(e, 1), i * TT:(i + 1) * TT].rearrange("p a t -> p (a t)"),
                                               scalar=vi, in1=lower[:, :], op0=ALU.is_ge, op1=ALU.mult).then_inc(cmp_ok, 1)
                        at_ += (i + 1) * TT
            dve.wait_ge(row_sum, NX + 2)
            dve.wait_ge(cs_mm, NX)
            steps.then(v.tensor_tensor(s["rank"][:, :, :], s["rank"][:, :, :],
                                       P[0:TT, 6, 0:NT * NX].rearrange("p (i e) -> p i e", e=NX), ALU.subtract))
            steps.then(v.tensor_tensor(s["rank"][:, :, :], s["rank"][:, :, :], per_token(s["left"]), ALU.add))
            v.tensor_scalar(s["keep"][:, :, :], s["rank"][:, :, :], float(CAP), None, ALU.is_lt)
            steps.then(v.tensor_scalar(s["rank"][:, :, :], s["rank"][:, :, :], float(CAP), None, ALU.min))
            steps.then(v.tensor_tensor(s["rank"][:, :, :], s["rank"][:, :, :], per_expert(io392), ALU.add))
            for k, (oh, sl, kp) in enumerate((("ohe1", "sl1", "kp1"), ("ohe2", "sl2", "kp2"))):
                steps.then(v.tensor_tensor(s["cand"][:, :, :], s[oh][:, :, :], s["rank"][:, :, :], ALU.mult))
                steps.then(v.tensor_reduce(s[sl][:, :], s["cand"][:, :, :], X, ALU.add))
                steps.then(v.tensor_tensor(s["cand"][:, :, :], s[oh][:, :, :], s["keep"][:, :, :], ALU.mult))
                steps.then(v.tensor_reduce(s[kp][:, :], s["cand"][:, :, :], X, ALU.add))
                steps.then(v.tensor_copy(gidx[:, k, :], s[sl][:, :]))
                steps.then(v.tensor_scalar(s["cm"][:, :], s[kp][:, :], -100000.0, 100000.0, ALU.mult, ALU.add))
                ins = v.tensor_tensor(sidx[:, k, :], s[sl][:, :], s["cm"][:, :], ALU.add)
                if k == 0:
                    steps.then(ins)
            ins.then_inc(sidx_ok, 1)
            v.tensor_tensor(s["wk1"][:, :], s["wk1"][:, :], s["kp1"][:, :], ALU.mult)
            steps.then(v.tensor_tensor(s["wk2"][:, :], s["wk2"][:, :], s["kp2"][:, :], ALU.mult))
            steps.then(v.tensor_tensor(s["den"][:, :], s["wk1"][:, :], s["wk2"][:, :], ALU.add))
            steps.then(v.tensor_scalar(s["den"][:, :], s["den"][:, :], EPS, None, ALU.max))
            steps.then(v.reciprocal(s["den"][:, :], s["den"][:, :]))
            v.tensor_tensor(s["wk1"][:, :], s["wk1"][:, :], s["den"][:, :], ALU.mult)
            steps.then(v.tensor_tensor(s["wk2"][:, :], s["wk2"][:, :], s["den"][:, :], ALU.mult))

            def ex_split_lo(e1, chunks=range(HC)):
                for h in chunks:
                    dve.wait_ge(exh, e1 * 8 + (h + 1))
                    v.tensor_tensor(ex_lo[:, h, :], P[:, h % 2, 0:CAPR], ex_hi[:, h, :].bitcast(F32), ALU.subtract).then_inc(exl, 1)

            def moe_lo(e, k, hi, lo, slots=range(8)):
                for q in slots:
                    dve.wait_ge(hi_ok, e * 24 + (MOE + 8 * k + q + 1))
                    v.tensor_tensor(lo[:, q, :], raw[:, q, :], hi[:, q, :].bitcast(F32), ALU.subtract).then_inc(lo_ok, 1)

            def swiglu(e, st):
                for m in range(FC):
                    dve.wait_ge(sg_ok, e * FC + (m + 1))
                    v.tensor_tensor(gf[:, m % 2, :], sg[:, m % 2, :], P[:, 2 + m % 2, 0:CAPR], ALU.mult).then_inc(gf_ok, 1)
                    dve.wait_ge(gh_ok, e * FC + (m + 1))
                    v.tensor_tensor(g_lo[:, m, :], gf[:, m % 2, :], g_hi[:, m, :].bitcast(F32), ALU.subtract).then_inc(gl_ok, 1)

            def result(e, u):
                dve.wait_ge(dn_mm, e * 8 + (u + 1))
                if u >= 4:
                    dve.wait_ge(eo_st[u % 4], e * 32 + 16)
                v.tensor_copy(eo[:, u % 4, :], P[0:CA, 6 + u % 2, :]).then_inc(eo_ok, 1)

            def results_stored(e):
                for c in range(4):
                    dve.wait_ge(eo_st[c], e * 32 + 32)

            moe_lo(0, 0, s0_hi, s0_lo)
            moe_lo(0, 1, s1_hi, s1_lo)
            moe_lo(0, 2, s2_hi, s2_lo)
            dve.wait_ge(tok_in, 16)
            v.tensor_copy(rowi[:, :], places_tok[:, 0, :]).then_inc(rowi_ok, 1)
            ex_split_lo(0)
            with dve.Fori(0, NX - 1) as e:
                v.tensor_copy(rowi[:, None, :], places_tok[:, bass.ds(e + 1, 1), :]).then_inc(rowi_ok, 1)
                swiglu(e, None)
                for u in range(9):
                    if u < 8:
                        ex_split_lo(e + 1, (u,))
                        hi, lo = ((s0_hi, s0_lo), (s1_hi, s1_lo))[u // 4]
                        moe_lo(e + 1, u // 4, hi, lo, (2 * (u % 4), 2 * (u % 4) + 1))
                    if u >= 1:
                        result(e, u - 1)
                results_stored(e)
                moe_lo(e + 1, 2, s2_hi, s2_lo)
            swiglu(NX - 1, None)
            for u in range(8):
                result(NX - 1, u)
            results_stored(NX - 1)
            dve.wait_ge(x2_in, 16 * NT)
            for i in range(NT):
                dve.wait_ge(g1_in[i], 32)
                steps.then(v.scalar_tensor_tensor(out=x2t[:, i, :], in0=r1t[:, i, :], scalar=s["wk1"][:, i:i + 1], in1=x2t[:, i, :],
                                                  op0=ALU.mult, op1=ALU.add))
                v.scalar_tensor_tensor(out=x2t[:, i, :], in0=r2t[:, i, :], scalar=s["wk2"][:, i:i + 1], in1=x2t[:, i, :],
                                       op0=ALU.mult, op1=ALU.add).then_inc(o_ok, 1)

        @block.tensor
        def _(pe):
            mm = nc.tensor.matmul

            def three(out, lh, ll, rh, rl_, first, last):
                mm(out, lh, rh, start=first, stop=False)
                mm(out, lh, rl_, start=False, stop=False)
                return mm(out, ll, rh, start=False, stop=last)

            pe.wait_ge(const_ok, 9)
            def norm_transposes(c, i):
                pe.wait_ge(xn_ok, i + 1)
                for h in range(HC):
                    ins = nc.tensor.transpose(P[:, 2 * c + h // 4, (h % 4) * TT:(h % 4 + 1) * TT],
                                              xin[:, c, h * 128:(h + 1) * 128], ident[0:TT, 0:TT])
                ins.then_inc(tr_done, 1)

            pe.wait_ge(ohb_ok, 2)
            for k in range(EC // 8):
                ins = mm(P[0:80, 7, 0:80], oh_d[:, 8 * k:8 * k + 8, :].rearrange("p a b -> p (a b)"),
                         oh_s[:, 8 * k:8 * k + 8, :].rearrange("p a b -> p (a b)"), start=(k == 0), stop=(k == EC // 8 - 1))
            ins.then_inc(graph_mm, 1)
            norm_transposes(0, 0)
            pe.wait_ge(gstep, 1)
            mm(P[0:NT, 7, 128:128 + NT], sel80[:, :], hs[:, :], start=True, stop=True).then_inc(graph_mm, 1)
            norm_transposes(1, 1)
            with pe.Fori(0, NT // 2 - 1) as it:
                for c in range(2):
                    pe.wait_ge(lo_x, it * 2 + (c + 1))
                    norm_transposes(c, it * 2 + (c + 2))
            pe.wait_ge(lo_x, NT)
            pe.wait_ge(gstep, 3)
            mm(P[0:NB, 7, 160:161], upper[:, :], nch[:, 0:1], start=True, stop=True).then_inc(graph_mm, 1)
            pe.wait_ge(gstep, 4)
            mm(P[0:1, 6, 0:NCH], ones[0:NB, 0:1], ge[:, :], start=True, stop=True).then_inc(graph_mm, 1)
            pe.wait_ge(gstep, 6)

            def positions(cg, b):
                pe.wait_ge(sm_ok, cg * BPG + (b + 1))
                for c in range(BC):
                    ins = mm(P[0:TT, 7, 256 + c:257 + c], sm[:, c * TT:(c + 1) * TT], ones[0:NB, 0:1], start=True, stop=True)
                ins.then_inc(graph_mm, 1)

            def row_tile(out, i, g, first, last, between=None):
                for s in range(8):
                    if first:
                        pe.wait_ge(lo_ok, g * 8 + (s + 1))
                    ins = three(out, xt_hi[:, s, i * TT:(i + 1) * TT], xt_lo[:, s, i * TT:(i + 1) * TT],
                                s0_hi[:, s, :], s0_lo[:, s, :], s == 0, s == 7)
                    if last and s < 7:
                        ins.then_inc(w_used, 1)
                    if between:
                        between(s)
                return ins

            def kv_tile(cg, i):
                pe.wait_ge(kv_evac, cg * 20 + (NT + i + 1))
                pe.wait_ge(phik_ok, cg * NT + (i + 1))
                if i == 0:
                    pe.wait_ge(at_evac, cg * 20 + 1)
                for j in range(PAIRS):
                    ins = mm(P[:, 4 + j // 2, (j % 2) * KVW:(j % 2 + 1) * KVW], phik[:, i, j * 128:(j + 1) * 128],
                             vt[:, i % 2, j, :], start=(i == 0 and j % 2 == 0), stop=(i == NT - 1), skip_group_check=True)
                ins.then_inc(kv_mm, 1)

            def attend(cg, j):
                pe.wait_ge(phiq_ok, cg * 12 + 3 * (j + 1))
                if j == 0:
                    pe.wait_ge(kvblk_ok, cg * 8 + 8)
                for gg in range(5):
                    u = 5 * j + gg
                    if u >= 2:
                        pe.wait_ge(at_evac, cg * 20 + u)
                    for t in range(2):
                        i = 2 * gg + t
                        ins = mm(P[0:TT, 4 + u % 2, t * AW:(t + 1) * AW], phiq[:, j % 2, i * TT:(i + 1) * TT],
                                 kvblk[:, j, :], start=True, stop=True)
                    ins.then_inc(at_mm, 1)

            with pe.Fori(0, HG) as cg:
                for i in range(NT):
                    if i >= 4:
                        pe.wait_ge(kv_evac, cg * 20 + (i - 3))
                    ins = row_tile(P[0:TT, i % 4, :], i, cg * 3, i == 0, i == NT - 1)
                    ins.then_inc(proj, 1)
                    if i == NT - 1:
                        pe.wait_ge(proj, cg * UNITS + (i + 1))
                        pe.nop().then_inc(w_used, 1)
                for i in range(NT):
                    pe.wait_ge(kv_evac, cg * 20 + (NT + i - 3))
                    ins = row_tile(P[0:TT, (NT + i) % 4, :], i, cg * 3 + 1, i == 0, i == NT - 1)
                    ins.then_inc(proj, 1)
                    if i == NT - 1:
                        pe.wait_ge(proj, cg * UNITS + (NT + i + 1))
                        pe.nop().then_inc(w_used, 1)
                    if i >= 1:
                        kv_tile(cg, i - 1)
                    if i >= 2:
                        positions(cg, i - 2)
                kv_tile(cg, NT - 1)
                for q in range(3 * PAIRS):
                    j, a = q // 3, QCUT[q % 3]
                    n = QCUT[q % 3 + 1] - a
                    if q < 4:
                        pe.wait_ge(kv_evac, cg * 20 + (2 * NT - 3 + q))
                    else:
                        pe.wait_ge(q_evac, cg * 12 + (q - 3))
                    for s in range(8):
                        if q == 0:
                            pe.wait_ge(lo_ok, cg * 24 + (16 + s + 1))
                        ins = three(P[:, q % 4, 0:n], s0_hi[:, s, j * 128:(j + 1) * 128], s0_lo[:, s, j * 128:(j + 1) * 128],
                                    xt_hi[:, s, a:a + n], xt_lo[:, s, a:a + n], s == 0, s == 7)
                        if q == 3 * PAIRS - 1 and s < 7:
                            ins.then_inc(w_used, 1)
                    ins.then_inc(proj, 1)
                    if q == 3 * PAIRS - 1:
                        pe.wait_ge(proj, cg * UNITS + UNITS)
                        pe.nop().then_inc(w_used, 1)
                    positions(cg, q + 8)
                    if q % 3 == 0 and j >= 1:
                        attend(cg, j - 1)
                attend(cg, PAIRS - 1)
            def chunk_group(p, n):
                pe.wait_ge(adj_sum, n * CG + CG)
                for c in range(CG):
                    pe.wait_ge(ohs_ok, n * 2 + (1 + c // 2))
                    pe.wait_ge(mv_ok, n * CG + (c + 1))
                    b, a = 4 + 2 * p + c // 2, (c % 2) * BW
                    mm(P[0:TT, b, a:a + TT + 2], ohs[:, p, c, 0:TT], mvt[:, p, c, 0:TT + 2], start=True, stop=True)
                    ins = mm(P[0:TT, b, a + TT + 2:a + BW], ohd[:, p, c, 0:TT], mvt[:, p, c, TT:TT + 2], start=True, stop=True)
                ins.then_inc(ch_mm, 1)

            for n in range(2 * NT):
                g, i = n // NT, n % NT
                if n >= 4:
                    pe.wait_ge(g_evac, n - 3)
                def between(s, n=n):
                    if n >= GT0 and 1 <= s <= 2 * GL:
                        k = 2 * GL * (n - GT0) + s - 1
                        chunk_group(k % 2, k)
                ins = row_tile(P[0:TT, n % 4, :], i, 6 + g, i == 0, i == NT - 1, between)
                ins.then_inc(proj, 1)
                if i == NT - 1:
                    pe.wait_ge(proj, HG * UNITS + n + 1)
                    pe.nop().then_inc(w_used, 1)
            for p in range(2):
                chunk_group(p, NGR - 2 + p)
            def aggregate(c, i):
                for j in range(NT):
                    pe.wait_ge(yl_ok, j + 1)
                    if j % 5 == 0:
                        pe.wait_ge(wl_ok, i * 2 + (j // 5 + 1))
                    for h in range(2):
                        ins = three(P[0:TT, 2 * c + h, :], w_hi[:, j, :], w_lo[:, j, :], y_hi[:, j, h * SC:(h + 1) * SC],
                                    y_lo[:, j, h * SC:(h + 1) * SC], j == 0, j == NT - 1)
                    if j == 4:
                        ins.then_inc(wh_free, 1)
                ins.then_inc(agg_mm, 1)
                pe.wait_ge(agg_mm, i + 1)
                pe.nop().then_inc(wh_free, 1)

            def h2_transposes(c, i):
                pe.wait_ge(h2_ok, i + 1)
                for h in range(HC):
                    ins = nc.tensor.transpose(P[:, 4 + h // 4, (h % 4) * TT:(h % 4 + 1) * TT],
                                              at2[:, c, h * 128:(h + 1) * 128], ident[0:TT, 0:TT])
                ins.then_inc(tr2, 1)

            def logits(i):
                pe.wait_ge(h2t_ok, i + 1)
                for h in range(HC):
                    ins = mm(P[0:TT, 6, bass.ds(i * NX, NX)], h2t[:, h, :], wrt[:, h, :], start=(h == 0), stop=(h == HC - 1))
                ins.then_inc(lg_mm, 1)

            pe.wait_ge(g_evac, 2 * NT)
            aggregate(0, 0)
            aggregate(1, 1)
            h2_transposes(0, 0)
            pe.wait_ge(wr_in, 16)
            with pe.Fori(0, NT // 2 - 1) as it:
                for c in range(2):
                    aggregate(c, it * 2 + (c + 2))
                    logits(it * 2 + c)
                    h2_transposes(1 - c, it * 2 + (c + 1))
            logits(NT - 2)
            h2_transposes((NT - 1) % 2, NT - 1)
            logits(NT - 1)
            for i in range(NT):
                c = i % 2
                pe.wait_ge(diag_ok, i + 1)
                if i >= 2:
                    pe.wait_ge(vb_ok, i - 1)
                for h in range(2):
                    ins = mm(P[0:TT, 2 * c + h, 0:500], ones[0:TT, 0:TT], diag[:, c, 4 * h:4 * h + 4, :].rearrange("p a b -> p (a b)"),
                             start=True, stop=True)
                ins.then_inc(vb_mm, 1)
            with pe.Fori(0, NX // 2) as it:
                for c in range(2):
                    at_ = 0
                    for i in range(NT):
                        pe.wait_ge(cmp_ok, it * 20 + (c * NT + i + 1))
                        for j in range(i + 1):
                            ins = mm(P[0:TT, 6, bass.ds(it * 2 + (c + j * NX), 1)], cmpm[:, c, at_ + j * TT:at_ + (j + 1) * TT],
                                     onesb[0:TT, 0:1], start=(i == 0), stop=(i == NT - 1), skip_group_check=True)
                        at_ += (i + 1) * TT
                    ins.then_inc(cs_mm, 1)

            def transposes(e1, chunks=range(HC)):
                pe.wait_ge(rows_in, e1 * 64 + 64)
                for h in chunks:
                    if h >= 2:
                        pe.wait_ge(exl, e1 * 8 + (h - 1))
                    for a in range(4):
                        ins = nc.tensor.transpose(P[:, h % 2, a * CA:(a + 1) * CA], rows[:, a, h * 128:(h + 1) * 128], ident[0:CA, 0:CA])
                    ins.then_inc(etr, 1)

            def up(e):
                for m in range(FC):
                    ms = slice(m * 128, (m + 1) * 128)
                    if m >= 2:
                        pe.wait_ge(gf_ok, e * FC + (m - 1))
                    for k, (hi, lo) in enumerate(((s0_hi, s0_lo), (s1_hi, s1_lo))):
                        for h in range(HC):
                            if m == 0:
                                pe.wait_ge(lo_ok, e * 24 + (MOE + 8 * k + h + 1))
                                if k == 0:
                                    pe.wait_ge(exl, e * 8 + (h + 1))
                            ins = three(P[:, 2 + 2 * k + m % 2, 0:CAPR], hi[:, h, ms], lo[:, h, ms], ex_hi[:, h, :], ex_lo[:, h, :],
                                        h == 0, h == HC - 1)
                            if m == FC - 1 and not (k == 1 and h == HC - 1):
                                ins.then_inc(w_used, 1)
                    ins.then_inc(pg_mm, 1)
                pe.wait_ge(pg_mm, e * FC + FC)
                pe.nop().then_inc(w_used, 1)

            def down(e, parts=range(8)):
                for u in parts:
                    a, h = u // 2, u % 2
                    if u >= 2:
                        pe.wait_ge(eo_ok, e * 8 + (u - 1))
                    for d in range(FC):
                        if u < 2:
                            pe.wait_ge(lo_ok, e * 24 + (MOE + 16 + 2 * d + h + 1))
                        if u == 0:
                            pe.wait_ge(gl_ok, e * FC + (d + 1))
                        ins = three(P[0:CA, 6 + u % 2, :], g_hi[:, d, a * CA:(a + 1) * CA], g_lo[:, d, a * CA:(a + 1) * CA],
                                    s2_hi[:, 2 * d + h, :], s2_lo[:, 2 * d + h, :], d == 0, d == FC - 1)
                    ins.then_inc(dn_mm, 1)
                    if u == 7:
                        pe.wait_ge(dn_mm, e * 8 + 8)
                        pe.nop().then_inc(w_used, 8)

            transposes(0)
            with pe.Fori(0, NX - 1) as e:
                up(e)
                transposes(e + 1, (0, 1))
                for u in range(8):
                    down(e, (u,))
                    if u + 2 < HC:
                        transposes(e + 1, (u + 2,))
            up(NX - 1)
            down(NX - 1)


def kernel(x, src, dst, edge_weight, L0_gnn_W, L0_gnn_b, L0_mix_W_qkv, L0_mix_b_qkv, L0_mix_W_proj, L0_mix_b_proj,
           L0_ffn_router_weight, L0_ffn_ff_pre_act_weight, L0_ffn_gate_weight, L0_ffn_ff_post_act_weight):
    import numpy as np
    import concourse.bacc as bacc
    from concourse.bass_utils import run_bass_kernel_spmd as run

    n = np.asarray
    src, dst, qkv, gw = n(src), n(dst), n(L0_mix_W_qkv), n(L0_gnn_W)
    parts = []
    for g in range(HG):
        c = slice(g * SC, (g + 1) * SC)
        parts += [qkv[:, D:2 * D][:, c], qkv[:, 2 * D:][:, c], qkv[:, :D][:, c]]
    parts += [gw[:, :SC], gw[:, SC:]]
    pre, gate, post = n(L0_ffn_ff_pre_act_weight), n(L0_ffn_gate_weight), n(L0_ffn_ff_post_act_weight)
    arrays = {
        "x": n(x),
        "edges_n": np.stack([src.reshape(TT, EC), dst.reshape(TT, EC)]),
        "edges_c": np.stack([np.ascontiguousarray(src.reshape(EC, TT).T), np.ascontiguousarray(dst.reshape(EC, TT).T)]),
        "w_c": np.ascontiguousarray(n(edge_weight).reshape(EC, TT).T),
        "wmain": np.stack(parts),
        "bqkv": n(L0_mix_b_qkv),
        "bg": n(L0_gnn_b),
        "wr_t": np.ascontiguousarray(n(L0_ffn_router_weight).T.reshape(HC, 128, NX).transpose(1, 0, 2)).reshape(128, HC * NX),
        "wpre": np.ascontiguousarray(pre.transpose(0, 2, 1).reshape(NX, HC, 128, DFF).transpose(2, 0, 1, 3)),
        "wgate": np.ascontiguousarray(gate.transpose(0, 2, 1).reshape(NX, HC, 128, DFF).transpose(2, 0, 1, 3)),
        "wpost": np.ascontiguousarray(post.transpose(0, 2, 1).reshape(NX, FC, 128, 2, SC).transpose(2, 0, 1, 3, 4)).reshape(128, NX, 8, SC),
    }
    nc = bacc.Bacc("TRN2", target_bir_lowering=False, num_devices=1)
    args = [nc.dram_tensor(k, a.shape, mybir.dt.from_np(a.dtype), kind="ExternalInput").ap() for k, a in arrays.items()]
    out = nc.dram_tensor("out", [T, D], F32, kind="ExternalOutput").ap()
    build(nc, *args, out)
    r = run(nc, [arrays], core_ids=[0])
    return r.results[0]["out"]
```
